# Optimizing a Trainium2 kernel written in Bass

```python
import numpy as np
import jax
import jax.numpy as jnp

def _softmax(x, axis=-1):
    return jax.nn.softmax(x, axis=axis)

def _gelu(x):
    return jax.nn.gelu(x, approximate=True)

def _silu(x):
    return jax.nn.silu(x)

def _sigmoid(x):
    return jax.nn.sigmoid(x)

def _layernorm(x, axis=-1, eps=1e-05):
    m = jnp.mean(x, axis=axis, keepdims=True)
    v = jnp.var(x, axis=axis, keepdims=True)
    return (x - m) / jnp.sqrt(v + eps)

def _scatter_add(tgt, idx, src, axis=0):
    return tgt.at[idx].add(src)

def _segment_sum(src, seg, n):
    return jax.ops.segment_sum(src, seg, n)
kernel_name = 'mk_gnn_resnorm_d4_gnn_r8_548fa7'

def setup_inputs(seed: int=0):
    np.random.seed(seed)
    _w = jnp.asarray

    def _rec_inputs():
        import jax
        import jax.numpy as jnp
        _gk = jax.random.key(seed)
        x = -0.000202 + 1 * jax.random.normal(jax.random.fold_in(_gk, 1), (6250, 128), jnp.float32)
        _s = jax.random.randint(jax.random.fold_in(_gk, 2), (50000,), 0, 6250, jnp.int32)
        _d = jax.random.randint(jax.random.fold_in(_gk, 3), (50000,), 0, 6250, jnp.int32)
        _loop = jnp.arange(6250, dtype=jnp.int32)
        src = jnp.concatenate([_s, _d, _loop])
        dst = jnp.concatenate([_d, _s, _loop])
        _o = jnp.argsort(dst, stable=True)
        src = src[_o]
        dst = dst[_o]
        edge_type_4 = jax.random.randint(jax.random.fold_in(_gk, 13), (106250,), 0, 4, jnp.int32)
        return (x, src, dst, edge_type_4)
    x, src, dst, edge_type_4 = _rec_inputs()

    def _L0_gnn_setup():
        import jax, jax.numpy as jnp
        import numpy as np
        N_NODES = 6250
        N_EDGES = 100000
        D_IN = 128
        N_HEAD = 4
        D_OUT = D_IN // N_HEAD
        key = jax.random.key(seed)
        k1, k2, k3, k4, k5 = jax.random.split(key, 5)
        in_feat = jax.random.normal(k1, (N_NODES, D_IN), dtype=jnp.float32)
        edge_ind = jax.random.randint(k2, (2, N_EDGES), 0, N_NODES, dtype=jnp.int64)
        W_proj = jax.random.normal(k3, (D_IN, N_HEAD * D_OUT), dtype=jnp.float32) * (1.0 / np.sqrt(D_IN))
        a_src = jax.random.normal(k4, (1, N_HEAD, D_OUT), dtype=jnp.float32) * (1.0 / np.sqrt(D_OUT))
        a_tgt = jax.random.normal(k5, (1, N_HEAD, D_OUT), dtype=jnp.float32) * (1.0 / np.sqrt(D_OUT))
        bias = jnp.zeros((N_HEAD * D_OUT,), dtype=jnp.float32)
        return {'in_feat': in_feat, 'edge_ind': edge_ind, 'edge_len': N_EDGES, 'W_proj': W_proj, 'a_src': a_src, 'a_tgt': a_tgt, 'bias': bias}
    _L0_gnn_all = _L0_gnn_setup()
    _L0_gnn_in = {k: v for k, v in _L0_gnn_all.items() if k in ('W_proj', 'a_src', 'a_tgt', 'bias')}
    del _L0_gnn_all

    def _L1_gnn_setup():
        import jax, jax.numpy as jnp
        import numpy as np
        LN_EPS = 1e-05
        key = jax.random.key(seed)
        ks = jax.random.split(key, 6)
        N, E, D = (12500, 80000, 128)
        x = jax.random.normal(ks[0], (N, D), dtype=jnp.float32)
        edge_index = jax.random.randint(ks[1], (2, E), 0, N, dtype=jnp.int64)
        W_msg = jax.random.normal(ks[2], (D, D), dtype=jnp.float32) / np.sqrt(D)
        W_self = jax.random.normal(ks[3], (D, D), dtype=jnp.float32) / np.sqrt(D)
        b_self = jax.random.normal(ks[4], (D,), dtype=jnp.float32) * 0.02
        gamma = jnp.ones((D,), dtype=jnp.float32)
        beta = jnp.zeros((D,), dtype=jnp.float32)
        return {'x': x, 'edge_index': edge_index, 'W_msg': W_msg, 'W_self': W_self, 'b_self': b_self, 'gamma': gamma, 'beta': beta}
    _L1_gnn_all = _L1_gnn_setup()
    _L1_gnn_in = {k: v for k, v in _L1_gnn_all.items() if k in ('W_msg', 'W_self', 'b_self', 'gamma', 'beta')}
    del _L1_gnn_all

    def _L2_gnn_setup():
        import jax, jax.numpy as jnp
        import numpy as np
        N_NODES = 12500
        N_EDGES = 200000
        HIDDEN = 128
        LEAKY_SLOPE = 0.01

        def _segment_softmax(e, seg, num_segments):
            seg_max = jax.ops.segment_max(e, seg, num_segments=num_segments)
            seg_max = jnp.where(jnp.isfinite(seg_max), seg_max, 0.0)
            e_exp = jnp.exp(e - seg_max[seg])
            denom = jax.ops.segment_sum(e_exp, seg, num_segments=num_segments)
            return e_exp / denom[seg]
        key = jax.random.key(seed)
        k1, k2, k3, k4 = jax.random.split(key, 4)
        x = jax.random.normal(k1, (N_NODES, HIDDEN), dtype=jnp.float32)
        edge_index = jax.random.randint(k2, (2, N_EDGES), 0, N_NODES, dtype=jnp.int64)
        w_i = jax.random.normal(k3, (HIDDEN,), dtype=jnp.float32) * (1.0 / np.sqrt(HIDDEN))
        w_j = jax.random.normal(k4, (HIDDEN,), dtype=jnp.float32) * (1.0 / np.sqrt(HIDDEN))
        return {'x': x, 'edge_index': edge_index, 'w_i': w_i, 'w_j': w_j}
    _L2_gnn_all = _L2_gnn_setup()
    _L2_gnn_in = {k: v for k, v in _L2_gnn_all.items() if k in ('w_i', 'w_j')}
    del _L2_gnn_all

    def _L3_gnn_setup():
        import jax, jax.numpy as jnp
        import numpy as np
        N, E, IN, OUT = (6250, 100000, 128, 128)
        R = 5
        key = jax.random.key(seed)
        k = jax.random.split(key, 6)
        x = jax.random.normal(k[0], (N, IN), jnp.float32)
        src = jax.random.randint(k[1], (E,), 0, N)
        dst = jax.random.randint(k[2], (E,), 0, N)
        rel = jax.random.randint(k[3], (E,), 0, R - 1)
        xavier = np.sqrt(2.0) * np.sqrt(6.0 / (IN + OUT))
        weight = jax.random.uniform(k[4], (R, IN, OUT), jnp.float32, -xavier, xavier)
        bias = jax.random.uniform(k[5], (R, OUT), jnp.float32, -xavier, xavier)
        return dict(x=x, weight=weight, bias=bias, src=src, dst=dst, rel=rel)
    _L3_gnn_all = _L3_gnn_setup()
    _L3_gnn_in = {k: v for k, v in _L3_gnn_all.items() if k in ('weight', 'bias')}
    del _L3_gnn_all
    return {'x': x, 'src': src, 'dst': dst, 'edge_type_4': edge_type_4, 'L0_gnn_W_proj': _L0_gnn_in['W_proj'], 'L0_gnn_a_src': _L0_gnn_in['a_src'], 'L0_gnn_a_tgt': _L0_gnn_in['a_tgt'], 'L0_gnn_bias': _L0_gnn_in['bias'], 'L1_gnn_W_msg': _L1_gnn_in['W_msg'], 'L1_gnn_W_self': _L1_gnn_in['W_self'], 'L1_gnn_b_self': _L1_gnn_in['b_self'], 'L1_gnn_gamma': _L1_gnn_in['gamma'], 'L1_gnn_beta': _L1_gnn_in['beta'], 'L2_gnn_w_i': _L2_gnn_in['w_i'], 'L2_gnn_w_j': _L2_gnn_in['w_j'], 'L3_gnn_weight': _L3_gnn_in['weight'], 'L3_gnn_bias': _L3_gnn_in['bias']}

def reference(x, src, dst, edge_type_4, L0_gnn_W_proj, L0_gnn_a_src, L0_gnn_a_tgt, L0_gnn_bias, L1_gnn_W_msg, L1_gnn_W_self, L1_gnn_b_self, L1_gnn_gamma, L1_gnn_beta, L2_gnn_w_i, L2_gnn_w_j, L3_gnn_weight, L3_gnn_bias):
    import jax
    import jax.numpy as jnp

    def _L0_gnn_ref(in_feat, edge_ind, edge_len, W_proj, a_src, a_tgt, bias):
        import jax, jax.numpy as jnp
        import numpy as np
        N_NODES = 6250
        N_EDGES = 100000
        D_IN = 128
        N_HEAD = 4
        D_OUT = D_IN // N_HEAD
        n_nodes = in_feat.shape[0]
        n_head, d_out = (a_src.shape[1], a_src.shape[2])
        proj_feat = (in_feat @ W_proj).reshape(n_nodes, n_head, d_out)
        src_score = jnp.sum(proj_feat * a_src, axis=-1)
        tgt_score = jnp.sum(proj_feat * a_tgt, axis=-1)
        src_ind, tgt_ind = (edge_ind[0], edge_ind[1])
        edge_score = jax.nn.leaky_relu(src_score[src_ind] + tgt_score[tgt_ind], negative_slope=0.2)
        edge_score = jnp.exp(edge_score - jnp.max(edge_score))
        neigh_sums = jax.ops.segment_sum(edge_score, tgt_ind, num_segments=n_nodes)
        att_per_edge = edge_score / (neigh_sums[tgt_ind] + 1e-16)
        src_feat_weighted = proj_feat[src_ind] * att_per_edge[..., None]
        out_feat = jax.ops.segment_sum(src_feat_weighted, tgt_ind, num_segments=n_nodes)
        return out_feat.reshape(n_nodes, -1) + bias

    def _L1_gnn_ref(x, edge_index, W_msg, W_self, b_self, gamma, beta):
        import jax, jax.numpy as jnp
        import numpy as np
        LN_EPS = 1e-05
        N = x.shape[0]
        src, dst = (edge_index[0], edge_index[1])
        msg = jnp.einsum('ed,fd->ef', x[src], W_msg)
        agg = jax.ops.segment_sum(msg, dst, num_segments=N)
        deg = jax.ops.segment_sum(jnp.ones_like(dst, dtype=x.dtype), dst, num_segments=N)
        agg = agg / jnp.maximum(deg, 1.0)[:, None]
        out = jnp.einsum('nd,fd->nf', x, W_self) + b_self + agg
        out = jax.nn.relu(out)
        mu = jnp.mean(out, axis=-1, keepdims=True)
        var = jnp.mean(jnp.square(out - mu), axis=-1, keepdims=True)
        return (out - mu) * jax.lax.rsqrt(var + LN_EPS) * gamma + beta

    def _L2_gnn_ref(x, edge_index, w_i, w_j):
        import jax, jax.numpy as jnp
        import numpy as np
        N_NODES = 12500
        N_EDGES = 200000
        HIDDEN = 128
        LEAKY_SLOPE = 0.01

        def _segment_softmax(e, seg, num_segments):
            seg_max = jax.ops.segment_max(e, seg, num_segments=num_segments)
            seg_max = jnp.where(jnp.isfinite(seg_max), seg_max, 0.0)
            e_exp = jnp.exp(e - seg_max[seg])
            denom = jax.ops.segment_sum(e_exp, seg, num_segments=num_segments)
            return e_exp / denom[seg]
        n = x.shape[0]
        idx_j = edge_index[0]
        idx_i = edge_index[1]
        ei_all = x @ w_i
        ej_all = x @ w_j
        e = ei_all[idx_i] + ej_all[idx_j]
        e = jnp.where(e > 0, e, LEAKY_SLOPE * e)
        alpha = _segment_softmax(e.astype(jnp.float32), idx_j, n)
        msgs = alpha[:, None] * x[idx_j]
        out = jax.ops.segment_sum(msgs, idx_i, num_segments=n)
        return jax.nn.relu(out)

    def _L3_gnn_ref(x, weight, bias, src, dst, rel):
        import jax, jax.numpy as jnp
        import numpy as np
        N, E, IN, OUT = (6250, 100000, 128, 128)
        R = 5
        num_nodes = x.shape[0]
        num_edge_rels = weight.shape[0] - 1
        x_src = x[src]
        msg = jnp.zeros((src.shape[0], weight.shape[2]), x.dtype)
        for r in range(num_edge_rels):
            hr = x_src @ weight[r] + bias[r]
            msg = jnp.where((rel == r)[:, None], hr, msg)
        agg = jax.ops.segment_max(msg, dst, num_segments=num_nodes)
        deg = jax.ops.segment_sum(jnp.ones_like(dst, jnp.float32), dst, num_segments=num_nodes)
        agg = jnp.where((deg > 0)[:, None], agg, jnp.zeros((), x.dtype))
        h = x @ weight[-1] + bias[-1] + agg
        return h
    edge_index = jnp.stack([src, dst])
    x = _layernorm(x + _L0_gnn_ref(x, edge_index, 106250, L0_gnn_W_proj, L0_gnn_a_src, L0_gnn_a_tgt, L0_gnn_bias), axis=-1)
    x = _layernorm(x + _L1_gnn_ref(x, edge_index, L1_gnn_W_msg, L1_gnn_W_self, L1_gnn_b_self, L1_gnn_gamma, L1_gnn_beta), axis=-1)
    x = _layernorm(x + _L2_gnn_ref(x, edge_index, L2_gnn_w_i, L2_gnn_w_j), axis=-1)
    x = _layernorm(x + _L3_gnn_ref(x, L3_gnn_weight, L3_gnn_bias, src, dst, edge_type_4), axis=-1)
    return x

_drawn_inputs = setup_inputs


def setup_inputs(seed=0):
    import zlib

    import numpy as np

    out = dict(_drawn_inputs(seed))
    spreads = {'L0_gnn_bias': (0.0, 0.1), 'L1_gnn_gamma': (1.0, 0.2), 'L1_gnn_beta': (0.0, 0.1)}
    factors = {}
    for name, (base, spread) in spreads.items():
        noise = np.random.default_rng([zlib.crc32(name.encode()), seed]).standard_normal(out[name].shape)
        drawn = base * np.exp(spread * noise) if base else spread * noise
        out[name] = jnp.asarray(drawn.astype(out[name].dtype))
    for name, factor in factors.items():
        out[name] = (out[name] * factor).astype(out[name].dtype)
    return out
```

```python
import numpy as np
from contextlib import ExitStack

import concourse.bass as bass
from concourse import mybir

FP = mybir.dt.float32
BF = mybir.dt.bfloat16
I32 = mybir.dt.int32
ALU = mybir.AluOpType
ACT = mybir.ActivationFunctionType
AXX = mybir.AxisListType.X
RMAX = bass.bass_isa.ReduceOp.max
ds = bass.ds

P = 128
N = 6250
E = 106250
D = 128
H = 4
DH = D // H
R = 4
NB = -(-N // P)
NP = NB * P
LAST = N - (NB - 1) * P
U = 8
RING = 4
K = -(-E // (P * U * RING)) * U * RING
GROUPS = K // U
LAPS = K // (U * RING)
AHEAD = U * RING
TG = -(-K // P)
KP = TG * P
W = 32
WIDE = NP + W
FAR = 32768
BIG = 3.38e38
GONE = -1.0e30
TINY = 1e-37
NODE_TURNS = 7
LN_EPS = 1e-5
SLOPE0, SLOPE2 = 0.2, 0.01
HALF = 4 * P


class Chain:

    def __init__(self, eng, sem, start=0):
        self.eng, self.sem, self.start, self.n = eng, sem, start, 0

    def step(self, ins):
        self.n += 1
        ins.then_inc(self.sem, 1)
        self.eng.wait_ge(self.sem, self.start + self.n)


def per(ap, n):
    return ap.unsqueeze(len(ap.shape)).to_broadcast([*ap.shape, n])


def times(ap, n):
    return ap.unsqueeze(1).to_broadcast([ap.shape[0], n, *ap.shape[1:]])


def build(nc, x, xT, src, dst, etype, w_proj, a_src, a_tgt, bias0, w_msgT, w_selfT, b_self,
          gamma, beta, w_i, w_j, w_rel, b_rel, out):
    v, t, a, g = nc.vector, nc.tensor, nc.scalar, nc.gpsimd
    ctx = ExitStack()
    with ctx:
        def sb(name, shape, dt=FP):
            return ctx.enter_context(nc.sbuf_tensor(name, shape, dt))

        def sem(name):
            return nc.alloc_semaphore(name=name)

        def dram(name, shape, dt=FP):
            return nc.dram_tensor(name, shape, dt, kind="Internal").ap()

        DSTP = dram("dst_padded", (KP * P + 1,), I32)
        SRCP = dram("src_padded", (KP * P,), I32)
        TYPP = dram("type_padded", (KP * P,), I32)
        BASED = dram("window_base", (KP,))
        MASKD = dram("run_mask", (KP * P,), BF)
        CUMD = dram("edges_up_to", (NP,))
        T0 = dram("table0", (NP, D + H))
        T1 = dram("table1", (NP, D))
        V2 = dram("table2v", (NP, 2))
        T2 = dram("table2", (NP, D + 2))
        T3 = dram("table3", (R * NP, D))
        IDX3D = dram("index3", (P, KP), I32)
        RUNS = dram("running_max", ((K + U) * P, D))

        XBUF = sb("XBUF", [P, WIDE])
        X = XBUF[:, 0:NP].rearrange("p (b f) -> p b f", f=D)
        DEN = XBUF[0:1 + H, :]
        ACC = sb("ACC", [P, WIDE])
        BUF = sb("BUF", [P, H * WIDE])
        TB = BUF[:, :].rearrange("p (h n) -> p h n", h=H)
        HS = BUF[:, 0:NP].rearrange("p (b f) -> p b f", f=D)
        UB = BUF[:, WIDE:2 * WIDE]
        AGG = BUF[:, 2 * WIDE:2 * WIDE + NP].rearrange("p (b f) -> p b f", f=D)
        OLO = BUF[:, 3 * WIDE:3 * WIDE + U * P].rearrange("p (u n) -> p u n", u=U)
        IDX3 = BUF[:, 4 * WIDE - KP:4 * WIDE].bitcast(I32)
        LO = BUF[:, 2 * WIDE:2 * WIDE + KP]
        HI = BUF[:, 2 * WIDE + KP:2 * WIDE + 2 * KP]
        REL0 = sb("REL0", [P, KP])
        REL = sb("REL", [P, KP])
        PEN = sb("PEN", [P, KP])
        SRC = sb("SRC", [P, KP], I32)
        BASE0 = sb("BASE0", [1, KP])
        BASE = sb("BASE", [1, KP], I32)
        SHIFT = sb("SHIFT", [P, 1])
        FLAG = sb("FLAG", [P, 4], I32)
        IOTA = sb("IOTA", [P, P])
        IDENT = sb("IDENT", [P, P])
        DEG = sb("DEG", [P, NB])
        MV = sb("MV", [P, NB, 2])
        RSTD = sb("RSTD", [P, NB])
        NBIA = sb("NBIA", [P, NB])
        EPS = sb("EPS", [P, 1])
        SC = sb("SC", [P, 16])
        SHIFT0 = sb("SHIFT0", [P, 1])
        NSHIFT0 = sb("NSHIFT0", [P, 1])
        GUARD0 = sb("GUARD0", [P, 1])
        RDEG = sb("RDEG", [P, NB])
        HAS = sb("HAS", [P, NB])
        ENDF = sb("ENDF", [P, NB])
        ENDI = sb("ENDI", [P, NB], I32)
        RDEN = sb("RDEN", [P, NB])
        VC = sb("VC", [P, NB, 2])
        ONE = sb("ONE", [P, P])
        ZERO = sb("ZERO", [P, U * W])
        G = sb("G", [P, RING, U, D + H])
        IC = sb("IC", [P, RING * U], I32)
        SEL = sb("SEL", [P, 2, U, W])
        PROD = sb("PROD", [P, U * H, W])
        Z = sb("Z", [P, U, H])
        ZL = sb("ZL", [P, 2, U, H])
        ZMAX = sb("ZMAX", [P, U, H])
        WE = sb("WE", [P, 2, U, 1 + H])
        GW = sb("GW", [P, 2, U, D])
        GF = G[:].rearrange("p r u f -> p (r u f)")
        SA, SX, YS, SD = (GF[:, i * 2 * HALF:(i + 1) * 2 * HALF].rearrange("p (q n) -> p q n", q=2) for i in range(4))
        SD = SD[0:1 + H]
        GWF = GW[:].rearrange("p q u f -> p (q u f)")
        YW = GWF[:, 0:8 * (D + H)].rearrange("p (u f) -> p u f", f=D + H)
        WS = GWF[:, 8 * (D + H):8 * (D + H) + 5 * D]
        WB = PROD[:].rearrange("p u n -> p (u n)")
        ST = sb("ST", [P, NB, 2 * H])
        BN6 = sb("BN6", [P, 2, 4, 6])
        SM = sb("SM", [P, 2, 4, 8])
        PS = [ctx.enter_context(nc.psum_tensor(f"PS{i}", [P, 512], FP)) for i in range(8)]

        passed = sem("passed")

        def pass_wait(eng):
            eng.sem_inc(passed, 1)

        def half(turn, b):
            return turn * 2 + b, 4 - b, turn * 7 + 4 * b, turn * 7 * P + HALF * b

        def passes(eng):
            return eng.value_load(FLAG[0:1, 0:1], min_val=1, max_val=NP // W + 1)

        def tiles_of(eng, turn, b):
            return eng.snap(turn * (U * RING) + b * U, min_val=0, max_val=K - U)

        def edge_lists():
            tiles = lambda i: BUF[:, i * KP:(i + 1) * KP].rearrange("p (g e) -> p g e", e=P)
            Fd, Fp, Fs, Ft, F1 = (tiles(i) for i in range(5))
            Rd, Rp, Rs, Rt = (BUF[:, i * KP:(i + 1) * KP].bitcast(I32).rearrange("p (g e) -> p g e", e=P)
                              for i in range(5, 9))
            flat = lambda y: y.rearrange("p g e -> p (g e)")
            MK = BUF[:, 9 * KP:9 * KP + KP // 2].bitcast(BF).rearrange("p (g e) -> p g e", e=P)
            idx3 = BUF[:, 10 * KP:11 * KP].bitcast(I32)
            bmin = sb("bmin", [P, TG])
            NPAD = KP * P - E
            far, zero = (BUF[0:1, 11 * KP + i * NPAD:11 * KP + i * NPAD + NPAD // 2].bitcast(I32) for i in range(2))
            neg = sb("neg", [1, 1], I32)
            pads, padded, rows_in = sem("pads"), sem("padded"), sem("rows_in")
            iotas, red_in, red_out = sem("iotas"), sem("red_in"), sem("red_out")
            ident_ready, rows_ready, turned = sem("ident_ready"), sem("rows_ready"), sem("turned")
            base_ready, mask_ready, stored = sem("base_ready"), sem("mask_ready"), sem("stored")
            base_in, chain, idx3_ready = sem("base_in"), sem("list_chain"), sem("idx3_ready")
            ipart = SC[:, 0:1]

            with nc.Block() as block:
                @block.sync
                def _(sp):
                    for to, of in ((DSTP[1:1 + E], dst), (SRCP[0:E], src), (TYPP[0:E], etype)):
                        sp.dma_start(to.rearrange("(a b) -> a b", b=850),
                                     of.rearrange("(a b) -> a b", b=850)).then_inc(padded, 16)
                    sp.wait_ge(pads, 1)
                    sp.dma_start(DSTP[0:1].unsqueeze(0), neg[:]).then_inc(padded, 16)
                    for h in range(2):
                        for to, of in ((DSTP[1 + E:], far), (SRCP[E:], zero), (TYPP[E:], zero)):
                            sp.dma_start(to[h * (NPAD // 2):(h + 1) * (NPAD // 2)].unsqueeze(0), of).then_inc(padded, 16)
                    sp.wait_ge(padded, 10 * 16)
                    lay = lambda y: y.rearrange("(g p e) -> p g e", p=P, e=P)
                    for to, of in ((Rd, DSTP[1:]), (Rp, DSTP[0:KP * P]), (Rs, SRCP), (Rt, TYPP)):
                        sp.dma_start(to, lay(of)).then_inc(rows_in, 16)
                    sp.wait_ge(base_ready, 1)
                    sp.dma_start(BASED.rearrange("(g p) -> p g", p=P), bmin[:], allow_slow_non_contiguous=True).then_inc(stored, 16)
                    sp.wait_ge(stored, 16)
                    sp.dma_start(BASE0[:], BASED.unsqueeze(0)).then_inc(base_in, 16)
                    sp.wait_ge(mask_ready, 1)
                    sp.dma_start(MASKD.rearrange("(g p e) -> p g e", p=P, e=P), MK[:]).then_inc(stored, 16)
                    sp.wait_ge(idx3_ready, 1)
                    sp.dma_start(IDX3D, idx3).then_inc(stored, 16)
                    sp.wait_ge(base_in, 16)
                    sp.wait_ge(stored, 48)

                @block.gpsimd
                def _(pool):
                    g.memset(far, FAR)
                    g.memset(neg[:], -1)
                    g.memset(zero, 0)
                    g.drain().then_inc(pads, 1)
                    g.iota(IOTA[:], [[1, P]], base=0, channel_multiplier=0,
                           allow_small_or_imprecise_dtypes=True)
                    g.iota(ipart, [[1, 1]], base=0, channel_multiplier=1,
                           allow_small_or_imprecise_dtypes=True)
                    g.drain().then_inc(iotas, 1)
                    pool.wait_ge(red_in, 1)
                    g.partition_all_reduce(SC[:, 4:6], SC[:, 2:4], P, RMAX).then_inc(red_out, 1)

                @block.vector
                def _(dve):
                    ch = Chain(dve, chain)
                    v.memset(EPS[:], LN_EPS)
                    v.memset(BASE[:], 0)
                    dve.wait_ge(iotas, 1)
                    v.tensor_scalar(IDENT[:], IOTA[:], ipart, None, ALU.is_equal).then_inc(ident_ready, 1)
                    dve.wait_ge(rows_in, 64)
                    v.tensor_copy(Fd, Rd)
                    v.tensor_copy(Fp, Rp)
                    v.tensor_copy(Fs, Rs)
                    ch.step(v.tensor_copy(Ft, Rt))
                    ch.step(v.tensor_reduce(bmin[:], Fd, AXX, ALU.min))
                    ch.step(v.tensor_scalar(bmin[:], bmin[:], float(NP - W), None, ALU.min))
                    dve.sem_inc(base_ready, 1)
                    ch.step(v.scalar_tensor_tensor(F1, Fd, float(N), Fd, ALU.is_lt, ALU.mult))
                    ch.step(v.tensor_tensor(F1, F1, per(bmin[:], P), ALU.subtract))
                    ch.step(v.tensor_reduce(SC[:, 2:3], flat(F1), AXX, ALU.max))
                    ch.step(v.tensor_tensor(F1, Fp, Fd, ALU.subtract))
                    ch.step(v.tensor_reduce(SC[:, 3:4], flat(F1), AXX, ALU.max))
                    dve.sem_inc(red_in, 1)
                    ch.step(v.tensor_tensor(F1, Fp, Fd, ALU.not_equal))
                    v.tensor_tensor(Fd, Fd, per(bmin[:], P), ALU.subtract)
                    ch.step(v.scalar_tensor_tensor(Ft, Ft, float(NP), Fs, ALU.mult, ALU.add))
                    dve.sem_inc(rows_ready, 1)
                    ch.step(v.tensor_scalar(F1, F1, -2.0, 1.0, ALU.mult, ALU.add))
                    ch.step(v.tensor_scalar(MK[:], F1, BIG, None, ALU.mult))
                    dve.sem_inc(mask_ready, 1)
                    for n, to in enumerate((REL0, SRC, idx3)):
                        for h, (g0, g1) in enumerate(((0, 4), (4, TG))):
                            dve.wait_ge(turned, 2 * n + h + 1)
                            ins = v.tensor_copy(to[:, g0 * P:g1 * P], PS[2 * n + h][:, 0:(g1 - g0) * P])
                    ch.step(ins)
                    v.tensor_copy(SRC[:, K:K + AHEAD], SRC[:, 0:AHEAD])
                    ch.step(v.tensor_copy(idx3[:, K:K + AHEAD], idx3[:, 0:AHEAD]))
                    dve.sem_inc(idx3_ready, 1)
                    dve.wait_ge(red_out, 1)
                    ch.step(v.tensor_copy(FLAG[:, 0:2], SC[:, 4:6]))
                    ch.step(v.tensor_scalar(FLAG[:, 0:1], FLAG[:, 0:1], 5, None, ALU.logical_shift_right))
                    ch.step(v.tensor_scalar(FLAG[:, 0:1], FLAG[:, 0:1], 1, None, ALU.add))

                @block.tensor
                def _(pe):
                    pe.wait_ge(ident_ready, 1)
                    pe.wait_ge(rows_ready, 1)
                    for n, lst in enumerate((Fd, Fs, Ft)):
                        for h, (g0, g1) in enumerate(((0, 4), (4, TG))):
                            for i in range(g0, g1):
                                last = t.transpose(PS[2 * n + h][:, (i - g0) * P:(i - g0 + 1) * P],
                                                   lst[:, i, :], IDENT[:])
                            last.then_inc(turned, 1)

        def table0():
            x_in, w_in, zeroed, w_ready = sem("t0_x_in"), sem("t0_w_in"), sem("t0_zeroed"), sem("t0_w_ready")
            xT_ready, pe_done, rows_done, tb_done = sem("t0_xT"), sem("t0_pe"), sem("t0_rows"), sem("t0_tb")
            stored = [sem("t0_stored0"), sem("t0_stored1")]
            red_in, red_out, chain = sem("t0_red_in"), sem("t0_red_out"), sem("t0_chain")
            WTB = WB[:, 0:H * D].rearrange("p (h m) -> p h m", h=H)
            rows = T0.rearrange("(b p) f -> p b f", p=P)
            with nc.Block() as block:
                @block.sync
                def _(sp):
                    sp.dma_start(WS[:, 0:D], w_proj).then_inc(w_in, 16)
                    sp.dma_start(SX[:, 0, 0:D], a_src.to_broadcast([P, D])).then_inc(w_in, 16)
                    sp.dma_start(SX[:, 0, D:2 * D], a_tgt.to_broadcast([P, D])).then_inc(w_in, 16)
                    sp.wait_ge(zeroed, 1)
                    sp.dma_start(ACC[:, 0:N], xT).then_inc(x_in, 16)
                    sp.sem_inc(stored[0], 16)
                    sp.sem_inc(stored[1], 16)
                    with sp.Fori(0, NODE_TURNS) as turn:
                        for b in range(2):
                            i, nb, blk, col = half(turn, b)
                            sp.wait_ge(rows_done, i + 3)
                            sp.dma_start(rows[:, ds(blk, nb), :], YW[:, 4 * b:4 * b + nb, :]).then_inc(stored[b], 16)
                    sp.wait_ge(stored[0], 16 * NODE_TURNS + 16)
                    sp.wait_ge(stored[1], 16 * NODE_TURNS + 16)

                @block.scalar
                def _(act):
                    act.sem_inc(tb_done, 1)
                    act.wait_ge(x_in, 16)
                    with act.Fori(0, NODE_TURNS) as turn:
                        for b in range(2):
                            i, nb, blk, col = half(turn, b)
                            act.wait_ge(pe_done, i + 1)
                            a.copy(SA[:, b, 0:nb * P], ACC[:, ds(col, nb * P)]).then_inc(xT_ready, 1)
                            act.wait_ge(pe_done, i + 3)
                            for h in range(H):
                                ins = a.copy(TB[:, h, ds(col, nb * P)], PS[4 + h][:, 0:nb * P])
                            ins.then_inc(tb_done, 1)

                @block.tensor
                def _(pe):
                    pe.sem_inc(pe_done, 2)
                    pe.wait_ge(w_ready, 1)
                    with pe.Fori(0, NODE_TURNS) as turn:
                        for b in range(2):
                            i, nb, blk, col = half(turn, b)
                            pe.wait_ge(xT_ready, i + 1)
                            pe.wait_ge(rows_done, i + 1)
                            pe.wait_ge(tb_done, i + 1)
                            for j in range(nb):
                                blkT = SA[:, b, j * P:(j + 1) * P]
                                t.matmul(PS[b][:, j * P:(j + 1) * P], blkT, WS[:, 0:D], start=True, stop=True)
                                t.matmul(PS[2 + b][:, j * 8:(j + 1) * 8], blkT, WS[:, D:D + 8],
                                         start=True, stop=True)
                            for h in range(H):
                                last = t.matmul(PS[4 + h][:, 0:nb * P], WTB[:, h, :], SA[:, b, 0:nb * P],
                                                start=True, stop=True)
                            last.then_inc(pe_done, 1)

                @block.gpsimd
                def _(pool):
                    pool.wait_ge(red_in, 1)
                    g.partition_all_reduce(SC[:, 8:12], SC[:, 0:4], P, RMAX).then_inc(red_out, 1)

                @block.vector
                def _(dve):
                    ch = Chain(dve, chain)
                    dve.sem_inc(rows_done, 2)
                    v.memset(ZERO[:], 0.0)
                    v.memset(TB[:, :, NP:WIDE], 0.0)
                    ch.step(v.memset(ACC[:, N:WIDE], 0.0))
                    dve.sem_inc(zeroed, 1)
                    dve.wait_ge(w_in, 48)
                    v.tensor_tensor(YS[:, 0, 0:D], WS[:, 0:D], SX[:, 0, 0:D], ALU.mult)
                    ch.step(v.tensor_tensor(YS[:, 0, D:2 * D], WS[:, 0:D], SX[:, 0, D:2 * D], ALU.mult))
                    ch.step(v.tensor_reduce(WS[:, D:D + 8],
                                            YS[:, 0, 0:2 * D].rearrange("p (h d) -> p h d", d=DH), AXX, ALU.add))
                    ch.step(v.tensor_copy(WTB, per(WS[:, D + H:D + 8], D)))
                    dve.sem_inc(w_ready, 1)
                    with dve.Fori(0, NODE_TURNS) as turn:
                        for b in range(2):
                            i, nb, blk, col = half(turn, b)
                            proj = PS[b][:, 0:nb * P].rearrange("p (b f) -> p b f", f=D)
                            scores = PS[2 + b][:, 0:nb * 8].rearrange("p (b f) -> p b f", f=8)
                            dve.wait_ge(pe_done, i + 3)
                            dve.wait_ge(stored[b], 16 * turn + 16)
                            v.tensor_copy(YW[:, 4 * b:4 * b + nb, 0:D], proj)
                            v.tensor_copy(YW[:, 4 * b:4 * b + nb, D:D + H], scores[:, :, 0:H])
                            v.tensor_copy(ST[:, ds(blk, nb), :], scores).then_inc(rows_done, 1)
                    dve.wait_ge(rows_done, 2 * NODE_TURNS + 2)
                    XY = mybir.AxisListType.XY
                    v.tensor_reduce(SC[:, 12:13], ST[:, :, 0:H], XY, ALU.max)
                    v.tensor_reduce(SC[:, 13:14], ST[:, :, H:8], XY, ALU.max)
                    v.tensor_reduce(SC[:, 14:15], ST[:, :, 0:H], XY, ALU.min)
                    ch.step(v.tensor_reduce(SC[:, 15:16], ST[:, :, H:8], XY, ALU.min))
                    v.tensor_copy(SC[:, 0:2], SC[:, 12:14])
                    ch.step(v.tensor_scalar(SC[:, 2:4], SC[:, 14:16], -1.0, None, ALU.mult))
                    dve.sem_inc(red_in, 1)
                    dve.wait_ge(red_out, 1)
                    ch.step(v.tensor_tensor(SC[:, 0:1], SC[:, 8:9], SC[:, 9:10], ALU.add))
                    ch.step(v.scalar_tensor_tensor(SHIFT0[:], SC[:, 0:1], SLOPE0, SC[:, 0:1], ALU.mult, ALU.max))
                    ch.step(v.tensor_scalar(NSHIFT0[:], SHIFT0[:], -1.0, None, ALU.mult))

        def number(pss, turn, b):
            return (pss * LAPS + turn) * RING + b

        def first_indices(rows, ready):
            a.copy(IC[:], rows[:, 0:AHEAD]).then_inc(ready, RING)

        def next_indices(act, rows, pss, turn, b, rows_used, ready):
            k = act.snap(turn * AHEAD + (b * U + AHEAD), min_val=AHEAD, max_val=K + AHEAD - U)
            act.wait_ge(rows_used, number(pss, turn, b) + 1)
            a.copy(IC[:, b * U:(b + 1) * U], rows[:, ds(k, U)]).then_inc(ready, 1)

        def gather_rows(pool, table, width, indices_ready, started, gathered, npass=None):
            with pool.Fori(0, passes(pool) if npass is None else npass) as pss:
                with pool.Fori(0, LAPS) as turn:
                    for b in range(RING):
                        pool.wait_ge(indices_ready, number(pss, turn, b) + 1)
                        pool.sem_inc(started, 1)
                        for u in range(U):
                            pool.indirect_dma_start(
                                out=G[:, b, u, 0:width], out_offset=None, in_=table,
                                in_offset=bass.IndirectOffsetOnAxis(
                                    ap=IC[:, b * U + u:b * U + u + 1], axis=0)).then_inc(gathered[b], 16)

        def place_windows(ch):
            v.tensor_scalar(BASE[:], BASE0[:], SHIFT[0:1, 0:1], float(NP), ALU.add, ALU.min)
            ch.step(v.tensor_scalar(REL[:], REL0[:], SHIFT[:, 0:1], None, ALU.subtract))
            v.tensor_scalar(PEN[:], REL[:], 0.0, GONE, ALU.is_lt, ALU.mult)
            ch.step(v.tensor_scalar(PROD[:].rearrange("p u n -> p (u n)")[:, 0:KP], REL[:], float(W), GONE, ALU.is_ge, ALU.mult))
            v.tensor_scalar(SHIFT[:], SHIFT[:], float(W), None, ALU.add)
            ch.step(v.tensor_tensor(PEN[:], PEN[:], PROD[:].rearrange("p u n -> p (u n)")[:, 0:KP], ALU.add))
            pass_wait(ch.eng)

        def select(b, k):
            return v.tensor_tensor(SEL[:, b % 2], times(IOTA[:, 0:W], U), per(REL[:, ds(k, U)], W), ALU.is_equal)

        def add_sums(dve, regs, before, parity, sum_chain, den_chain=None):
            for u in range(U):
                w = dve.snap(regs[u], min_val=0, max_val=NP)
                dve.wait_ge(sum_chain, before + (u + 1))
                v.tensor_tensor(ACC[:, ds(w, W)], ACC[:, ds(w, W)], PS[parity][:, u * W:(u + 1) * W],
                                ALU.add).then_inc(sum_chain, 1)
                if den_chain is not None:
                    dve.wait_ge(den_chain, before + (u + 1))
                    v.tensor_tensor(DEN[:, ds(w, W)], DEN[:, ds(w, W)],
                                    PS[2 + parity][0:1 + H, u * W:(u + 1) * W], ALU.add).then_inc(den_chain, 1)
            dve.wait_ge(sum_chain, before + (U + 1))
            if den_chain is not None:
                dve.wait_ge(den_chain, before + (U + 1))

        def edges0():
            ic_ready, pool_go, sel_ready, pe_done = sem("e0_ic"), sem("e0_go"), sem("e0_sel"), sem("e0_pe")
            rows_used, z_ready, w_ready, added = sem("e0_used"), sem("e0_z"), sem("e0_w"), sem("e0_added")
            acc_chain, den_chain, chain = sem("e0_acc"), sem("e0_den"), sem("e0_chain")
            pass_chain, zeroed = sem("e0_pass"), sem("e0_zeroed")
            red_in, red_out, guard_in, guard_out = sem("e0_red_in"), sem("e0_red_out"), sem("e0_gin"), sem("e0_gout")
            gathered = [sem(f"e0_gathered{b}") for b in range(RING)]
            cum_ready, cum_out = sem("e0_cum"), sem("e0_cumout")
            CUM = BUF[0:1, 3 * WIDE:3 * WIDE + NP]
            STEPS = 6
            with nc.Block() as block:
                @block.sync
                def _(sp):
                    sp.wait_ge(cum_ready, 1)
                    sp.dma_start(CUMD.unsqueeze(0), CUM).then_inc(cum_out, 16)
                    sp.wait_ge(cum_out, 16)

                @block.scalar
                def _(act):
                    first_indices(SRC, ic_ready)
                    with act.Fori(0, passes(act)) as pss:
                        with act.Fori(0, LAPS) as turn:
                            for b in range(RING):
                                act.wait_ge(z_ready, number(pss, turn, b) + 1)
                                a.activation(WE[:, b % 2, :, 1:1 + H], ZL[:, b % 2], ACT.Exp,
                                             bias=NSHIFT0[:]).then_inc(w_ready, 1)
                                next_indices(act, SRC, pss, turn, b, rows_used, ic_ready)
                    act.wait_ge(guard_in, 1)
                    a.activation(SC[:, 3:4], SC[:, 2:3], ACT.Exp, bias=NSHIFT0[:]).then_inc(guard_out, 1)

                @block.gpsimd
                def _(pool):
                    gather_rows(pool, T0, D + H, ic_ready, pool_go, gathered)
                    pool.wait_ge(red_in, 1)
                    g.partition_all_reduce(SC[:, 1:2], SC[:, 0:1], P, RMAX).then_inc(red_out, 1)

                @block.tensor
                def _(pe):
                    t.matmul(PS[1][:, 0:U * W], ZERO[:, 0:P], ZERO[:], start=True, stop=True)
                    t.matmul(PS[3][0:1 + H, 0:U * W], ZERO[:, 0:1 + H], ZERO[:], start=True,
                             stop=True).then_inc(pe_done, 2)
                    with pe.Fori(0, passes(pe)) as pss:
                        with pe.Fori(0, LAPS) as turn:
                            for b in range(RING):
                                i = number(pss, turn, b)
                                pe.wait_ge(sel_ready, i + 1)
                                pe.wait_ge(added, i + 1)
                                for u in range(U):
                                    s = SEL[:, b % 2, u, :]
                                    t.matmul(PS[b % 2][:, u * W:(u + 1) * W], GW[:, b % 2, u, :], s,
                                             start=True, stop=True)
                                    last = t.matmul(PS[2 + b % 2][0:1 + H, u * W:(u + 1) * W],
                                                    WE[:, b % 2, u, :], s, start=True, stop=True)
                                last.then_inc(pe_done, 1)

                @block.vector
                def _(dve):
                    regs = [[dve.alloc_register(f"e0_base{q}_{u}") for u in range(U)] for q in range(2)]
                    v.memset(ACC[:], 0.0).then_inc(acc_chain, 1)
                    v.memset(DEN[:], 0.0).then_inc(den_chain, 1)
                    v.memset(SHIFT[:], 0.0)
                    v.memset(WE[:], 1.0)
                    v.memset(ZMAX[:], GONE).then_inc(zeroed, 1)
                    dve.wait_ge(zeroed, 1)
                    dve.sem_inc(added, 1)
                    dve.reg_load(regs[1], BASE[0:1, 0:U])
                    np_ = passes(dve)
                    with dve.Fori(0, np_) as pss:
                        ch = Chain(dve, pass_chain, pss * 3)
                        place_windows(ch)
                        with dve.Fori(0, LAPS) as turn:
                            cg = None
                            for b in range(RING):
                                i = number(pss, turn, b)
                                k = tiles_of(dve, turn, b)
                                cg = Chain(dve, chain, i * STEPS)
                                dve.reg_load(regs[b % 2], BASE[0:1, ds(k, U)])
                                dve.wait_ge(pe_done, i + 1)
                                cg.step(select(b, k))
                                for u in range(U):
                                    w = dve.snap(regs[b % 2][u], min_val=0, max_val=NP)
                                    ins = v.tensor_tensor(PROD[:, u * H:(u + 1) * H, :],
                                                          times(SEL[:, b % 2, u, :], H), TB[:, :, ds(w, W)], ALU.mult)
                                cg.step(ins)
                                cg.step(v.tensor_reduce(Z[:], PROD[:].rearrange("p (u h) n -> p u h n", h=H),
                                                        AXX, ALU.add))
                                dve.wait_ge(gathered[b], (pss * LAPS + turn) * (16 * U) + 16 * U)
                                cg.step(v.tensor_tensor(Z[:], Z[:], G[:, b, :, D:D + H], ALU.add))
                                cg.step(v.tensor_tensor(Z[:], Z[:], per(PEN[:, ds(k, U)], H), ALU.add))
                                v.tensor_tensor(ZMAX[:], ZMAX[:], Z[:], ALU.max)
                                v.scalar_tensor_tensor(ZL[:, b % 2], Z[:], SLOPE0, Z[:], ALU.mult,
                                                       ALU.max).then_inc(z_ready, 1)
                                dve.wait_ge(pe_done, i + 2)
                                add_sums(dve, regs[1 - b % 2], i * U, 1 - b % 2, acc_chain, den_chain)
                                dve.sem_inc(added, 1)
                                dve.wait_ge(w_ready, i + 1)
                                cg.step(v.tensor_tensor(
                                    GW[:, b % 2].rearrange("p u (h f) -> p u h f", h=H),
                                    G[:, b, :, 0:D].rearrange("p u (h f) -> p u h f", h=H),
                                    per(WE[:, b % 2, :, 1:1 + H], DH), ALU.mult))
                                dve.sem_inc(rows_used, 1)
                                dve.sem_inc(sel_ready, 1)
                                assert cg.n == STEPS
                    dve.wait_ge(pe_done, np_ * GROUPS + 2)
                    add_sums(dve, regs[1], np_ * (GROUPS * U), 1, acc_chain, den_chain)
                    ce = Chain(dve, zeroed, 1)
                    ce.step(v.memset(ONE[:], 1.0))
                    ce.step(v.tensor_tensor_scan(CUM, ONE[0:1, 0:1].to_broadcast([1, NP]), DEN[0:1, 0:NP], 0.0,
                                                 ALU.mult, ALU.add))
                    dve.sem_inc(cum_ready, 1)
                    ce.step(v.tensor_reduce(SC[:, 0:1], ZMAX[:].rearrange("p u h -> p (u h)"), AXX, ALU.max))
                    dve.sem_inc(red_in, 1)
                    dve.wait_ge(red_out, 1)
                    ce.step(v.scalar_tensor_tensor(SC[:, 2:3], SC[:, 1:2], SLOPE0, SC[:, 1:2], ALU.mult, ALU.max))
                    dve.sem_inc(guard_in, 1)
                    dve.wait_ge(guard_out, 1)
                    ce.step(v.tensor_scalar(GUARD0[:], SC[:, 3:4], 1e-16, None, ALU.mult))

        def edges1():
            ic_ready, pool_go, sel_ready, pe_done = sem("e1_ic"), sem("e1_go"), sem("e1_sel"), sem("e1_pe")
            added, acc_chain, pass_chain, zeroed = sem("e1_added"), sem("e1_acc"), sem("e1_pass"), sem("e1_zeroed")
            rows_used = sem("e1_used")
            gathered = [sem(f"e1_gathered{b}") for b in range(RING)]
            with nc.Block() as block:
                @block.scalar
                def _(act):
                    first_indices(SRC, ic_ready)
                    with act.Fori(0, passes(act)) as pss:
                        with act.Fori(0, LAPS) as turn:
                            for b in range(RING):
                                k = act.snap(turn * AHEAD + (b * U + AHEAD), min_val=AHEAD, max_val=K + AHEAD - U)
                                act.wait_ge(pe_done, number(pss, turn, b) + 3)
                                a.copy(IC[:, b * U:(b + 1) * U], SRC[:, ds(k, U)]).then_inc(ic_ready, 1)

                @block.gpsimd
                def _(pool):
                    gather_rows(pool, T1, D, ic_ready, pool_go, gathered)

                @block.tensor
                def _(pe):
                    t.matmul(PS[1][:, 0:U * W], ZERO[:, 0:P], ZERO[:], start=True, stop=True).then_inc(pe_done, 2)
                    with pe.Fori(0, passes(pe)) as pss:
                        with pe.Fori(0, LAPS) as turn:
                            for b in range(RING):
                                i = number(pss, turn, b)
                                pe.wait_ge(gathered[b], (pss * LAPS + turn) * (16 * U) + 16 * U)
                                pe.wait_ge(sel_ready, i + 1)
                                pe.wait_ge(added, i + 1)
                                for u in range(U):
                                    last = t.matmul(PS[b % 2][:, u * W:(u + 1) * W], G[:, b, u, 0:D],
                                                    SEL[:, b % 2, u, :], start=True, stop=True)
                                last.then_inc(pe_done, 1)

                @block.vector
                def _(dve):
                    regs = [[dve.alloc_register(f"e1_base{q}_{u}") for u in range(U)] for q in range(2)]
                    v.memset(ACC[:], 0.0).then_inc(acc_chain, 1)
                    v.memset(SHIFT[:], 0.0).then_inc(zeroed, 1)
                    dve.wait_ge(zeroed, 1)
                    dve.sem_inc(added, 1)
                    dve.reg_load(regs[1], BASE[0:1, 0:U])
                    np_ = passes(dve)
                    with dve.Fori(0, np_) as pss:
                        place_windows(Chain(dve, pass_chain, pss * 3))
                        with dve.Fori(0, LAPS) as turn:
                            for b in range(RING):
                                i = number(pss, turn, b)
                                k = tiles_of(dve, turn, b)
                                dve.reg_load(regs[b % 2], BASE[0:1, ds(k, U)])
                                dve.wait_ge(pe_done, i + 1)
                                select(b, k).then_inc(sel_ready, 1)
                                dve.wait_ge(pe_done, i + 2)
                                add_sums(dve, regs[1 - b % 2], i * U, 1 - b % 2, acc_chain)
                                dve.sem_inc(added, 1)
                    dve.wait_ge(pe_done, np_ * GROUPS + 2)
                    add_sums(dve, regs[1], np_ * (GROUPS * U), 1, acc_chain)
                    pass_wait(dve)

        def edges2v():
            ic_ready, pool_go, hot_ready, pe_done = sem("ev_ic"), sem("ev_go"), sem("ev_hot"), sem("ev_pe")
            rows_used, z_ready, w_ready, last_sum = sem("ev_used"), sem("ev_z"), sem("ev_w"), sem("ev_last")
            chain, pass_chain, zeroed = sem("ev_chain"), sem("ev_pass"), sem("ev_zeroed")
            gathered = [sem(f"ev_gathered{b}") for b in range(RING)]
            STEPS = 7
            HOTW = GW[:, :, :, 0:NB]
            with nc.Block() as block:
                @block.scalar
                def _(act):
                    first_indices(SRC, ic_ready)
                    with act.Fori(0, passes(act)) as pss:
                        with act.Fori(0, LAPS) as turn:
                            for b in range(RING):
                                act.wait_ge(z_ready, number(pss, turn, b) + 1)
                                a.activation(WE[:, b % 2, :, 0], ZL[:, b % 2, :, 0], ACT.Exp).then_inc(w_ready, 1)
                                next_indices(act, SRC, pss, turn, b, rows_used, ic_ready)

                @block.gpsimd
                def _(pool):
                    gather_rows(pool, V2, 2, ic_ready, pool_go, gathered)

                @block.tensor
                def _(pe):
                    t.matmul(PS[0][:, 0:NB], ZERO[:, 0:P], ZERO[:, 0:NB], start=True, stop=False).then_inc(pe_done, 1)
                    with pe.Fori(0, passes(pe)) as pss:
                        with pe.Fori(0, LAPS) as turn:
                            for b in range(RING):
                                pe.wait_ge(hot_ready, number(pss, turn, b) + 1)
                                for u in range(U):
                                    last = t.matmul(PS[0][:, 0:NB], OLO[:, u, :], HOTW[:, b % 2, u, :],
                                                    start=False, stop=False)
                                last.then_inc(pe_done, 1)
                    t.matmul(PS[0][:, 0:NB], ZERO[:, 0:P], ZERO[:, 0:NB], start=False, stop=True).then_inc(last_sum, 1)

                @block.vector
                def _(dve):
                    regs = [dve.alloc_register(f"ev_base_{u}") for u in range(U)]
                    v.memset(SHIFT[:], 0.0).then_inc(zeroed, 1)
                    dve.wait_ge(zeroed, 1)
                    with dve.Fori(0, passes(dve)) as pss:
                        place_windows(Chain(dve, pass_chain, pss * 3))
                        with dve.Fori(0, LAPS) as turn:
                            for b in range(RING):
                                i = number(pss, turn, b)
                                k = tiles_of(dve, turn, b)
                                cg = Chain(dve, chain, i * STEPS)
                                dve.reg_load(regs, BASE[0:1, ds(k, U)])
                                cg.step(select(b, k))
                                for u in range(U):
                                    w = dve.snap(regs[u], min_val=0, max_val=NP)
                                    ins = v.tensor_tensor(PROD[:, u, :], SEL[:, b % 2, u, :], UB[:, ds(w, W)], ALU.mult)
                                cg.step(ins)
                                cg.step(v.tensor_reduce(Z[:, :, 0], PROD[:, 0:U, :], AXX, ALU.add))
                                dve.wait_ge(gathered[b], (pss * LAPS + turn) * (16 * U) + 16 * U)
                                cg.step(v.tensor_tensor(Z[:, :, 0], Z[:, :, 0], G[:, b, :, 0], ALU.add))
                                cg.step(v.scalar_tensor_tensor(Z[:, :, 0], Z[:, :, 0], SLOPE2, Z[:, :, 0],
                                                               ALU.mult, ALU.max))
                                cg.step(v.tensor_tensor(Z[:, :, 0], Z[:, :, 0], G[:, b, :, 1], ALU.subtract))
                                v.tensor_tensor(ZL[:, b % 2, :, 0], Z[:, :, 0], PEN[:, ds(k, U)],
                                                ALU.add).then_inc(z_ready, 1)
                                dve.sem_inc(rows_used, 1)
                                dve.wait_ge(pe_done, i + 1)
                                v.tensor_tensor(OLO, times(IOTA[:], U), per(LO[:, ds(k, U)], P), ALU.is_equal)
                                cg.step(v.tensor_tensor(HOTW[:, b % 2], times(IOTA[:, 0:NB], U),
                                                        per(HI[:, ds(k, U)], NB), ALU.is_equal))
                                dve.wait_ge(w_ready, i + 1)
                                v.tensor_tensor(HOTW[:, b % 2], HOTW[:, b % 2], per(WE[:, b % 2, :, 0], NB),
                                                ALU.mult).then_inc(hot_ready, 1)
                                assert cg.n == STEPS
                    dve.wait_ge(last_sum, 1)
                    ce = Chain(dve, zeroed, 1)
                    ce.step(v.tensor_scalar(RDEN[:], PS[0][:, 0:NB], TINY, None, ALU.max))
                    ce.step(v.reciprocal(RDEN[:], RDEN[:]))

        def edges2():
            ic_ready, pool_go, sel_ready, pe_done = sem("e2_ic"), sem("e2_go"), sem("e2_sel"), sem("e2_pe")
            rows_used, z_ready, w_ready, added = sem("e2_used"), sem("e2_z"), sem("e2_w"), sem("e2_added")
            acc_chain, chain = sem("e2_acc"), sem("e2_chain")
            pass_chain, zeroed = sem("e2_pass"), sem("e2_zeroed")
            gathered = [sem(f"e2_gathered{b}") for b in range(RING)]
            STEPS = 6
            with nc.Block() as block:
                @block.scalar
                def _(act):
                    first_indices(SRC, ic_ready)
                    with act.Fori(0, passes(act)) as pss:
                        with act.Fori(0, LAPS) as turn:
                            for b in range(RING):
                                act.wait_ge(z_ready, number(pss, turn, b) + 1)
                                a.activation(WE[:, b % 2, :, 0], ZL[:, b % 2, :, 0], ACT.Exp).then_inc(w_ready, 1)
                                k = act.snap(turn * AHEAD + (b * U + AHEAD), min_val=AHEAD, max_val=K + AHEAD - U)
                                act.wait_ge(pe_done, number(pss, turn, b) + 3)
                                a.copy(IC[:, b * U:(b + 1) * U], SRC[:, ds(k, U)]).then_inc(ic_ready, 1)

                @block.gpsimd
                def _(pool):
                    gather_rows(pool, T2, D + 2, ic_ready, pool_go, gathered)

                @block.tensor
                def _(pe):
                    t.matmul(PS[1][:, 0:U * W], ZERO[:, 0:P], ZERO[:], start=True, stop=True).then_inc(pe_done, 2)
                    with pe.Fori(0, passes(pe)) as pss:
                        with pe.Fori(0, LAPS) as turn:
                            for b in range(RING):
                                i = number(pss, turn, b)
                                pe.wait_ge(sel_ready, i + 1)
                                pe.wait_ge(gathered[b], (pss * LAPS + turn) * (16 * U) + 16 * U)
                                pe.wait_ge(added, i + 1)
                                for u in range(U):
                                    last = t.matmul(PS[b % 2][:, u * W:(u + 1) * W], G[:, b, u, 0:D],
                                                    SEL[:, b % 2, u, :], start=True, stop=True)
                                last.then_inc(pe_done, 1)

                @block.vector
                def _(dve):
                    regs = [[dve.alloc_register(f"e2_base{q}_{u}") for u in range(U)] for q in range(2)]
                    v.memset(ACC[:], 0.0).then_inc(acc_chain, 1)
                    v.memset(SHIFT[:], 0.0).then_inc(zeroed, 1)
                    dve.wait_ge(zeroed, 1)
                    dve.sem_inc(added, 1)
                    dve.reg_load(regs[1], BASE[0:1, 0:U])
                    np_ = passes(dve)
                    with dve.Fori(0, np_) as pss:
                        place_windows(Chain(dve, pass_chain, pss * 3))
                        with dve.Fori(0, LAPS) as turn:
                            for b in range(RING):
                                i = number(pss, turn, b)
                                k = tiles_of(dve, turn, b)
                                cg = Chain(dve, chain, i * STEPS)
                                dve.reg_load(regs[b % 2], BASE[0:1, ds(k, U)])
                                dve.wait_ge(pe_done, i + 1)
                                cg.step(select(b, k))
                                for u in range(U):
                                    w = dve.snap(regs[b % 2][u], min_val=0, max_val=NP)
                                    ins = v.tensor_tensor(PROD[:, u, :], SEL[:, b % 2, u, :], UB[:, ds(w, W)], ALU.mult)
                                cg.step(ins)
                                cg.step(v.tensor_reduce(Z[:, :, 0], PROD[:, 0:U, :], AXX, ALU.add))
                                dve.wait_ge(gathered[b], (pss * LAPS + turn) * (16 * U) + 16 * U)
                                cg.step(v.tensor_tensor(Z[:, :, 0], Z[:, :, 0], G[:, b, :, D], ALU.add))
                                cg.step(v.scalar_tensor_tensor(Z[:, :, 0], Z[:, :, 0], SLOPE2, Z[:, :, 0],
                                                               ALU.mult, ALU.max))
                                cg.step(v.tensor_tensor(Z[:, :, 0], Z[:, :, 0], G[:, b, :, D + 1], ALU.subtract))
                                v.tensor_tensor(ZL[:, b % 2, :, 0], Z[:, :, 0], PEN[:, ds(k, U)],
                                                ALU.add).then_inc(z_ready, 1)
                                dve.wait_ge(pe_done, i + 2)
                                add_sums(dve, regs[1 - b % 2], i * U, 1 - b % 2, acc_chain)
                                dve.sem_inc(added, 1)
                                dve.wait_ge(w_ready, i + 1)
                                v.tensor_tensor(SEL[:, b % 2], SEL[:, b % 2], per(WE[:, b % 2, :, 0], W),
                                                ALU.mult).then_inc(sel_ready, 1)
                                assert cg.n == STEPS
                    dve.wait_ge(pe_done, np_ * GROUPS + 2)
                    add_sums(dve, regs[1], np_ * (GROUPS * U), 1, acc_chain)
                    pass_wait(dve)

        def edges3():
            ic_ready, pool_go, turned, scanned = sem("e3_ic"), sem("e3_go"), sem("e3_turned"), sem("e3_scanned")
            back, copied, zeroed = sem("e3_back"), sem("e3_copied"), sem("e3_zeroed")
            gathered = [sem(f"e3_gathered{b}") for b in range(RING)]
            mask_in, stored = [sem("e3_mask0"), sem("e3_mask1")], [sem("e3_stored0"), sem("e3_stored1")]
            chain = sem("e3_chain")
            L = U * P
            MB = BUF[:, 3 * WIDE:3 * WIDE + L].bitcast(BF).rearrange("p (q e) -> p q e", q=2)
            RM = GW[:].rearrange("p q u f -> p q (u f)")
            RB = BUF[:, 3 * WIDE + L:3 * WIDE + 3 * L].rearrange("p (q u f) -> p q u f", q=2, u=U)
            groups_out = RUNS.rearrange("(i u p) f -> p i u f", u=U, p=P)
            with nc.Block() as block:
                @block.scalar
                def _(act):
                    first_indices(IDX3, ic_ready)
                    act.sem_inc(copied, 2)
                    with act.Fori(0, LAPS) as turn:
                        for b in range(RING):
                            i, q = turn * RING + b, 1 - b % 2
                            k = act.snap(turn * AHEAD + (b * U + AHEAD), min_val=AHEAD, max_val=K + AHEAD - U)
                            act.wait_ge(turned, i + 1)
                            a.copy(IC[:, b * U:(b + 1) * U], IDX3[:, ds(k, U)]).then_inc(ic_ready, 1)
                            act.wait_ge(back, i + 2)
                            act.wait_ge(stored[q], (turn * 2 + b // 2) * 16 + 16)
                            a.copy(RB[:, q, 0:4, :], PS[4 + 2 * q][:].rearrange("p (u f) -> p u f", u=4))
                            a.copy(RB[:, q, 4:8, :], PS[5 + 2 * q][:].rearrange("p (u f) -> p u f", u=4)).then_inc(copied, 1)
                    act.wait_ge(back, GROUPS + 2)
                    act.wait_ge(stored[1], (LAPS * 2) * 16 + 16)
                    a.copy(RB[:, 1, 0:4, :], PS[6][:].rearrange("p (u f) -> p u f", u=4))
                    a.copy(RB[:, 1, 4:8, :], PS[7][:].rearrange("p (u f) -> p u f", u=4)).then_inc(copied, 1)

                @block.gpsimd
                def _(pool):
                    gather_rows(pool, T3, D, ic_ready, pool_go, gathered, npass=1)

                @block.sync
                def _(sp):
                    sp.sem_inc(stored[0], 16)
                    sp.sem_inc(stored[1], 16)
                    sp.wait_ge(zeroed, 1)
                    with sp.Fori(0, LAPS) as turn:
                        for b in range(RING):
                            i, q = turn * RING + b, 1 - b % 2
                            sp.wait_ge(scanned, i + 1)
                            sp.dma_start(MB[:, b % 2, :], MASKD[ds(turn * (RING * L) + b * L, L)].unsqueeze(0)
                                         .to_broadcast([P, L])).then_inc(mask_in[b % 2], 16)
                            sp.wait_ge(copied, i + 3)
                            sp.dma_start(groups_out[:, ds(i, 1), :, :].rearrange("p i u f -> p (i u) f"),
                                         RB[:, q]).then_inc(stored[q], 16)
                    sp.wait_ge(copied, GROUPS + 3)
                    sp.dma_start(groups_out[:, GROUPS, :, :], RB[:, 1]).then_inc(stored[1], 16)
                    sp.wait_ge(stored[0], LAPS * 2 * 16 + 16)
                    sp.wait_ge(stored[1], LAPS * 2 * 16 + 32)

                def turn_back(pe, q):
                    for u in range(U):
                        last = t.transpose(PS[4 + 2 * q + u // 4][:, (u % 4) * P:(u % 4 + 1) * P],
                                           RM[:, q, u * P:(u + 1) * P], IDENT[:])
                    last.then_inc(back, 1)

                @block.tensor
                def _(pe):
                    pe.sem_inc(back, 1)
                    with pe.Fori(0, LAPS) as turn:
                        for b in range(RING):
                            i, q = turn * RING + b, b % 2
                            pe.wait_ge(gathered[b], turn * (16 * U) + 16 * U)
                            pe.wait_ge(scanned, i + 1)
                            for u in range(U):
                                last = t.transpose(PS[2 * q + u // 4][:, (u % 4) * P:(u % 4 + 1) * P],
                                                   G[:, b, u, 0:D], IDENT[:])
                            last.then_inc(turned, 1)
                            pe.wait_ge(scanned, i + 2)
                            pe.wait_ge(copied, i + 1)
                            turn_back(pe, 1 - q)
                    pe.wait_ge(scanned, GROUPS + 2)
                    pe.wait_ge(copied, GROUPS + 1)
                    turn_back(pe, 1)

                @block.vector
                def _(dve):
                    v.memset(GW[:], 0.0).then_inc(chain, 1)
                    dve.wait_ge(chain, 1)
                    dve.sem_inc(scanned, 2)
                    dve.sem_inc(zeroed, 1)
                    with dve.Fori(0, LAPS) as turn:
                        for b in range(RING):
                            i, q = turn * RING + b, b % 2
                            dve.wait_ge(turned, i + 1)
                            dve.wait_ge(mask_in[q], (turn * 2 + b // 2) * 16 + 16)
                            dve.wait_ge(back, i + 1)
                            for h in range(2):
                                before = RM[:, 1 - q, L - 1:L] if h == 0 else RM[:, q, L // 2 - 1:L // 2]
                                dve.wait_ge(chain, i * 2 + h + 1)
                                v.tensor_tensor_scan(RM[:, q, h * 512:(h + 1) * 512],
                                                     MB[:, q, h * 512:(h + 1) * 512], PS[2 * q + h][:],
                                                     before, ALU.min, ALU.max).then_inc(chain, 1)
                            dve.wait_ge(chain, i * 2 + 3)
                            dve.sem_inc(scanned, 1)

        def moments(ch, b, nb, blk):
            pass_wait(ch.eng)
            for j in range(nb):
                ins = v.bn_stats(BN6[:, b, j, :], X[:, ds(blk + j, 1), :].rearrange("p o f -> p (o f)"))
            ch.step(ins)
            pass_wait(ch.eng)
            for j in range(nb):
                ins = v.bn_aggr(SM[:, b, j, 4:6], BN6[:, b, j, :])
            ch.step(ins)
            return v.tensor_copy(MV[:, ds(blk, nb), :], SM[:, b, 0:nb, 4:6])

        def normalize(dve, ch, root_in, root_out):
            ch.step(v.tensor_copy(RSTD[:], MV[:, :, 1]))
            dve.sem_inc(root_in, 1)
            dve.wait_ge(root_out, 1)
            ch.step(v.reciprocal(RSTD[:], RSTD[:]))
            ch.step(v.scalar_tensor_tensor(NBIA[:], MV[:, :, 0], -1.0, RSTD[:], ALU.mult, ALU.mult))

        def rows(ap, nb):
            return ap[:, 0:nb * P].rearrange("p (b f) -> p b f", f=D)

        def close0():
            w_in, sums_ready, pe_done, taken, chain = sem("c0_w"), sem("c0_sums"), sem("c0_pe"), sem("c0_taken"), sem("c0_chain")
            x_in, x_used, x_tail, sx_zero = [sem("c0_x0"), sem("c0_x1")], sem("c0_xused"), sem("c0_xtail"), sem("c0_sxzero")
            STEPS = 8
            B0 = WS[:, 0:D]
            with nc.Block() as block:
                @block.sync
                def _(sp):
                    sp.dma_start(B0, bias0.to_broadcast([P, D])).then_inc(w_in, 16)
                    with sp.Fori(0, NODE_TURNS - 1) as turn:
                        for b in range(2):
                            i, nb, blk, col = half(turn, b)
                            sp.wait_ge(x_used, i + 1)
                            sp.dma_start(rows(SX[:, b], nb),
                                         x[ds(col, nb * P), :].rearrange("(b p) f -> p b f", p=P)).then_inc(x_in[b], 16)
                    last = NODE_TURNS - 1
                    for b in range(2):
                        i, nb, blk, col = half(last, b)
                        whole = nb - b
                        sp.wait_ge(x_used, i + 1)
                        if b:
                            sp.dma_start(SX[0:LAST, b, whole * P:nb * P], x[(NB - 1) * P:N]).then_inc(x_tail, 16)
                            sp.wait_ge(x_tail, 16)
                        sp.dma_start(rows(SX[:, b], whole),
                                     x[col:col + whole * P].rearrange("(b p) f -> p b f", p=P)).then_inc(x_in[b], 16)
                    sp.wait_ge(w_in, 16)

                @block.scalar
                def _(act):
                    with act.Fori(0, NODE_TURNS) as turn:
                        for b in range(2):
                            i, nb, blk, col = half(turn, b)
                            act.wait_ge(pe_done, i + 1)
                            a.copy(SA[:, b, 0:nb * P], ACC[:, ds(col, nb * P)])
                            a.copy(SD[:, b, 0:nb * P], DEN[:, ds(col, nb * P)]).then_inc(sums_ready, 1)

                @block.tensor
                def _(pe):
                    pe.sem_inc(pe_done, 2)
                    with pe.Fori(0, NODE_TURNS) as turn:
                        for b in range(2):
                            i, nb, blk, col = half(turn, b)
                            pe.wait_ge(sums_ready, i + 1)
                            pe.wait_ge(taken, i + 1)
                            for j in range(nb):
                                t.transpose(PS[b][:, j * P:(j + 1) * P], SA[:, b, j * P:(j + 1) * P], IDENT[:])
                                last = t.transpose(PS[2 + b][:, j * 8:j * 8 + 1 + H], SD[:, b, j * P:(j + 1) * P],
                                                   IDENT[0:1 + H, 0:1 + H])
                            last.then_inc(pe_done, 1)

                @block.vector
                def _(dve):
                    dve.sem_inc(taken, 2)
                    v.memset(SX[:], 0.0).then_inc(sx_zero, 1)
                    dve.wait_ge(sx_zero, 1)
                    dve.sem_inc(x_used, 2)
                    dve.wait_ge(w_in, 16)
                    with dve.Fori(0, NODE_TURNS) as turn:
                        for b in range(2):
                            i, nb, blk, col = half(turn, b)
                            ch = Chain(dve, chain, i * STEPS)
                            den = PS[2 + b][:, 0:nb * 8].rearrange("p (b h) -> p b h", h=8)
                            rec = SM[:, b, 0:nb, 0:H]
                            heads = lambda y: y.rearrange("p (c f) -> p c f", f=DH)
                            Y = YS[:, b, 0:nb * P]
                            dve.wait_ge(pe_done, i + 3)
                            v.tensor_copy(DEG[:, ds(blk, nb)], den[:, :, 0])
                            ch.step(v.tensor_scalar(rec, den[:, :, 1:1 + H], GUARD0[:], None, ALU.add))
                            ch.step(v.reciprocal(rec, rec))
                            ch.step(v.tensor_tensor(Y.rearrange("p (b h f) -> p b h f", h=H, f=DH),
                                                    PS[b][:, 0:nb * P].rearrange("p (b h f) -> p b h f", h=H, f=DH),
                                                    per(rec, DH), ALU.mult))
                            dve.sem_inc(taken, 1)
                            ch.step(v.tensor_tensor(rows(Y, nb), rows(Y, nb), times(B0, nb), ALU.add))
                            dve.wait_ge(x_in[b], turn * 16 + 16)
                            ch.step(v.tensor_tensor(X[:, ds(blk, nb), :], rows(SX[:, b], nb), rows(Y, nb), ALU.add))
                            dve.sem_inc(x_used, 1)
                            ch.step(moments(ch, b, nb, blk))
                            assert ch.n == STEPS

        def open1():
            w_in, root_in, root_out, chain = sem("o1_w"), sem("o1_rin"), sem("o1_rout"), sem("o1_chain")
            loop_chain, sx_ready, x_done, pe_turned = sem("o1_lchain"), sem("o1_sx"), sem("o1_x"), sem("o1_turned")
            sa_ready, pe_done, hs_done = sem("o1_sa"), sem("o1_pe"), sem("o1_hs")
            cum_in = sem("o1_cumin")
            stored = [sem("o1_stored0"), sem("o1_stored1")]
            table = T1.rearrange("(b p) f -> p b f", p=P)
            with nc.Block() as block:
                @block.sync
                def _(sp):
                    sp.dma_start(WS[:, 0:D], w_selfT).then_inc(w_in, 16)
                    sp.dma_start(WB[0:1, 0:D], b_self).then_inc(w_in, 16)
                    sp.sem_inc(stored[0], 16)
                    sp.sem_inc(stored[1], 16)
                    sp.dma_start(ENDF[:], CUMD.rearrange("(b p) -> p b", p=P), allow_slow_non_contiguous=True).then_inc(cum_in, 16)
                    with sp.Fori(0, NODE_TURNS) as turn:
                        for b in range(2):
                            i, nb, blk, col = half(turn, b)
                            sp.wait_ge(sx_ready, i + 1)
                            sp.dma_start(table[:, ds(blk, nb), :], rows(SX[:, b], nb)).then_inc(stored[b], 16)
                    sp.wait_ge(stored[0], NODE_TURNS * 16 + 16)
                    sp.wait_ge(stored[1], NODE_TURNS * 16 + 16)
                    sp.wait_ge(cum_in, 16)

                @block.vector
                def _(dve):
                    ch = Chain(dve, chain)
                    normalize(dve, ch, root_in, root_out)
                    with dve.Fori(0, NODE_TURNS) as turn:
                        for b in range(2):
                            i, nb, blk, col = half(turn, b)
                            cl = Chain(dve, loop_chain, i)
                            dve.wait_ge(stored[b], turn * 16 + 16)
                            dve.wait_ge(x_done, i + 1)
                            dve.wait_ge(pe_turned, i + 1)
                            cl.step(v.tensor_tensor(rows(YS[:, b], nb), X[:, ds(blk, nb), :],
                                                    per(RSTD[:, ds(blk, nb)], D), ALU.mult))
                            v.tensor_tensor(rows(SX[:, b], nb), rows(YS[:, b], nb),
                                            per(NBIA[:, ds(blk, nb)], D), ALU.add).then_inc(sx_ready, 1)
                    ch.step(v.tensor_scalar(RDEG[:], DEG[:], 1.0, None, ALU.max))
                    v.reciprocal(RDEG[:], RDEG[:])
                    v.tensor_scalar(HAS[:], DEG[:], 0.0, None, ALU.is_gt)
                    dve.wait_ge(cum_in, 16)
                    ch.step(v.tensor_scalar(ENDF[:], ENDF[:], -1.0, 0.0, ALU.add, ALU.max))
                    ch.step(v.tensor_scalar(ENDI[:], ENDF[:], float(U * P), None, ALU.add))

                @block.gpsimd
                def _(pool):
                    pool.sem_inc(x_done, 2)
                    with pool.Fori(0, NODE_TURNS) as turn:
                        for b in range(2):
                            i, nb, blk, col = half(turn, b)
                            pool.wait_ge(sx_ready, i + 1)
                            g.tensor_copy(X[:, ds(blk, nb), :], rows(SX[:, b], nb)).then_inc(x_done, 1)

                @block.tensor
                def _(pe):
                    pe.sem_inc(pe_turned, 2)
                    pe.wait_ge(w_in, 32)
                    with pe.Fori(0, NODE_TURNS) as turn:
                        for b in range(2):
                            i, nb, blk, col = half(turn, b)
                            pe.wait_ge(sx_ready, i + 1)
                            pe.wait_ge(hs_done, i + 1)
                            for j in range(nb):
                                last = t.transpose(PS[b][:, j * P:(j + 1) * P], SX[:, b, j * P:(j + 1) * P], IDENT[:])
                            last.then_inc(pe_turned, 1)
                            pe.wait_ge(sa_ready, i + 1)
                            for j in range(nb):
                                o = PS[2 + b][:, j * P:(j + 1) * P]
                                t.matmul(o, SA[:, b, j * P:(j + 1) * P], WS[:, 0:D], start=True, stop=False)
                                last = t.matmul(o, ONE[0:1, :], WB[0:1, 0:D], start=False, stop=True)
                            last.then_inc(pe_done, 1)

                @block.scalar
                def _(act):
                    act.sem_inc(hs_done, 2)
                    act.wait_ge(root_in, 1)
                    a.activation(RSTD[:], RSTD[:], ACT.Sqrt, bias=EPS[:]).then_inc(root_out, 1)
                    with act.Fori(0, NODE_TURNS) as turn:
                        for b in range(2):
                            i, nb, blk, col = half(turn, b)
                            act.wait_ge(pe_turned, i + 3)
                            a.copy(SA[:, b, 0:nb * P], PS[b][:, 0:nb * P]).then_inc(sa_ready, 1)
                            act.wait_ge(pe_done, i + 1)
                            a.copy(HS[:, ds(blk, nb), :], rows(PS[2 + b], nb)).then_inc(hs_done, 1)

        def close1():
            w_in, sums_ready, pe_done, taken, chain = sem("c1_w"), sem("c1_sums"), sem("c1_pe"), sem("c1_taken"), sem("c1_chain")
            root_in, root_out, going = sem("c1_rin"), sem("c1_rout"), sem("c1_going")
            STEPS = 14
            GA, BE = WS[:, D:2 * D], WS[:, 2 * D:3 * D]
            with nc.Block() as block:
                @block.sync
                def _(sp):
                    sp.dma_start(WS[:, 0:D], w_msgT).then_inc(w_in, 16)
                    sp.dma_start(GA, gamma.to_broadcast([P, D])).then_inc(w_in, 16)
                    sp.dma_start(BE, beta.to_broadcast([P, D])).then_inc(w_in, 16)
                    sp.wait_ge(w_in, 48)

                @block.scalar
                def _(act):
                    with act.Fori(0, NODE_TURNS) as turn:
                        for b in range(2):
                            i, nb, blk, col = half(turn, b)
                            act.wait_ge(root_in, i + 1)
                            a.activation(SM[:, b, 0:nb, 2], SM[:, b, 0:nb, 5], ACT.Sqrt,
                                         bias=EPS[:]).then_inc(root_out, 1)

                @block.gpsimd
                def _(pool):
                    with pool.Fori(0, NODE_TURNS) as turn:
                        for b in range(2):
                            i, nb, blk, col = half(turn, b)
                            pool.wait_ge(pe_done, i + 1)
                            pool.sem_inc(going, 1)
                            g.tensor_copy(SA[:, b, 0:nb * P], ACC[:, ds(col, nb * P)]).then_inc(sums_ready, 1)

                @block.tensor
                def _(pe):
                    pe.sem_inc(pe_done, 2)
                    pe.wait_ge(w_in, 48)
                    with pe.Fori(0, NODE_TURNS) as turn:
                        for b in range(2):
                            i, nb, blk, col = half(turn, b)
                            pe.wait_ge(sums_ready, i + 1)
                            pe.wait_ge(taken, i + 1)
                            for j in range(nb):
                                last = t.matmul(PS[b][:, j * P:(j + 1) * P], SA[:, b, j * P:(j + 1) * P],
                                                WS[:, 0:D], start=True, stop=True)
                            last.then_inc(pe_done, 1)

                @block.vector
                def _(dve):
                    dve.sem_inc(taken, 2)
                    dve.wait_ge(w_in, 48)
                    with dve.Fori(0, NODE_TURNS) as turn:
                        for b in range(2):
                            i, nb, blk, col = half(turn, b)
                            ch = Chain(dve, chain, i * STEPS)
                            Y = rows(YS[:, b], nb)
                            mean, dev = SM[:, b, 0:nb, 4], SM[:, b, 0:nb, 2]
                            dve.wait_ge(pe_done, i + 3)
                            ch.step(v.tensor_tensor(Y, rows(PS[b], nb), per(RDEG[:, ds(blk, nb)], D), ALU.mult))
                            dve.sem_inc(taken, 1)
                            ch.step(v.tensor_tensor(Y, Y, HS[:, ds(blk, nb), :], ALU.add))
                            ch.step(v.tensor_scalar(Y, Y, 0.0, None, ALU.max))
                            for j in range(nb):
                                ins = v.bn_stats(BN6[:, b, j, :], YS[:, b, j * P:(j + 1) * P])
                            ch.step(ins)
                            pass_wait(dve)
                            for j in range(nb):
                                ins = v.bn_aggr(SM[:, b, j, 4:6], BN6[:, b, j, :])
                            ch.step(ins)
                            dve.sem_inc(root_in, 1)
                            ch.step(v.tensor_tensor(Y, Y, per(mean, D), ALU.subtract))
                            dve.wait_ge(root_out, i + 1)
                            ch.step(v.reciprocal(dev, dev))
                            ch.step(v.tensor_tensor(Y, Y, per(dev, D), ALU.mult))
                            ch.step(v.tensor_tensor(Y, Y, times(GA, nb), ALU.mult))
                            ch.step(v.tensor_tensor(Y, Y, times(BE, nb), ALU.add))
                            ch.step(v.tensor_tensor(X[:, ds(blk, nb), :], X[:, ds(blk, nb), :], Y, ALU.add))
                            ch.step(moments(ch, b, nb, blk))
                            assert ch.n == STEPS

        def open2():
            w_in, root_in, root_out, chain = sem("o2_w"), sem("o2_rin"), sem("o2_rout"), sem("o2_chain")
            loop_chain, sx_ready, x_done, pe_turned = sem("o2_lchain"), sem("o2_sx"), sem("o2_x"), sem("o2_turned")
            sa_ready, pe_done, u_done, w_ready = sem("o2_sa"), sem("o2_pe"), sem("o2_u"), sem("o2_wready")
            stored, shifts, going = sem("o2_stored"), sem("o2_shifts"), sem("o2_going")
            with nc.Block() as block:
                @block.sync
                def _(sp):
                    sp.dma_start(WS[:, 0:1], w_i).then_inc(w_in, 16)
                    sp.dma_start(WS[:, 1:2], w_j).then_inc(w_in, 16)
                    sp.wait_ge(shifts, 1)
                    with nc.allow_non_contiguous_dma("pairs"):
                        sp.dma_start(V2.rearrange("(b p) f -> p b f", p=P), VC[:]).then_inc(stored, 16)
                    sp.wait_ge(stored, 16)

                @block.vector
                def _(dve):
                    ch = Chain(dve, chain)
                    normalize(dve, ch, root_in, root_out)
                    v.memset(UB[:, NP:WIDE], 0.0)
                    dve.wait_ge(w_in, 32)
                    ch.step(v.tensor_copy(WB[:, 0:D], WS[:, 0:1].to_broadcast([P, D])))
                    dve.sem_inc(w_ready, 1)
                    with dve.Fori(0, NODE_TURNS) as turn:
                        for b in range(2):
                            i, nb, blk, col = half(turn, b)
                            cl = Chain(dve, loop_chain, i)
                            dve.wait_ge(x_done, i + 1)
                            dve.wait_ge(pe_turned, i + 1)
                            cl.step(v.tensor_tensor(rows(YS[:, b], nb), X[:, ds(blk, nb), :],
                                                    per(RSTD[:, ds(blk, nb)], D), ALU.mult))
                            v.tensor_tensor(rows(SX[:, b], nb), rows(YS[:, b], nb),
                                            per(NBIA[:, ds(blk, nb)], D), ALU.add).then_inc(sx_ready, 1)
                    ch.step(v.tensor_scalar(HI.bitcast(I32), SRC[:], P - 1, None, ALU.bitwise_and))
                    ch.step(v.tensor_copy(LO, HI.bitcast(I32)))
                    ch.step(v.tensor_scalar(REL[:].bitcast(I32), SRC[:], 7, None, ALU.logical_shift_right))
                    v.tensor_copy(HI, REL[:].bitcast(I32))
                    dve.wait_ge(u_done, 2 * NODE_TURNS + 2)
                    ch.step(v.tensor_reduce(SC[:, 0:1], UB[:, 0:N], AXX, ALU.max))
                    ch.step(v.tensor_scalar(VC[:, :, 1], VC[:, :, 0], SC[:, 0:1], None, ALU.add))
                    ch.step(v.scalar_tensor_tensor(VC[:, :, 1], VC[:, :, 1], SLOPE2, VC[:, :, 1], ALU.mult, ALU.max))
                    dve.sem_inc(shifts, 1)

                @block.gpsimd
                def _(pool):
                    pool.sem_inc(x_done, 2)
                    with pool.Fori(0, NODE_TURNS) as turn:
                        for b in range(2):
                            i, nb, blk, col = half(turn, b)
                            pool.wait_ge(sx_ready, i + 1)
                            pool.sem_inc(going, 1)
                            g.tensor_copy(X[:, ds(blk, nb), :], rows(SX[:, b], nb)).then_inc(x_done, 1)

                @block.tensor
                def _(pe):
                    pe.sem_inc(pe_turned, 2)
                    pe.wait_ge(w_ready, 1)
                    with pe.Fori(0, NODE_TURNS) as turn:
                        for b in range(2):
                            i, nb, blk, col = half(turn, b)
                            pe.wait_ge(sx_ready, i + 1)
                            pe.wait_ge(u_done, i + 1)
                            for j in range(nb):
                                last = t.transpose(PS[b][:, j * P:(j + 1) * P], SX[:, b, j * P:(j + 1) * P], IDENT[:])
                            last.then_inc(pe_turned, 1)
                            pe.wait_ge(sa_ready, i + 1)
                            for j in range(nb):
                                t.matmul(PS[2 + b][:, j:j + 1], SA[:, b, j * P:(j + 1) * P], WS[:, 1:2],
                                         start=True, stop=True)
                            t.matmul(PS[4 + b][:, 0:nb * P], WB[:, 0:D], SA[:, b, 0:nb * P],
                                     start=True, stop=True).then_inc(pe_done, 1)

                @block.scalar
                def _(act):
                    act.sem_inc(u_done, 2)
                    act.wait_ge(root_in, 1)
                    a.activation(RSTD[:], RSTD[:], ACT.Sqrt, bias=EPS[:]).then_inc(root_out, 1)
                    with act.Fori(0, NODE_TURNS) as turn:
                        for b in range(2):
                            i, nb, blk, col = half(turn, b)
                            act.wait_ge(pe_turned, i + 3)
                            a.copy(SA[:, b, 0:nb * P], PS[b][:, 0:nb * P]).then_inc(sa_ready, 1)
                            act.wait_ge(pe_done, i + 1)
                            a.copy(VC[:, ds(blk, nb), 0], PS[2 + b][:, 0:nb])
                            a.copy(UB[:, ds(col, nb * P)], PS[4 + b][:, 0:nb * P]).then_inc(u_done, 1)

        def table2():
            made, stored = sem("t2_made"), [sem("t2_stored0"), sem("t2_stored1")]
            table = T2.rearrange("(b p) f -> p b f", p=P)
            with nc.Block() as block:
                @block.sync
                def _(sp):
                    sp.sem_inc(stored[0], 16)
                    sp.sem_inc(stored[1], 16)
                    with sp.Fori(0, NODE_TURNS) as turn:
                        for b in range(2):
                            i, nb, blk, col = half(turn, b)
                            sp.wait_ge(made, i + 1)
                            sp.dma_start(table[:, ds(blk, nb), :], YW[:, 4 * b:4 * b + nb, 0:D + 2]).then_inc(stored[b], 16)
                    sp.wait_ge(stored[0], NODE_TURNS * 16 + 16)
                    sp.wait_ge(stored[1], NODE_TURNS * 16 + 16)

                @block.vector
                def _(dve):
                    with dve.Fori(0, NODE_TURNS) as turn:
                        for b in range(2):
                            i, nb, blk, col = half(turn, b)
                            dve.wait_ge(stored[b], turn * 16 + 16)
                            v.tensor_tensor(YW[:, 4 * b:4 * b + nb, 0:D], X[:, ds(blk, nb), :],
                                            per(RDEN[:, ds(blk, nb)], D), ALU.mult)
                            v.tensor_copy(YW[:, 4 * b:4 * b + nb, D:D + 2], VC[:, ds(blk, nb), :]).then_inc(made, 1)

        def close2():
            sums_ready, pe_done, taken, chain = sem("c2_sums"), sem("c2_pe"), sem("c2_taken"), sem("c2_chain")
            STEPS = 4
            with nc.Block() as block:
                @block.scalar
                def _(act):
                    with act.Fori(0, NODE_TURNS) as turn:
                        for b in range(2):
                            i, nb, blk, col = half(turn, b)
                            act.wait_ge(pe_done, i + 1)
                            a.copy(SA[:, b, 0:nb * P], ACC[:, ds(col, nb * P)]).then_inc(sums_ready, 1)

                @block.tensor
                def _(pe):
                    pe.sem_inc(pe_done, 2)
                    with pe.Fori(0, NODE_TURNS) as turn:
                        for b in range(2):
                            i, nb, blk, col = half(turn, b)
                            pe.wait_ge(sums_ready, i + 1)
                            pe.wait_ge(taken, i + 1)
                            for j in range(nb):
                                last = t.transpose(PS[b][:, j * P:(j + 1) * P], SA[:, b, j * P:(j + 1) * P], IDENT[:])
                            last.then_inc(pe_done, 1)

                @block.vector
                def _(dve):
                    dve.sem_inc(taken, 2)
                    with dve.Fori(0, NODE_TURNS) as turn:
                        for b in range(2):
                            i, nb, blk, col = half(turn, b)
                            ch = Chain(dve, chain, i * STEPS)
                            dve.wait_ge(pe_done, i + 3)
                            ch.step(v.scalar_tensor_tensor(X[:, ds(blk, nb), :], rows(PS[b], nb), 0.0,
                                                           X[:, ds(blk, nb), :], ALU.max, ALU.add))
                            dve.sem_inc(taken, 1)
                            ch.step(moments(ch, b, nb, blk))
                            assert ch.n == STEPS

        def open3():
            w_in, root_in, root_out, chain = sem("o3_w"), sem("o3_rin"), sem("o3_rout"), sem("o3_chain")
            loop_chain, sx_ready, x_done, pe_turned = sem("o3_lchain"), sem("o3_sx"), sem("o3_x"), sem("o3_turned")
            sa_ready, pe_done, hs_done, msg_done = sem("o3_sa"), sem("o3_pe"), sem("o3_hs"), sem("o3_msg")
            idx_in, going = sem("o3_idx"), sem("o3_going")
            stored = [sem("o3_stored0"), sem("o3_stored1")]
            table = T3.rearrange("(r b p) f -> p r b f", r=R, p=P)
            MS = BUF[:, 3 * WIDE:3 * WIDE + 8 * R * D].rearrange("p (q b m) -> p q b m", q=2, b=4)
            BR = WB[:, 0:R * D]
            with nc.Block() as block:
                @block.sync
                def _(sp):
                    sp.dma_start(WS[:].rearrange("p (r f) -> p r f", r=R + 1),
                                 w_rel.rearrange("r k f -> k r f")).then_inc(w_in, 16)
                    sp.dma_start(BR, b_rel[0:R, :].rearrange("r f -> (r f)").unsqueeze(0).to_broadcast([P, R * D])).then_inc(w_in, 16)
                    sp.dma_start(WB[:, R * D:(R + 1) * D], b_rel[R:R + 1, :].to_broadcast([P, D])).then_inc(w_in, 16)
                    sp.dma_start(IDX3, IDX3D).then_inc(idx_in, 16)
                    sp.sem_inc(stored[0], 16 * R)
                    sp.sem_inc(stored[1], 16 * R)
                    with sp.Fori(0, NODE_TURNS) as turn:
                        for b in range(2):
                            i, nb, blk, col = half(turn, b)
                            sp.wait_ge(msg_done, i + 3)
                            for r in range(R):
                                sp.dma_start(table[:, r, ds(blk, nb), :],
                                             MS[:, b, 0:nb, r * D:(r + 1) * D]).then_inc(stored[b], 16)
                    sp.wait_ge(stored[0], (NODE_TURNS + 1) * 16 * R)
                    sp.wait_ge(stored[1], (NODE_TURNS + 1) * 16 * R)
                    sp.wait_ge(idx_in, 16)

                @block.vector
                def _(dve):
                    ch = Chain(dve, chain)
                    normalize(dve, ch, root_in, root_out)
                    dve.sem_inc(msg_done, 2)
                    dve.wait_ge(w_in, 48)
                    with dve.Fori(0, NODE_TURNS) as turn:
                        for b in range(2):
                            i, nb, blk, col = half(turn, b)
                            cl = Chain(dve, loop_chain, i)
                            dve.wait_ge(x_done, i + 1)
                            dve.wait_ge(pe_turned, i + 1)
                            cl.step(v.tensor_tensor(rows(YS[:, b], nb), X[:, ds(blk, nb), :],
                                                    per(RSTD[:, ds(blk, nb)], D), ALU.mult))
                            v.tensor_tensor(rows(SX[:, b], nb), rows(YS[:, b], nb),
                                            per(NBIA[:, ds(blk, nb)], D), ALU.add).then_inc(sx_ready, 1)
                            dve.wait_ge(pe_done, i + 1)
                            dve.wait_ge(stored[b], turn * (16 * R) + 16 * R)
                            for j in range(nb):
                                ins = v.tensor_tensor(MS[:, b, j, :], PS[2 + j][:], BR, ALU.add)
                            ins.then_inc(msg_done, 1)

                @block.gpsimd
                def _(pool):
                    pool.sem_inc(x_done, 2)
                    with pool.Fori(0, NODE_TURNS) as turn:
                        for b in range(2):
                            i, nb, blk, col = half(turn, b)
                            pool.wait_ge(sx_ready, i + 1)
                            pool.sem_inc(going, 1)
                            g.tensor_copy(X[:, ds(blk, nb), :], rows(SX[:, b], nb)).then_inc(x_done, 1)

                @block.tensor
                def _(pe):
                    pe.sem_inc(pe_turned, 2)
                    pe.wait_ge(w_in, 48)
                    with pe.Fori(0, NODE_TURNS) as turn:
                        for b in range(2):
                            i, nb, blk, col = half(turn, b)
                            pe.wait_ge(sx_ready, i + 1)
                            pe.wait_ge(hs_done, i + 1)
                            for j in range(nb):
                                last = t.transpose(PS[b][:, j * P:(j + 1) * P], SX[:, b, j * P:(j + 1) * P], IDENT[:])
                            last.then_inc(pe_turned, 1)
                            pe.wait_ge(sa_ready, i + 1)
                            pe.wait_ge(msg_done, i + 2)
                            for j in range(nb):
                                blkT = SA[:, b, j * P:(j + 1) * P]
                                o = PS[6 + b][:, j * P:(j + 1) * P]
                                t.matmul(PS[2 + j][:], blkT, WS[:, 0:R * D], start=True, stop=True)
                                t.matmul(o, blkT, WS[:, R * D:(R + 1) * D], start=True, stop=False)
                                last = t.matmul(o, ONE[0:1, :], WB[0:1, R * D:(R + 1) * D], start=False, stop=True)
                            last.then_inc(pe_done, 1)

                @block.scalar
                def _(act):
                    act.sem_inc(hs_done, 2)
                    act.wait_ge(root_in, 1)
                    a.activation(RSTD[:], RSTD[:], ACT.Sqrt, bias=EPS[:]).then_inc(root_out, 1)
                    with act.Fori(0, NODE_TURNS) as turn:
                        for b in range(2):
                            i, nb, blk, col = half(turn, b)
                            act.wait_ge(pe_turned, i + 3)
                            a.copy(SA[:, b, 0:nb * P], PS[b][:, 0:nb * P]).then_inc(sa_ready, 1)
                            act.wait_ge(pe_done, i + 1)
                            a.copy(HS[:, ds(blk, nb), :], rows(PS[6 + b], nb)).then_inc(hs_done, 1)

        def finish():
            got, chain, loop_chain, more = sem("f_got"), sem("f_chain"), sem("f_lchain"), sem("f_more")
            root_in, root_out, stored = sem("f_rin"), sem("f_rout"), sem("f_stored")
            STEPS = 6
            with nc.Block() as block:
                @block.gpsimd
                def _(pool):
                    for blk in range(NB):
                        pool.indirect_dma_start(out=AGG[:, blk, :], out_offset=None, in_=RUNS,
                                                in_offset=bass.IndirectOffsetOnAxis(ap=ENDI[:, blk:blk + 1], axis=0)
                                                ).then_inc(got, 16)

                @block.scalar
                def _(act):
                    act.wait_ge(root_in, 1)
                    a.activation(RSTD[:], RSTD[:], ACT.Sqrt, bias=EPS[:]).then_inc(root_out, 1)

                @block.vector
                def _(dve):
                    dve.wait_ge(got, NB * 16)
                    with dve.Fori(0, NODE_TURNS) as turn:
                        for b in range(2):
                            i, nb, blk, col = half(turn, b)
                            cl = Chain(dve, loop_chain, i * STEPS)
                            Y = rows(YS[:, b], nb)
                            cl.step(v.tensor_tensor(Y, AGG[:, ds(blk, nb), :], per(HAS[:, ds(blk, nb)], D), ALU.mult))
                            cl.step(v.tensor_tensor(Y, Y, HS[:, ds(blk, nb), :], ALU.add))
                            cl.step(v.tensor_tensor(X[:, ds(blk, nb), :], X[:, ds(blk, nb), :], Y, ALU.add))
                            cl.step(moments(cl, b, nb, blk))
                            pass_wait(dve)
                            assert cl.n == STEPS
                    ch = Chain(dve, chain)
                    normalize(dve, ch, root_in, root_out)
                    with dve.Fori(0, NODE_TURNS) as turn:
                        for b in range(2):
                            i, nb, blk, col = half(turn, b)
                            cm = Chain(dve, more, i * 2)
                            cm.step(v.tensor_tensor(X[:, ds(blk, nb), :], X[:, ds(blk, nb), :],
                                                    per(RSTD[:, ds(blk, nb)], D), ALU.mult))
                            cm.step(v.tensor_tensor(X[:, ds(blk, nb), :], X[:, ds(blk, nb), :],
                                                    per(NBIA[:, ds(blk, nb)], D), ALU.add))
                            pass_wait(dve)

                @block.sync
                def _(sp):
                    sp.wait_ge(more, 4 * NODE_TURNS)
                    sp.dma_start(out[0:(NB - 1) * P].rearrange("(b p) f -> p b f", p=P), X[:, 0:NB - 1, :]).then_inc(stored, 16)
                    sp.dma_start(out[(NB - 1) * P:N], X[0:LAST, NB - 1, :]).then_inc(stored, 16)
                    sp.wait_ge(stored, 32)

        for stage in (edge_lists, table0, edges0, close0, open1, edges1, close1, open2, edges2v, table2, edges2,
                      close2, open3, edges3, finish):
            before = nc.snapshot_sems()
            stage()
            nc.clear_and_free_semaphores(nc.allocated_since(before))
            nc.all_engine_barrier()


def kernel(x, src, dst, edge_type_4, L0_gnn_W_proj, L0_gnn_a_src, L0_gnn_a_tgt, L0_gnn_bias, L1_gnn_W_msg,
           L1_gnn_W_self, L1_gnn_b_self, L1_gnn_gamma, L1_gnn_beta, L2_gnn_w_i, L2_gnn_w_j, L3_gnn_weight,
           L3_gnn_bias):
    import concourse.bacc as bacc
    from concourse.bass_utils import run_bass_kernel_spmd

    x = np.asarray(x)
    row = lambda y: np.asarray(y).reshape(1, -1)
    arrays = {
        "x": x, "xT": x.T, "src": src, "dst": dst, "etype": edge_type_4, "w_proj": L0_gnn_W_proj,
        "a_src": row(L0_gnn_a_src), "a_tgt": row(L0_gnn_a_tgt), "bias0": row(L0_gnn_bias),
        "w_msgT": np.asarray(L1_gnn_W_msg).T, "w_selfT": np.asarray(L1_gnn_W_self).T, "b_self": row(L1_gnn_b_self),
        "gamma": row(L1_gnn_gamma), "beta": row(L1_gnn_beta), "w_i": row(L2_gnn_w_i).T, "w_j": row(L2_gnn_w_j).T,
        "w_rel": L3_gnn_weight, "b_rel": L3_gnn_bias,
    }
    arrays = {n: np.ascontiguousarray(y) for n, y in arrays.items()}
    nc = bacc.Bacc("TRN2", target_bir_lowering=False, num_devices=1)
    args = {n: nc.dram_tensor(n, y.shape, mybir.dt.from_np(y.dtype), kind="ExternalInput").ap()
            for n, y in arrays.items()}
    args["out"] = nc.dram_tensor("out", (N, D), FP, kind="ExternalOutput").ap()
    build(nc, **args)
    return run_bass_kernel_spmd(nc, [arrays], core_ids=[0]).results[0]["out"]
```

```python
import numpy as np
from contextlib import ExitStack

import concourse.bass as bass
from concourse import mybir

FP = mybir.dt.float32
BF = mybir.dt.bfloat16
I32 = mybir.dt.int32
ALU = mybir.AluOpType
ACT = mybir.ActivationFunctionType
AXX = mybir.AxisListType.X
RMAX = bass.bass_isa.ReduceOp.max
ds = bass.ds

P = 128
N = 6250
E = 106250
D = 128
H = 4
DH = D // H
R = 4
NB = -(-N // P)
NP = NB * P
LAST = N - (NB - 1) * P
U = 8
RING = 4
K = -(-E // (P * U * RING)) * U * RING
GROUPS = K // U
LAPS = K // (U * RING)
AHEAD = U * RING
TG = -(-K // P)
KP = TG * P
W = 32
WIDE = NP + W
FAR = 32768
BIG = 3.38e38
GONE = -1.0e30
TINY = 1e-37
SPREAD = 60.0
NODE_TURNS = 7
LN_EPS = 1e-5
SLOPE0, SLOPE2 = 0.2, 0.01
HALF = 4 * P


class Chain:

    def __init__(self, eng, sem, start=0):
        self.eng, self.sem, self.start, self.n = eng, sem, start, 0

    def step(self, ins):
        self.n += 1
        ins.then_inc(self.sem, 1)
        self.eng.wait_ge(self.sem, self.start + self.n)


def per(ap, n):
    return ap.unsqueeze(len(ap.shape)).to_broadcast([*ap.shape, n])


def times(ap, n):
    return ap.unsqueeze(1).to_broadcast([ap.shape[0], n, *ap.shape[1:]])


def build(nc, x, xT, src, dst, etype, w_proj, a_src, a_tgt, bias0, w_msgT, w_selfT, b_self,
          gamma, beta, w_i, w_j, w_rel, b_rel, out):
    v, t, a, g = nc.vector, nc.tensor, nc.scalar, nc.gpsimd
    ctx = ExitStack()
    with ctx:
        def sb(name, shape, dt=FP):
            return ctx.enter_context(nc.sbuf_tensor(name, shape, dt))

        def sem(name):
            return nc.alloc_semaphore(name=name)

        def dram(name, shape, dt=FP):
            return nc.dram_tensor(name, shape, dt, kind="Internal").ap()

        DSTP = dram("dst_padded", (KP * P + 1,), I32)
        SRCP = dram("src_padded", (KP * P,), I32)
        TYPP = dram("type_padded", (KP * P,), I32)
        BASED = dram("window_base", (KP,))
        MASKD = dram("run_mask", (KP * P,), BF)
        LOD = dram("source_in_block", (KP * P,), BF)
        CUMD = dram("edges_up_to", (NP,))
        T0 = dram("table0", (NP, D + H))
        T1 = dram("table1", (NP, D))
        V2 = dram("table2v", (NP, 2))
        T2 = dram("table2", (NP, D + 2))
        T3 = dram("table3", (R * NP, D))
        IDX3D = dram("index3", (P, KP), I32)
        RUNS = dram("running_max", ((K + U) * P, D))

        XBUF = sb("XBUF", [P, WIDE])
        X = XBUF[:, 0:NP].rearrange("p (b f) -> p b f", f=D)
        DEN = XBUF[0:1 + H, :]
        ACC = sb("ACC", [P, WIDE])
        BUF = sb("BUF", [P, H * WIDE])
        TB = BUF[:, :].rearrange("p (h n) -> p h n", h=H)
        HS = BUF[:, 0:NP].rearrange("p (b f) -> p b f", f=D)
        UB = BUF[:, WIDE:2 * WIDE]
        AGG = BUF[:, 2 * WIDE:2 * WIDE + NP].rearrange("p (b f) -> p b f", f=D)
        OLO = BUF[:, 3 * WIDE:3 * WIDE + U * P].rearrange("p (u n) -> p u n", u=U)
        IDX3 = BUF[:, 4 * WIDE - KP:4 * WIDE].bitcast(I32)
        LO = BUF[:, 2 * WIDE:2 * WIDE + KP]
        HI = BUF[:, 2 * WIDE + KP:2 * WIDE + 2 * KP]
        REL0 = sb("REL0", [P, KP])
        REL = sb("REL", [P, KP])
        PEN = sb("PEN", [P, KP])
        SRC = sb("SRC", [P, KP], I32)
        BASE0 = sb("BASE0", [1, KP])
        BASE = sb("BASE", [1, KP], I32)
        SHIFT = sb("SHIFT", [P, 1])
        FLAG = sb("FLAG", [P, 4], I32)
        IOTA = sb("IOTA", [P, P])
        IDENT = sb("IDENT", [P, P])
        DEG = sb("DEG", [P, NB])
        MV = sb("MV", [P, NB, 2])
        RSTD = sb("RSTD", [P, NB])
        NBIA = sb("NBIA", [P, NB])
        EPS = sb("EPS", [P, 1])
        SC = sb("SC", [P, 16])
        SHIFT0 = sb("SHIFT0", [P, 1])
        NSHIFT0 = sb("NSHIFT0", [P, 1])
        GUARD0 = sb("GUARD0", [P, 1])
        RDEG = sb("RDEG", [P, NB])
        HAS = sb("HAS", [P, NB])
        ENDF = sb("ENDF", [P, NB])
        ENDI = sb("ENDI", [P, NB], I32)
        RDEN = sb("RDEN", [P, NB])
        VC = sb("VC", [P, NB, 2])
        ONE = sb("ONE", [P, P])
        ZERO = sb("ZERO", [P, U * W])
        G = sb("G", [P, RING, U, D + H])
        IC = sb("IC", [P, RING * U], I32)
        SEL = sb("SEL", [P, 2, U, W])
        PROD = sb("PROD", [P, U * H, W])
        Z = sb("Z", [P, U, H])
        ZL = sb("ZL", [P, 2, U, H])
        ZMAX = sb("ZMAX", [P, U, H])
        WE = sb("WE", [P, 2, U, 1 + H])
        GW = sb("GW", [P, 2, U, D])
        GF = G[:].rearrange("p r u f -> p (r u f)")
        SA, SX, YS, SD = (GF[:, i * 2 * HALF:(i + 1) * 2 * HALF].rearrange("p (q n) -> p q n", q=2) for i in range(4))
        SD = SD[0:1 + H]
        GWF = GW[:].rearrange("p q u f -> p (q u f)")
        YW = GWF[:, 0:8 * (D + H)].rearrange("p (u f) -> p u f", f=D + H)
        WS = GWF[:, 8 * (D + H):8 * (D + H) + 5 * D]
        WB = PROD[:].rearrange("p u n -> p (u n)")
        ST = sb("ST", [P, NB, 2 * H])
        BN6 = sb("BN6", [P, 2, 4, 6])
        SM = sb("SM", [P, 2, 4, 8])
        PS = [ctx.enter_context(nc.psum_tensor(f"PS{i}", [P, 512], FP)) for i in range(8)]

        def is_wide(ch, spread, flag):
            ch.step(v.tensor_scalar(spread, spread, SPREAD, None, ALU.is_le))
            ch.step(v.tensor_scalar(flag, spread, -1.0, 1.0, ALU.mult, ALU.add))

        passed = sem("passed")

        def pass_wait(eng):
            eng.sem_inc(passed, 1)

        def half(turn, b):
            return turn * 2 + b, 4 - b, turn * 7 + 4 * b, turn * 7 * P + HALF * b

        def passes(eng):
            return eng.value_load(FLAG[0:1, 0:1], min_val=1, max_val=NP // W + 1)

        def tiles_of(eng, turn, b):
            return eng.snap(turn * (U * RING) + b * U, min_val=0, max_val=K - U)

        def edge_lists():
            tiles = lambda i: BUF[:, i * KP:(i + 1) * KP].rearrange("p (g e) -> p g e", e=P)
            Fd, Fp, Fs, Ft, F1 = (tiles(i) for i in range(5))
            Rd, Rp, Rs, Rt = (BUF[:, i * KP:(i + 1) * KP].bitcast(I32).rearrange("p (g e) -> p g e", e=P)
                              for i in range(5, 9))
            flat = lambda y: y.rearrange("p g e -> p (g e)")
            MK = BUF[:, 9 * KP:9 * KP + KP // 2].bitcast(BF).rearrange("p (g e) -> p g e", e=P)
            LB = BUF[:, 9 * KP + KP // 2:10 * KP].bitcast(BF).rearrange("p (g e) -> p g e", e=P)
            idx3 = BUF[:, 10 * KP:11 * KP].bitcast(I32)
            bmin = sb("bmin", [P, TG])
            NPAD = KP * P - E
            far, zero = (BUF[0:1, 11 * KP + i * NPAD:11 * KP + i * NPAD + NPAD // 2].bitcast(I32) for i in range(2))
            neg = sb("neg", [1, 1], I32)
            pads, padded, rows_in = sem("pads"), sem("padded"), sem("rows_in")
            iotas, red_in, red_out = sem("iotas"), sem("red_in"), sem("red_out")
            ident_ready, rows_ready, turned = sem("ident_ready"), sem("rows_ready"), sem("turned")
            base_ready, mask_ready, stored = sem("base_ready"), sem("mask_ready"), sem("stored")
            base_in, chain, idx3_ready = sem("base_in"), sem("list_chain"), sem("idx3_ready")
            lo_ready = sem("lo_ready")
            ipart = SC[:, 0:1]

            with nc.Block() as block:
                @block.sync
                def _(sp):
                    for to, of in ((DSTP[1:1 + E], dst), (SRCP[0:E], src), (TYPP[0:E], etype)):
                        sp.dma_start(to.rearrange("(a b) -> a b", b=850),
                                     of.rearrange("(a b) -> a b", b=850)).then_inc(padded, 16)
                    sp.wait_ge(pads, 1)
                    sp.dma_start(DSTP[0:1].unsqueeze(0), neg[:]).then_inc(padded, 16)
                    for h in range(2):
                        for to, of in ((DSTP[1 + E:], far), (SRCP[E:], zero), (TYPP[E:], zero)):
                            sp.dma_start(to[h * (NPAD // 2):(h + 1) * (NPAD // 2)].unsqueeze(0), of).then_inc(padded, 16)
                    sp.wait_ge(padded, 10 * 16)
                    lay = lambda y: y.rearrange("(g p e) -> p g e", p=P, e=P)
                    for to, of in ((Rd, DSTP[1:]), (Rp, DSTP[0:KP * P]), (Rs, SRCP), (Rt, TYPP)):
                        sp.dma_start(to, lay(of)).then_inc(rows_in, 16)
                    sp.wait_ge(base_ready, 1)
                    sp.dma_start(BASED.rearrange("(g p) -> p g", p=P), bmin[:], allow_slow_non_contiguous=True).then_inc(stored, 16)
                    sp.wait_ge(stored, 16)
                    sp.dma_start(BASE0[:], BASED.unsqueeze(0)).then_inc(base_in, 16)
                    sp.wait_ge(lo_ready, 1)
                    sp.dma_start(LOD.rearrange("(g p e) -> p g e", p=P, e=P), LB[:]).then_inc(stored, 16)
                    sp.wait_ge(mask_ready, 1)
                    sp.dma_start(MASKD.rearrange("(g p e) -> p g e", p=P, e=P), MK[:]).then_inc(stored, 16)
                    sp.wait_ge(idx3_ready, 1)
                    sp.dma_start(IDX3D, idx3).then_inc(stored, 16)
                    sp.wait_ge(base_in, 16)
                    sp.wait_ge(stored, 64)

                @block.gpsimd
                def _(pool):
                    g.memset(far, FAR)
                    g.memset(neg[:], -1)
                    g.memset(zero, 0)
                    g.drain().then_inc(pads, 1)
                    g.iota(IOTA[:], [[1, P]], base=0, channel_multiplier=0,
                           allow_small_or_imprecise_dtypes=True)
                    g.iota(ipart, [[1, 1]], base=0, channel_multiplier=1,
                           allow_small_or_imprecise_dtypes=True)
                    g.drain().then_inc(iotas, 1)
                    pool.wait_ge(red_in, 1)
                    g.partition_all_reduce(SC[:, 4:6], SC[:, 2:4], P, RMAX).then_inc(red_out, 1)

                @block.vector
                def _(dve):
                    ch = Chain(dve, chain)
                    v.memset(EPS[:], LN_EPS)
                    v.memset(ONE[:], 1.0)
                    v.memset(BASE[:], 0)
                    dve.wait_ge(iotas, 1)
                    v.tensor_scalar(IDENT[:], IOTA[:], ipart, None, ALU.is_equal).then_inc(ident_ready, 1)
                    dve.wait_ge(rows_in, 64)
                    v.tensor_copy(Fd, Rd)
                    v.tensor_copy(Fp, Rp)
                    v.tensor_copy(Fs, Rs)
                    ch.step(v.tensor_copy(Ft, Rt))
                    ch.step(v.tensor_scalar(Rs, Rs, P - 1, None, ALU.bitwise_and))
                    v.tensor_copy(LB, Rs).then_inc(lo_ready, 1)
                    ch.step(v.tensor_reduce(bmin[:], Fd, AXX, ALU.min))
                    ch.step(v.tensor_scalar(bmin[:], bmin[:], float(NP - W), None, ALU.min))
                    dve.sem_inc(base_ready, 1)
                    ch.step(v.scalar_tensor_tensor(F1, Fd, float(N), Fd, ALU.is_lt, ALU.mult))
                    ch.step(v.tensor_tensor(F1, F1, per(bmin[:], P), ALU.subtract))
                    ch.step(v.tensor_reduce(SC[:, 2:3], flat(F1), AXX, ALU.max))
                    ch.step(v.tensor_tensor(F1, Fp, Fd, ALU.subtract))
                    ch.step(v.tensor_reduce(SC[:, 3:4], flat(F1), AXX, ALU.max))
                    dve.sem_inc(red_in, 1)
                    ch.step(v.tensor_tensor(F1, Fp, Fd, ALU.not_equal))
                    v.tensor_tensor(Fd, Fd, per(bmin[:], P), ALU.subtract)
                    ch.step(v.scalar_tensor_tensor(Ft, Ft, float(NP), Fs, ALU.mult, ALU.add))
                    dve.sem_inc(rows_ready, 1)
                    ch.step(v.tensor_scalar(F1, F1, -2.0, 1.0, ALU.mult, ALU.add))
                    ch.step(v.tensor_scalar(MK[:], F1, BIG, None, ALU.mult))
                    dve.sem_inc(mask_ready, 1)
                    for n, to in enumerate((REL0, SRC, idx3)):
                        for h, (g0, g1) in enumerate(((0, 4), (4, TG))):
                            dve.wait_ge(turned, 2 * n + h + 1)
                            ins = v.tensor_copy(to[:, g0 * P:g1 * P], PS[2 * n + h][:, 0:(g1 - g0) * P])
                    ch.step(ins)
                    v.tensor_copy(SRC[:, K:K + AHEAD], SRC[:, 0:AHEAD])
                    ch.step(v.tensor_copy(idx3[:, K:K + AHEAD], idx3[:, 0:AHEAD]))
                    dve.sem_inc(idx3_ready, 1)
                    dve.wait_ge(red_out, 1)
                    ch.step(v.tensor_scalar(SC[:, 5:6], SC[:, 5:6], 0.0, None, ALU.is_gt))
                    ch.step(v.tensor_copy(FLAG[:, 0:2], SC[:, 4:6]))
                    ch.step(v.tensor_scalar(FLAG[:, 0:1], FLAG[:, 0:1], 5, None, ALU.logical_shift_right))
                    ch.step(v.tensor_scalar(FLAG[:, 0:1], FLAG[:, 0:1], 1, None, ALU.add))

                @block.tensor
                def _(pe):
                    pe.wait_ge(ident_ready, 1)
                    pe.wait_ge(rows_ready, 1)
                    for n, lst in enumerate((Fd, Fs, Ft)):
                        for h, (g0, g1) in enumerate(((0, 4), (4, TG))):
                            for i in range(g0, g1):
                                last = t.transpose(PS[2 * n + h][:, (i - g0) * P:(i - g0 + 1) * P],
                                                   lst[:, i, :], IDENT[:])
                            last.then_inc(turned, 1)

        def table0():
            x_in, w_in, zeroed, w_ready = sem("t0_x_in"), sem("t0_w_in"), sem("t0_zeroed"), sem("t0_w_ready")
            xT_ready, pe_done, rows_done, tb_done = sem("t0_xT"), sem("t0_pe"), sem("t0_rows"), sem("t0_tb")
            stored = [sem("t0_stored0"), sem("t0_stored1")]
            red_in, red_out, chain = sem("t0_red_in"), sem("t0_red_out"), sem("t0_chain")
            WTB = WB[:, 0:H * D].rearrange("p (h m) -> p h m", h=H)
            rows = T0.rearrange("(b p) f -> p b f", p=P)
            with nc.Block() as block:
                @block.sync
                def _(sp):
                    sp.dma_start(WS[:, 0:D], w_proj).then_inc(w_in, 16)
                    sp.dma_start(SX[:, 0, 0:D], a_src.to_broadcast([P, D])).then_inc(w_in, 16)
                    sp.dma_start(SX[:, 0, D:2 * D], a_tgt.to_broadcast([P, D])).then_inc(w_in, 16)
                    sp.wait_ge(zeroed, 1)
                    sp.dma_start(ACC[:, 0:N], xT).then_inc(x_in, 16)
                    sp.sem_inc(stored[0], 16)
                    sp.sem_inc(stored[1], 16)
                    with sp.Fori(0, NODE_TURNS) as turn:
                        for b in range(2):
                            i, nb, blk, col = half(turn, b)
                            sp.wait_ge(rows_done, i + 3)
                            sp.dma_start(rows[:, ds(blk, nb), :], YW[:, 4 * b:4 * b + nb, :]).then_inc(stored[b], 16)
                    sp.wait_ge(stored[0], 16 * NODE_TURNS + 16)
                    sp.wait_ge(stored[1], 16 * NODE_TURNS + 16)

                @block.scalar
                def _(act):
                    act.sem_inc(tb_done, 1)
                    act.wait_ge(x_in, 16)
                    with act.Fori(0, NODE_TURNS) as turn:
                        for b in range(2):
                            i, nb, blk, col = half(turn, b)
                            act.wait_ge(pe_done, i + 1)
                            a.copy(SA[:, b, 0:nb * P], ACC[:, ds(col, nb * P)]).then_inc(xT_ready, 1)
                            act.wait_ge(pe_done, i + 3)
                            for h in range(H):
                                ins = a.copy(TB[:, h, ds(col, nb * P)], PS[4 + h][:, 0:nb * P])
                            ins.then_inc(tb_done, 1)

                @block.tensor
                def _(pe):
                    pe.sem_inc(pe_done, 2)
                    pe.wait_ge(w_ready, 1)
                    with pe.Fori(0, NODE_TURNS) as turn:
                        for b in range(2):
                            i, nb, blk, col = half(turn, b)
                            pe.wait_ge(xT_ready, i + 1)
                            pe.wait_ge(rows_done, i + 1)
                            pe.wait_ge(tb_done, i + 1)
                            for j in range(nb):
                                blkT = SA[:, b, j * P:(j + 1) * P]
                                t.matmul(PS[b][:, j * P:(j + 1) * P], blkT, WS[:, 0:D], start=True, stop=True)
                                t.matmul(PS[2 + b][:, j * 8:(j + 1) * 8], blkT, WS[:, D:D + 8],
                                         start=True, stop=True)
                            for h in range(H):
                                last = t.matmul(PS[4 + h][:, 0:nb * P], WTB[:, h, :], SA[:, b, 0:nb * P],
                                                start=True, stop=True)
                            last.then_inc(pe_done, 1)

                @block.gpsimd
                def _(pool):
                    pool.wait_ge(red_in, 1)
                    g.partition_all_reduce(SC[:, 8:12], SC[:, 0:4], P, RMAX).then_inc(red_out, 1)

                @block.vector
                def _(dve):
                    ch = Chain(dve, chain)
                    dve.sem_inc(rows_done, 2)
                    v.memset(ZERO[:], 0.0)
                    v.memset(TB[:, :, NP:WIDE], 0.0)
                    ch.step(v.memset(ACC[:, N:WIDE], 0.0))
                    dve.sem_inc(zeroed, 1)
                    dve.wait_ge(w_in, 48)
                    v.tensor_tensor(YS[:, 0, 0:D], WS[:, 0:D], SX[:, 0, 0:D], ALU.mult)
                    ch.step(v.tensor_tensor(YS[:, 0, D:2 * D], WS[:, 0:D], SX[:, 0, D:2 * D], ALU.mult))
                    ch.step(v.tensor_reduce(WS[:, D:D + 8],
                                            YS[:, 0, 0:2 * D].rearrange("p (h d) -> p h d", d=DH), AXX, ALU.add))
                    ch.step(v.tensor_copy(WTB, per(WS[:, D + H:D + 8], D)))
                    dve.sem_inc(w_ready, 1)
                    with dve.Fori(0, NODE_TURNS) as turn:
                        for b in range(2):
                            i, nb, blk, col = half(turn, b)
                            proj = PS[b][:, 0:nb * P].rearrange("p (b f) -> p b f", f=D)
                            scores = PS[2 + b][:, 0:nb * 8].rearrange("p (b f) -> p b f", f=8)
                            dve.wait_ge(pe_done, i + 3)
                            dve.wait_ge(stored[b], 16 * turn + 16)
                            v.tensor_copy(YW[:, 4 * b:4 * b + nb, 0:D], proj)
                            v.tensor_copy(YW[:, 4 * b:4 * b + nb, D:D + H], scores[:, :, 0:H])
                            v.tensor_copy(ST[:, ds(blk, nb), :], scores).then_inc(rows_done, 1)
                    dve.wait_ge(rows_done, 2 * NODE_TURNS + 2)
                    XY = mybir.AxisListType.XY
                    v.tensor_reduce(SC[:, 12:13], ST[:, :, 0:H], XY, ALU.max)
                    v.tensor_reduce(SC[:, 13:14], ST[:, :, H:8], XY, ALU.max)
                    v.tensor_reduce(SC[:, 14:15], ST[:, :, 0:H], XY, ALU.min)
                    ch.step(v.tensor_reduce(SC[:, 15:16], ST[:, :, H:8], XY, ALU.min))
                    v.tensor_copy(SC[:, 0:2], SC[:, 12:14])
                    ch.step(v.tensor_scalar(SC[:, 2:4], SC[:, 14:16], -1.0, None, ALU.mult))
                    dve.sem_inc(red_in, 1)
                    dve.wait_ge(red_out, 1)
                    ch.step(v.tensor_tensor(SC[:, 0:1], SC[:, 8:9], SC[:, 9:10], ALU.add))
                    ch.step(v.tensor_tensor(SC[:, 1:2], SC[:, 10:11], SC[:, 11:12], ALU.add))
                    ch.step(v.tensor_tensor(SC[:, 1:2], SC[:, 1:2], SC[:, 0:1], ALU.add))
                    is_wide(ch, SC[:, 1:2], FLAG[:, 2:3])
                    ch.step(v.scalar_tensor_tensor(SHIFT0[:], SC[:, 0:1], SLOPE0, SC[:, 0:1], ALU.mult, ALU.max))
                    ch.step(v.tensor_scalar(NSHIFT0[:], SHIFT0[:], -1.0, None, ALU.mult))

        def number(pss, turn, b):
            return (pss * LAPS + turn) * RING + b

        def first_indices(rows, ready):
            a.copy(IC[:], rows[:, 0:AHEAD]).then_inc(ready, RING)

        def next_indices(act, rows, pss, turn, b, rows_used, ready):
            k = act.snap(turn * AHEAD + (b * U + AHEAD), min_val=AHEAD, max_val=K + AHEAD - U)
            act.wait_ge(rows_used, number(pss, turn, b) + 1)
            a.copy(IC[:, b * U:(b + 1) * U], rows[:, ds(k, U)]).then_inc(ready, 1)

        def gather_group(pool, table, width, b, gathered):
            for u in range(U):
                pool.indirect_dma_start(
                    out=G[:, b, u, 0:width], out_offset=None, in_=table,
                    in_offset=bass.IndirectOffsetOnAxis(
                        ap=IC[:, b * U + u:b * U + u + 1], axis=0)).then_inc(gathered[b], 16)

        def gather_rows(pool, table, width, indices_ready, opened, gathered, used, ahead):
            with pool.Fori(0, passes(pool)) as pss:
                pool.sem_inc(opened, 1)
                with pool.Fori(0, LAPS) as turn:
                    for b in range(RING):
                        pool.wait_ge(indices_ready, number(pss, turn, b) + 1)
                        pass_wait(pool)
                        gather_group(pool, table, width, b, gathered)
                pool.wait_ge(used, pss * GROUPS + (GROUPS + ahead))
                pass_wait(pool)
                pool.inc_swdge_sem(gathered, [16 * U * LAPS] * RING, mode="sub")

        def place_windows(ch):
            v.tensor_scalar(BASE[:], BASE0[:], SHIFT[0:1, 0:1], float(NP), ALU.add, ALU.min)
            ch.step(v.tensor_scalar(REL[:], REL0[:], SHIFT[:, 0:1], None, ALU.subtract))
            v.tensor_scalar(PEN[:], REL[:], 0.0, GONE, ALU.is_lt, ALU.mult)
            ch.step(v.tensor_scalar(PROD[:].rearrange("p u n -> p (u n)")[:, 0:KP], REL[:], float(W), GONE, ALU.is_ge, ALU.mult))
            v.tensor_scalar(SHIFT[:], SHIFT[:], float(W), None, ALU.add)
            ch.step(v.tensor_tensor(PEN[:], PEN[:], PROD[:].rearrange("p u n -> p (u n)")[:, 0:KP], ALU.add))
            pass_wait(ch.eng)

        def select(b, k):
            return v.tensor_tensor(SEL[:, b % 2], times(IOTA[:, 0:W], U), per(REL[:, ds(k, U)], W), ALU.is_equal)

        def add_sums(dve, regs, before, parity, sum_chain, den_chain=None):
            for u in range(U):
                w = dve.snap(regs[u], min_val=0, max_val=NP)
                dve.wait_ge(sum_chain, before + (u + 1))
                v.tensor_tensor(ACC[:, ds(w, W)], ACC[:, ds(w, W)], PS[parity][:, u * W:(u + 1) * W],
                                ALU.add).then_inc(sum_chain, 1)
                if den_chain is not None:
                    dve.wait_ge(den_chain, before + (u + 1))
                    v.tensor_tensor(DEN[:, ds(w, W)], DEN[:, ds(w, W)],
                                    PS[2 + parity][0:1 + H, u * W:(u + 1) * W], ALU.add).then_inc(den_chain, 1)
            dve.wait_ge(sum_chain, before + (U + 1))
            if den_chain is not None:
                dve.wait_ge(den_chain, before + (U + 1))

        def edges0():
            ic_ready, opened, sel_ready, pe_done = sem("e0_ic"), sem("e0_opened"), sem("e0_sel"), sem("e0_pe")
            rows_used, z_ready, w_ready, added = sem("e0_used"), sem("e0_z"), sem("e0_w"), sem("e0_added")
            acc_chain, den_chain, chain = sem("e0_acc"), sem("e0_den"), sem("e0_chain")
            pass_chain, zeroed = sem("e0_pass"), sem("e0_zeroed")
            red_in, red_out, guard_in, guard_out = sem("e0_red_in"), sem("e0_red_out"), sem("e0_gin"), sem("e0_gout")
            gathered = [sem(f"e0_gathered{b}") for b in range(RING)]
            cum_ready, cum_out = sem("e0_cum"), sem("e0_cumout")
            CUM = BUF[0:1, 3 * WIDE:3 * WIDE + NP]
            STEPS = 6
            with nc.Block() as block:
                @block.sync
                def _(sp):
                    sp.wait_ge(cum_ready, 1)
                    sp.dma_start(CUMD.unsqueeze(0), CUM).then_inc(cum_out, 16)
                    sp.wait_ge(cum_out, 16)

                @block.scalar
                def _(act):
                    first_indices(SRC, ic_ready)
                    with act.Fori(0, passes(act)) as pss:
                        with act.Fori(0, LAPS) as turn:
                            for b in range(RING):
                                act.wait_ge(z_ready, number(pss, turn, b) + 1)
                                a.activation(WE[:, b % 2, :, 1:1 + H], ZL[:, b % 2], ACT.Exp,
                                             bias=NSHIFT0[:]).then_inc(w_ready, 1)
                                next_indices(act, SRC, pss, turn, b, rows_used, ic_ready)
                    act.wait_ge(guard_in, 1)
                    a.activation(SC[:, 3:4], SC[:, 2:3], ACT.Exp, bias=NSHIFT0[:]).then_inc(guard_out, 1)

                @block.gpsimd
                def _(pool):
                    gather_rows(pool, T0, D + H, ic_ready, opened, gathered, rows_used, 0)
                    pool.wait_ge(red_in, 1)
                    g.partition_all_reduce(SC[:, 1:2], SC[:, 0:1], P, RMAX).then_inc(red_out, 1)

                @block.tensor
                def _(pe):
                    t.matmul(PS[1][:, 0:U * W], ZERO[:, 0:P], ZERO[:], start=True, stop=True)
                    t.matmul(PS[3][0:1 + H, 0:U * W], ZERO[:, 0:1 + H], ZERO[:], start=True,
                             stop=True).then_inc(pe_done, 2)
                    with pe.Fori(0, passes(pe)) as pss:
                        with pe.Fori(0, LAPS) as turn:
                            for b in range(RING):
                                i = number(pss, turn, b)
                                pe.wait_ge(sel_ready, i + 1)
                                pe.wait_ge(added, i + 1)
                                for u in range(U):
                                    s = SEL[:, b % 2, u, :]
                                    t.matmul(PS[b % 2][:, u * W:(u + 1) * W], GW[:, b % 2, u, :], s,
                                             start=True, stop=True)
                                    last = t.matmul(PS[2 + b % 2][0:1 + H, u * W:(u + 1) * W],
                                                    WE[:, b % 2, u, :], s, start=True, stop=True)
                                last.then_inc(pe_done, 1)

                @block.vector
                def _(dve):
                    regs = [[dve.alloc_register(f"e0_base{q}_{u}") for u in range(U)] for q in range(2)]
                    v.memset(ACC[:], 0.0).then_inc(acc_chain, 1)
                    v.memset(DEN[:], 0.0).then_inc(den_chain, 1)
                    v.memset(SHIFT[:], 0.0)
                    v.memset(WE[:], 1.0)
                    v.memset(ZMAX[:], GONE).then_inc(zeroed, 1)
                    dve.wait_ge(zeroed, 1)
                    dve.sem_inc(added, 1)
                    dve.reg_load(regs[1], BASE[0:1, 0:U])
                    np_ = passes(dve)
                    with dve.Fori(0, np_) as pss:
                        place_windows(Chain(dve, pass_chain, pss * 3))
                        dve.wait_ge(opened, pss + 1)
                        pass_wait(dve)
                        with dve.Fori(0, LAPS) as turn:
                            for b in range(RING):
                                i = number(pss, turn, b)
                                k = tiles_of(dve, turn, b)
                                cg = Chain(dve, chain, i * STEPS)
                                dve.reg_load(regs[b % 2], BASE[0:1, ds(k, U)])
                                dve.wait_ge(pe_done, i + 1)
                                cg.step(select(b, k))
                                for u in range(U):
                                    w = dve.snap(regs[b % 2][u], min_val=0, max_val=NP)
                                    ins = v.tensor_tensor(PROD[:, u * H:(u + 1) * H, :],
                                                          times(SEL[:, b % 2, u, :], H), TB[:, :, ds(w, W)], ALU.mult)
                                cg.step(ins)
                                cg.step(v.tensor_reduce(Z[:], PROD[:].rearrange("p (u h) n -> p u h n", h=H),
                                                        AXX, ALU.add))
                                dve.wait_ge(gathered[b], turn * (16 * U) + 16 * U)
                                cg.step(v.tensor_tensor(Z[:], Z[:], G[:, b, :, D:D + H], ALU.add))
                                cg.step(v.tensor_tensor(Z[:], Z[:], per(PEN[:, ds(k, U)], H), ALU.add))
                                v.tensor_tensor(ZMAX[:], ZMAX[:], Z[:], ALU.max)
                                v.scalar_tensor_tensor(ZL[:, b % 2], Z[:], SLOPE0, Z[:], ALU.mult,
                                                       ALU.max).then_inc(z_ready, 1)
                                dve.wait_ge(pe_done, i + 2)
                                add_sums(dve, regs[1 - b % 2], i * U, 1 - b % 2, acc_chain, den_chain)
                                dve.sem_inc(added, 1)
                                dve.wait_ge(w_ready, i + 1)
                                cg.step(v.tensor_tensor(
                                    GW[:, b % 2].rearrange("p u (h f) -> p u h f", h=H),
                                    G[:, b, :, 0:D].rearrange("p u (h f) -> p u h f", h=H),
                                    per(WE[:, b % 2, :, 1:1 + H], DH), ALU.mult))
                                dve.sem_inc(rows_used, 1)
                                dve.sem_inc(sel_ready, 1)
                                assert cg.n == STEPS
                    dve.wait_ge(pe_done, np_ * GROUPS + 2)
                    add_sums(dve, regs[1], np_ * (GROUPS * U), 1, acc_chain, den_chain)
                    ce = Chain(dve, zeroed, 1)
                    ce.step(v.tensor_tensor_scan(CUM, ONE[0:1, 0:1].to_broadcast([1, NP]), DEN[0:1, 0:NP], 0.0,
                                                 ALU.mult, ALU.add))
                    dve.sem_inc(cum_ready, 1)
                    ce.step(v.tensor_reduce(SC[:, 0:1], ZMAX[:].rearrange("p u h -> p (u h)"), AXX, ALU.max))
                    dve.sem_inc(red_in, 1)
                    dve.wait_ge(red_out, 1)
                    ce.step(v.scalar_tensor_tensor(SC[:, 2:3], SC[:, 1:2], SLOPE0, SC[:, 1:2], ALU.mult, ALU.max))
                    dve.sem_inc(guard_in, 1)
                    dve.wait_ge(guard_out, 1)
                    ce.step(v.tensor_scalar(GUARD0[:], SC[:, 3:4], 1e-16, None, ALU.mult))

        def edges1():
            ic_ready, opened, sel_ready, pe_done = sem("e1_ic"), sem("e1_opened"), sem("e1_sel"), sem("e1_pe")
            added, acc_chain, pass_chain, zeroed = sem("e1_added"), sem("e1_acc"), sem("e1_pass"), sem("e1_zeroed")
            rows_used = sem("e1_used")
            gathered = [sem(f"e1_gathered{b}") for b in range(RING)]
            with nc.Block() as block:
                @block.scalar
                def _(act):
                    first_indices(SRC, ic_ready)
                    with act.Fori(0, passes(act)) as pss:
                        with act.Fori(0, LAPS) as turn:
                            for b in range(RING):
                                k = act.snap(turn * AHEAD + (b * U + AHEAD), min_val=AHEAD, max_val=K + AHEAD - U)
                                act.wait_ge(pe_done, number(pss, turn, b) + 3)
                                a.copy(IC[:, b * U:(b + 1) * U], SRC[:, ds(k, U)]).then_inc(ic_ready, 1)

                @block.gpsimd
                def _(pool):
                    gather_rows(pool, T1, D, ic_ready, opened, gathered, pe_done, 2)

                @block.tensor
                def _(pe):
                    t.matmul(PS[1][:, 0:U * W], ZERO[:, 0:P], ZERO[:], start=True, stop=True).then_inc(pe_done, 2)
                    with pe.Fori(0, passes(pe)) as pss:
                        pe.wait_ge(opened, pss + 1)
                        pe.sem_inc(passed, 1)
                        with pe.Fori(0, LAPS) as turn:
                            for b in range(RING):
                                i = number(pss, turn, b)
                                pe.wait_ge(gathered[b], turn * (16 * U) + 16 * U)
                                pe.wait_ge(sel_ready, i + 1)
                                pe.wait_ge(added, i + 1)
                                for u in range(U):
                                    last = t.matmul(PS[b % 2][:, u * W:(u + 1) * W], G[:, b, u, 0:D],
                                                    SEL[:, b % 2, u, :], start=True, stop=True)
                                last.then_inc(pe_done, 1)

                @block.vector
                def _(dve):
                    regs = [[dve.alloc_register(f"e1_base{q}_{u}") for u in range(U)] for q in range(2)]
                    v.memset(ACC[:], 0.0).then_inc(acc_chain, 1)
                    v.memset(SHIFT[:], 0.0).then_inc(zeroed, 1)
                    dve.wait_ge(zeroed, 1)
                    dve.sem_inc(added, 1)
                    dve.reg_load(regs[1], BASE[0:1, 0:U])
                    np_ = passes(dve)
                    with dve.Fori(0, np_) as pss:
                        place_windows(Chain(dve, pass_chain, pss * 3))
                        with dve.Fori(0, LAPS) as turn:
                            for b in range(RING):
                                i = number(pss, turn, b)
                                k = tiles_of(dve, turn, b)
                                dve.reg_load(regs[b % 2], BASE[0:1, ds(k, U)])
                                dve.wait_ge(pe_done, i + 1)
                                select(b, k).then_inc(sel_ready, 1)
                                dve.wait_ge(pe_done, i + 2)
                                add_sums(dve, regs[1 - b % 2], i * U, 1 - b % 2, acc_chain)
                                dve.sem_inc(added, 1)
                    dve.wait_ge(pe_done, np_ * GROUPS + 2)
                    add_sums(dve, regs[1], np_ * (GROUPS * U), 1, acc_chain)
                    pass_wait(dve)

        def edge_nodes(sp, tile, nodes, read, arrived):
            sp.wait_ge(read, tile + 1)
            sp.dma_start(nodes[0:1, 0:P], SRCP[ds(tile * P, P)].unsqueeze(0)).then_inc(arrived, 16)
            sp.dma_start(nodes[0:1, P:2 * P], DSTP[ds(tile * P + 1, P)].unsqueeze(0)).then_inc(arrived, 16)

        def exact0():
            arrived, read, chain, run_chain = sem("x0_arrived"), sem("x0_read"), sem("x0_chain"), sem("x0_run")
            ic_ready, gathered, turned, done = sem("x0_ic"), sem("x0_gathered"), sem("x0_turned"), sem("x0_done")
            go, spread, started = sem("x0_go"), sem("x0_spread"), sem("x0_started")
            nodes = SEL[:].rearrange("p q u n -> p (q u n)").bitcast(I32)
            near = PROD[:].rearrange("p u n -> p (u n)").bitcast(I32)
            run, z = SC[0:1, 0:H], SC[0:1, H:2 * H]
            with nc.Block() as block:
                @block.sync
                def _(sp):
                    with sp.If(sp.value_load(FLAG[0:1, 2:3], min_val=0, max_val=1) > 0):
                        with sp.Fori(0, K) as tile:
                            edge_nodes(sp, tile, nodes, read, arrived)
                        sp.wait_ge(arrived, 32 * K)
                    sp.nop()

                @block.scalar
                def _(act):
                    with act.If(act.value_load(FLAG[0:1, 2:3], min_val=0, max_val=1) > 0):
                        with act.Fori(0, K) as tile:
                            act.wait_ge(read, tile + 1)
                            a.copy(IC[:, 0:1], SRC[:, ds(tile, 1)]).then_inc(ic_ready, 1)
                    act.nop()

                @block.gpsimd
                def _(pool):
                    with pool.If(pool.value_load(FLAG[0:1, 2:3], min_val=0, max_val=1) > 0):
                        with pool.Fori(0, K) as tile:
                            pool.wait_ge(ic_ready, tile + 1)
                            pool.sem_inc(started, 1)
                            pool.indirect_dma_start(
                                out=G[:, 0, 0, :], out_offset=None, in_=T0,
                                in_offset=bass.IndirectOffsetOnAxis(ap=IC[:, 0:1], axis=0)).then_inc(gathered, 16)
                    pool.nop()

                @block.tensor
                def _(pe):
                    with pe.If(pe.value_load(FLAG[0:1, 2:3], min_val=0, max_val=1) > 0):
                        with pe.Fori(0, K) as tile:
                            pe.wait_ge(gathered, tile * 16 + 16)
                            for h in range(H):
                                last = t.matmul(PS[0][0:1, h * P:(h + 1) * P], G[:, 0, 0, D + h:D + h + 1], IDENT[:],
                                                start=True, stop=True)
                            last.then_inc(turned, 1)
                        pe.wait_ge(done, 1)
                        t.matmul(PS[1][:, 0:1], ONE[0:1, :], SHIFT0[0:1, 0:1], start=True, stop=True).then_inc(spread, 1)
                    pe.nop()

                @block.vector
                def _(dve):
                    with dve.If(dve.value_load(FLAG[0:1, 2:3], min_val=0, max_val=1) > 0):
                        v.memset(SC[0:1, 0:2 * H], -BIG).then_inc(go, 1)
                        dve.wait_ge(go, 1)
                        dve.sem_inc(read, 1)
                        with dve.Fori(0, K) as tile:
                            dve.wait_ge(arrived, tile * 32 + 32)
                            v.tensor_scalar(near[0:1, 0:P], nodes[0:1, P:2 * P], NP, None, ALU.min).then_inc(go, 1)
                            dve.wait_ge(go, tile + 2)
                            dve.wait_ge(turned, tile + 1)
                            scores = PS[0][0:1, :].rearrange("p (h e) -> p h e", h=H)
                            pass_wait(dve)
                            with dve.Fori(0, P) as e:
                                to = dve.value_load(near[0:1, ds(e, 1)], min_val=0, max_val=NP)
                                v.tensor_tensor(z, scores[:, :, ds(e, 1)].rearrange("p h o -> p (h o)"),
                                                TB[0:1, :, ds(to, 1)].rearrange("p h o -> p (h o)"),
                                                ALU.add).then_inc(chain, 1)
                                dve.wait_ge(chain, (tile * P + e) * 2 + 1)
                                v.tensor_tensor(run, run, z, ALU.max).then_inc(chain, 1)
                                dve.wait_ge(chain, (tile * P + e) * 2 + 2)
                                pass_wait(dve)
                            dve.sem_inc(read, 1)
                        ce = Chain(dve, run_chain)
                        ce.step(v.tensor_reduce(SC[0:1, 8:9], run, AXX, ALU.max))
                        ce.step(v.scalar_tensor_tensor(SHIFT0[0:1, :], SC[0:1, 8:9], SLOPE0, SC[0:1, 8:9],
                                                       ALU.mult, ALU.max))
                        dve.sem_inc(done, 1)
                        dve.wait_ge(spread, 1)
                        ce.step(v.tensor_copy(SHIFT0[:], PS[1][:, 0:1]))
                        ce.step(v.tensor_scalar(NSHIFT0[:], SHIFT0[:], -1.0, None, ALU.mult))
                    dve.nop()

        def exact2():
            arrived, read, chain, go = sem("x2_arrived"), sem("x2_read"), sem("x2_chain"), sem("x2_go")
            all_done, stored, back, shifts = sem("x2_all"), sem("x2_stored"), sem("x2_back"), sem("x2_shifts")
            ve, kept = sem("x2_ve"), sem("x2_kept")
            nodes = SEL[:].rearrange("p q u n -> p (q u n)").bitcast(I32)
            near = PROD[:].rearrange("p u n -> p (u n)").bitcast(I32)
            TOP = ACC[0:1, :]
            with nc.Block() as block:
                @block.sync
                def _(sp):
                    with sp.If(sp.value_load(FLAG[0:1, 3:4], min_val=0, max_val=1) > 0):
                        with sp.Fori(0, K) as tile:
                            edge_nodes(sp, tile, nodes, read, arrived)
                        sp.wait_ge(all_done, 1)
                        sp.dma_start(CUMD.unsqueeze(0), TOP[:, 0:NP]).then_inc(stored, 16)
                        sp.wait_ge(stored, 16)
                        sp.dma_start(RDEN[:], CUMD.rearrange("(b p) -> p b", p=P),
                                     allow_slow_non_contiguous=True).then_inc(back, 16)
                    sp.wait_ge(shifts, 1)
                    sp.dma_start(V2.rearrange("(b p) f -> p b f", p=P), VC[:]).then_inc(kept, 16)
                    sp.wait_ge(kept, 16)

                @block.vector
                def _(dve):
                    with dve.If(dve.value_load(FLAG[0:1, 3:4], min_val=0, max_val=1) > 0):
                        v.memset(ACC[:], 0.0).then_inc(go, 1)
                        dve.wait_ge(go, 1)
                        v.tensor_scalar(TOP, TOP, SC[0:1, 1:2], None, ALU.add).then_inc(go, 1)
                        dve.wait_ge(go, 2)
                        dve.sem_inc(read, 1)
                        dve.sem_inc(chain, 1)
                        with dve.Fori(0, K) as tile:
                            dve.wait_ge(arrived, tile * 32 + 32)
                            v.tensor_scalar(near[0:1, P:2 * P], nodes[0:1, P:2 * P], FAR, NP, ALU.is_equal, ALU.mult)
                            v.tensor_scalar(near[0:1, 0:P], nodes[0:1, P:2 * P], NP, None, ALU.min).then_inc(go, 1)
                            dve.wait_ge(go, tile + 3)
                            v.tensor_tensor(near[0:1, P:2 * P], near[0:1, P:2 * P], nodes[0:1, 0:P],
                                            ALU.max).then_inc(ve, 1)
                            dve.wait_ge(ve, tile + 1)
                            pass_wait(dve)
                            with dve.Fori(0, P) as e:
                                to = dve.value_load(near[0:1, ds(e, 1)], min_val=0, max_val=NP)
                                of = dve.value_load(near[0:1, ds(e + P, 1)], min_val=0, max_val=NP)
                                dve.wait_ge(chain, tile * P + e + 1)
                                v.tensor_tensor(TOP[:, ds(of, 1)], TOP[:, ds(of, 1)], UB[0:1, ds(to, 1)],
                                                ALU.max).then_inc(chain, 1)
                            dve.sem_inc(read, 1)
                        dve.wait_ge(chain, K * P + 1)
                        dve.sem_inc(all_done, 1)
                        dve.wait_ge(back, 16)
                        v.tensor_tensor(RDEN[:], RDEN[:], VC[:, :, 0], ALU.add).then_inc(all_done, 1)
                        dve.wait_ge(all_done, 2)
                        v.scalar_tensor_tensor(VC[:, :, 1], RDEN[:], SLOPE2, RDEN[:], ALU.mult,
                                               ALU.max).then_inc(all_done, 1)
                        dve.wait_ge(all_done, 3)
                    dve.sem_inc(shifts, 1)

        def exact3():
            arrived, read, chain, go = sem("x3_arrived"), sem("x3_read"), sem("x3_chain"), sem("x3_go")
            ic_ready, gathered, turned, started = sem("x3_ic"), sem("x3_gathered"), sem("x3_turned"), sem("x3_started")
            col_ready, col_done, taken = sem("x3_col"), sem("x3_coldone"), sem("x3_taken")
            all_done = sem("x3_all")
            nodes = SEL[:].rearrange("p q u n -> p (q u n)").bitcast(I32)
            near = PROD[:].rearrange("p u n -> p (u n)").bitcast(I32)
            with nc.Block() as block:
                @block.sync
                def _(sp):
                    with sp.If(sp.value_load(FLAG[0:1, 1:2], min_val=0, max_val=1) > 0):
                        with sp.Fori(0, K) as tile:
                            edge_nodes(sp, tile, nodes, read, arrived)
                        sp.wait_ge(arrived, 32 * K)
                    sp.nop()

                @block.gpsimd
                def _(pool):
                    with pool.If(pool.value_load(FLAG[0:1, 1:2], min_val=0, max_val=1) > 0):
                        with pool.Fori(0, K) as tile:
                            pool.wait_ge(ic_ready, tile + 1)
                            pool.sem_inc(started, 1)
                            pool.indirect_dma_start(
                                out=G[:, 0, 0, 0:D], out_offset=None, in_=T3,
                                in_offset=bass.IndirectOffsetOnAxis(ap=IC[:, 0:1], axis=0)).then_inc(gathered, 16)
                    pool.nop()

                @block.scalar
                def _(act):
                    with act.If(act.value_load(FLAG[0:1, 1:2], min_val=0, max_val=1) > 0):
                        with act.Fori(0, K) as tile:
                            act.wait_ge(read, tile + 1)
                            a.copy(IC[:, 0:1], IDX3[:, ds(tile, 1)]).then_inc(ic_ready, 1)
                        act.wait_ge(all_done, 1)
                        with act.Fori(0, NB) as blk:
                            act.wait_ge(taken, blk + 1)
                            a.copy(GW[:, 0, 0, :], ACC[:, ds(blk * P, P)]).then_inc(col_ready, 1)
                    act.nop()

                @block.tensor
                def _(pe):
                    with pe.If(pe.value_load(FLAG[0:1, 1:2], min_val=0, max_val=1) > 0):
                        with pe.Fori(0, K) as tile:
                            pe.wait_ge(gathered, tile * 16 + 16)
                            t.transpose(PS[0][:, 0:P], G[:, 0, 0, 0:D], IDENT[:]).then_inc(turned, 1)
                        with pe.Fori(0, NB) as blk:
                            pe.wait_ge(col_ready, blk + 1)
                            t.transpose(PS[1][:, 0:P], GW[:, 0, 0, :], IDENT[:]).then_inc(col_done, 1)
                    pe.nop()

                @block.vector
                def _(dve):
                    with dve.If(dve.value_load(FLAG[0:1, 1:2], min_val=0, max_val=1) > 0):
                        v.memset(ACC[:], -BIG).then_inc(chain, 1)
                        dve.sem_inc(read, 1)
                        with dve.Fori(0, K) as tile:
                            dve.wait_ge(arrived, tile * 32 + 32)
                            v.tensor_scalar(near[0:1, 0:P], nodes[0:1, P:2 * P], NP, None, ALU.min).then_inc(go, 1)
                            dve.wait_ge(go, tile + 1)
                            dve.wait_ge(turned, tile + 1)
                            pass_wait(dve)
                            with dve.Fori(0, P) as e:
                                to = dve.value_load(near[0:1, ds(e, 1)], min_val=0, max_val=NP)
                                dve.wait_ge(chain, tile * P + e + 1)
                                v.tensor_tensor(ACC[:, ds(to, 1)], ACC[:, ds(to, 1)], PS[0][:, ds(e, 1)],
                                                ALU.max).then_inc(chain, 1)
                            dve.sem_inc(read, 1)
                        dve.wait_ge(chain, K * P + 1)
                        dve.sem_inc(all_done, 1)
                        dve.sem_inc(taken, 1)
                        with dve.Fori(0, NB) as blk:
                            dve.wait_ge(col_done, blk + 1)
                            v.tensor_copy(AGG[:, ds(blk, 1), :], PS[1][:, 0:P].unsqueeze(1)).then_inc(taken, 1)
                    dve.nop()

        def edges2v_wide():
            ic_ready, opened, hot_ready, pe_done = sem("ev_ic"), sem("ev_opened"), sem("ev_hot"), sem("ev_pe")
            rows_used, z_ready, w_ready, last_sum = sem("ev_used"), sem("ev_z"), sem("ev_w"), sem("ev_last")
            chain, pass_chain, zeroed = sem("ev_chain"), sem("ev_pass"), sem("ev_zeroed")
            gathered = [sem(f"ev_gathered{b}") for b in range(RING)]
            STEPS = 7
            HOTW = GW[:, :, :, 0:NB]
            with nc.Block() as block:
                @block.scalar
                def _(act):
                    with act.If(act.value_load(FLAG[0:1, 3:4], min_val=0, max_val=1) > 0):
                        first_indices(SRC, ic_ready)
                        with act.Fori(0, passes(act)) as pss:
                            with act.Fori(0, LAPS) as turn:
                                for b in range(RING):
                                    act.wait_ge(z_ready, number(pss, turn, b) + 1)
                                    a.activation(WE[:, b % 2, :, 0], ZL[:, b % 2, :, 0], ACT.Exp).then_inc(w_ready, 1)
                                    next_indices(act, SRC, pss, turn, b, rows_used, ic_ready)

                @block.gpsimd
                def _(pool):
                    with pool.If(pool.value_load(FLAG[0:1, 3:4], min_val=0, max_val=1) > 0):
                        gather_rows(pool, V2, 2, ic_ready, opened, gathered, rows_used, 0)

                @block.tensor
                def _(pe):
                    with pe.If(pe.value_load(FLAG[0:1, 3:4], min_val=0, max_val=1) > 0):
                        t.matmul(PS[0][:, 0:NB], ZERO[:, 0:P], ZERO[:, 0:NB], start=True, stop=False).then_inc(pe_done, 1)
                        with pe.Fori(0, passes(pe)) as pss:
                            with pe.Fori(0, LAPS) as turn:
                                for b in range(RING):
                                    pe.wait_ge(hot_ready, number(pss, turn, b) + 1)
                                    for u in range(U):
                                        last = t.matmul(PS[0][:, 0:NB], OLO[:, u, :], HOTW[:, b % 2, u, :],
                                                        start=False, stop=False)
                                    last.then_inc(pe_done, 1)
                        t.matmul(PS[0][:, 0:NB], ZERO[:, 0:P], ZERO[:, 0:NB], start=False, stop=True).then_inc(last_sum, 1)

                @block.vector
                def _(dve):
                    with dve.If(dve.value_load(FLAG[0:1, 3:4], min_val=0, max_val=1) > 0):
                        regs = [dve.alloc_register(f"ev_base_{u}") for u in range(U)]
                        v.memset(SHIFT[:], 0.0).then_inc(zeroed, 1)
                        dve.wait_ge(zeroed, 1)
                        with dve.Fori(0, passes(dve)) as pss:
                            place_windows(Chain(dve, pass_chain, pss * 3))
                            dve.wait_ge(opened, pss + 1)
                            pass_wait(dve)
                            with dve.Fori(0, LAPS) as turn:
                                for b in range(RING):
                                    i = number(pss, turn, b)
                                    k = tiles_of(dve, turn, b)
                                    cg = Chain(dve, chain, i * STEPS)
                                    dve.reg_load(regs, BASE[0:1, ds(k, U)])
                                    cg.step(select(b, k))
                                    for u in range(U):
                                        w = dve.snap(regs[u], min_val=0, max_val=NP)
                                        ins = v.tensor_tensor(PROD[:, u, :], SEL[:, b % 2, u, :], UB[:, ds(w, W)], ALU.mult)
                                    cg.step(ins)
                                    cg.step(v.tensor_reduce(Z[:, :, 0], PROD[:, 0:U, :], AXX, ALU.add))
                                    dve.wait_ge(gathered[b], turn * (16 * U) + 16 * U)
                                    cg.step(v.tensor_tensor(Z[:, :, 0], Z[:, :, 0], G[:, b, :, 0], ALU.add))
                                    cg.step(v.scalar_tensor_tensor(Z[:, :, 0], Z[:, :, 0], SLOPE2, Z[:, :, 0],
                                                                   ALU.mult, ALU.max))
                                    cg.step(v.tensor_tensor(Z[:, :, 0], Z[:, :, 0], G[:, b, :, 1], ALU.subtract))
                                    v.tensor_tensor(ZL[:, b % 2, :, 0], Z[:, :, 0], PEN[:, ds(k, U)],
                                                    ALU.add).then_inc(z_ready, 1)
                                    dve.sem_inc(rows_used, 1)
                                    dve.wait_ge(pe_done, i + 1)
                                    v.tensor_tensor(OLO, times(IOTA[:], U), per(LO[:, ds(k, U)], P), ALU.is_equal)
                                    cg.step(v.tensor_tensor(HOTW[:, b % 2], times(IOTA[:, 0:NB], U),
                                                            per(HI[:, ds(k, U)], NB), ALU.is_equal))
                                    dve.wait_ge(w_ready, i + 1)
                                    v.tensor_tensor(HOTW[:, b % 2], HOTW[:, b % 2], per(WE[:, b % 2, :, 0], NB),
                                                    ALU.mult).then_inc(hot_ready, 1)
                                    assert cg.n == STEPS
                        dve.wait_ge(last_sum, 1)
                        ce = Chain(dve, zeroed, 1)
                        ce.step(v.tensor_scalar(RDEN[:], PS[0][:, 0:NB], TINY, None, ALU.max))
                        ce.step(v.reciprocal(RDEN[:], RDEN[:]))

        def edges2v_near():
            lo_in = [sem("en_lo_in0"), sem("en_lo_in1")]
            lo_hot, v_ready, place_ready, place_copied = sem("en_lohot"), sem("en_v"), sem("en_place"), sem("en_copied")
            block_ready, z_ready, w_ready = sem("en_block"), sem("en_z"), sem("en_w")
            hot_ready, summed, last_sum, begun = sem("en_hot"), sem("en_summed"), sem("en_last"), sem("en_begun")
            chain, pass_chain, zeroed, split = sem("en_chain"), sem("en_pass"), sem("en_zeroed"), sem("en_split")
            numbered = sem("en_numbered")
            L, STEPS = U * P, 7
            PLACE = GF[:, 0:2 * L].rearrange("p (q u n) -> p q u n", q=2, u=U)
            LOB = GF[:, 2 * L:3 * L].bitcast(BF).rearrange("p (q e) -> p q e", q=2)
            LOT = GF[:, 3 * L:4 * L].bitcast(BF).rearrange("p (q e) -> p q e", q=2)
            HOTW = GW[:, :, :, 0:NB]
            at = 3 * WIDE
            PICK = PROD[:].rearrange("p u n -> p (u n)")[:, U * W:U * W + U * NB].rearrange("p (u n) -> p u n", u=U)
            BLOCK = BUF[:, at:at + 2 * U * NB].rearrange("p (q u n) -> p q u n", q=2, u=U)
            at += 2 * U * NB
            ROW = BUF[:, at:at + 4 * U].rearrange("p (r u) -> p r u", u=U)
            PART, REST = BUF[:, at + 4 * U:at + 4 * U + 1], BUF[:, at + 40:at + 40 + NB]
            at += 40 + NB
            SPLIT = BUF[:, at:at + 3 * 32].bitcast(BF).rearrange("p (r n) -> p r n", r=3)
            SPLIT = SPLIT[:, :, 0:NB]
            IDB = BUF[:, at + 96:at + 96 + P // 2].bitcast(BF)

            def near(eng):
                return eng.value_load(FLAG[0:1, 3:4], min_val=0, max_val=1) < 1

            with nc.Block() as block:
                @block.sync
                def _(sp):
                    with sp.If(near(sp)):
                        with sp.Fori(0, passes(sp)) as pss:
                            with sp.Fori(0, LAPS) as turn:
                                for b in range(RING):
                                    sp.wait_ge(lo_hot, number(pss, turn, b) + 1)
                                    sp.dma_start(LOB[:, b % 2, :], LOD[ds(turn * (RING * L) + b * L, L)].unsqueeze(0)
                                                 .to_broadcast([P, L])).then_inc(lo_in[b % 2], 16)
                        sp.wait_ge(lo_hot, passes(sp) * GROUPS + 1)
                        sp.dma_start(LOB[:, 0, :], LOD[0:L].unsqueeze(0).to_broadcast([P, L])).then_inc(lo_in[0], 16)

                @block.scalar
                def _(act):
                    with act.If(near(act)):
                        with act.Fori(0, passes(act)) as pss:
                            with act.Fori(0, LAPS) as turn:
                                for b in range(RING):
                                    i, q = number(pss, turn, b), b % 2
                                    act.wait_ge(place_ready, i + 2)
                                    act.wait_ge(summed, i + 1)
                                    a.copy(PLACE[:, q, 0:4, :], PS[3 + 2 * q][:].rearrange("p (u n) -> p u n", u=4))
                                    a.copy(PLACE[:, q, 4:8, :],
                                           PS[4 + 2 * q][:].rearrange("p (u n) -> p u n", u=4)).then_inc(place_copied, 1)
                                    act.wait_ge(z_ready, i + 1)
                                    a.activation(WE[:, q, :, 0], ZL[:, q, :, 0], ACT.Exp).then_inc(w_ready, 1)

                @block.gpsimd
                def _(pool):
                    with pool.If(near(pool)):
                        g.iota(PART, [[1, 1]], base=0, channel_multiplier=1,
                               allow_small_or_imprecise_dtypes=True)
                        g.drain().then_inc(numbered, 1)
                        with pool.Fori(0, passes(pool)) as pss:
                            with pool.Fori(0, LAPS) as turn:
                                for b in range(RING):
                                    i, q = number(pss, turn, b), b % 2
                                    pool.wait_ge(block_ready, i + 1)
                                    pool.wait_ge(summed, i + 1)
                                    pool.wait_ge(w_ready, i + 1)
                                    pass_wait(pool)
                                    g.tensor_tensor(HOTW[:, q], BLOCK[:, q], per(WE[:, q, :, 0], NB),
                                                    ALU.mult).then_inc(hot_ready, 1)

                def add_group(q):
                    for u in range(U):
                        last = t.matmul(PS[0][:, 0:NB], PLACE[:, q, u, :], HOTW[:, q, u, :], start=False, stop=False)
                    last.then_inc(summed, 1)

                @block.tensor
                def _(pe):
                    with pe.If(near(pe)):
                        t.matmul(PS[0][:, 0:NB], ZERO[:, 0:P], ZERO[:, 0:NB], start=True, stop=False).then_inc(begun, 1)
                        pe.sem_inc(summed, 1)
                        pe.sem_inc(place_copied, 2)
                        pe.sem_inc(place_ready, 1)
                        pe.wait_ge(split, 1)
                        np_ = passes(pe)
                        with pe.Fori(0, np_) as pss:
                            with pe.Fori(0, LAPS) as turn:
                                for b in range(RING):
                                    i, q = number(pss, turn, b), b % 2
                                    pe.wait_ge(lo_hot, i + 3)
                                    for u in range(U):
                                        for r in range(3):
                                            last = t.matmul(PS[1 + q][:, u * NB:(u + 1) * NB],
                                                            LOT[:, q, u * P:(u + 1) * P], SPLIT[:, r, :],
                                                            start=r == 0, stop=r == 2)
                                    last.then_inc(v_ready, 1)
                                    pe.wait_ge(place_copied, i + 1)
                                    for u in range(U):
                                        last = t.matmul(PS[3 + 2 * q + u // 4][:, (u % 4) * P:(u % 4 + 1) * P],
                                                        LOT[:, q, u * P:(u + 1) * P], IDB, start=True, stop=True)
                                    last.then_inc(place_ready, 1)
                                    pe.wait_ge(place_copied, i + 2)
                                    pe.wait_ge(hot_ready, i + 2)
                                    add_group(1 - q)
                        pe.wait_ge(place_copied, np_ * GROUPS + 2)
                        pe.wait_ge(hot_ready, np_ * GROUPS + 2)
                        add_group(1)
                        t.matmul(PS[0][:, 0:NB], ZERO[:, 0:P], ZERO[:, 0:NB], start=False, stop=True).then_inc(last_sum, 1)

                def place_hot(dve, count, q):
                    dve.wait_ge(lo_in[q], count)
                    v.tensor_scalar(LOT[:, q, :], LOB[:, q, :], PART, None, ALU.is_equal).then_inc(lo_hot, 1)

                @block.vector
                def _(dve):
                    with dve.If(near(dve)):
                        regs = [dve.alloc_register(f"en_base_{u}") for u in range(U)]
                        ce = Chain(dve, zeroed)
                        v.memset(GW[:], 0.0)
                        v.memset(PLACE, 0.0)
                        v.memset(SHIFT[:], 0.0)
                        v.tensor_copy(IDB, IDENT[:])
                        ce.step(v.tensor_copy(SPLIT[:, 0], VC[:, :, 0]))
                        ce.step(v.tensor_tensor(REST, VC[:, :, 0], SPLIT[:, 0], ALU.subtract))
                        ce.step(v.tensor_copy(SPLIT[:, 1], REST))
                        ce.step(v.tensor_tensor(REST, REST, SPLIT[:, 1], ALU.subtract))
                        ce.step(v.tensor_copy(SPLIT[:, 2], REST))
                        dve.sem_inc(split, 1)
                        dve.sem_inc(hot_ready, 2)
                        dve.sem_inc(lo_hot, 2)
                        dve.wait_ge(numbered, 1)
                        place_hot(dve, 16, 0)
                        with dve.Fori(0, passes(dve)) as pss:
                            place_windows(Chain(dve, pass_chain, pss * 3))
                            with dve.Fori(0, LAPS) as turn:
                                for b in range(RING):
                                    i, q = number(pss, turn, b), b % 2
                                    k = tiles_of(dve, turn, b)
                                    cg = Chain(dve, chain, i * STEPS)
                                    own, shift, score = ROW[:, 0], ROW[:, 1], ROW[:, 2]
                                    dve.reg_load(regs, BASE[0:1, ds(k, U)])
                                    select(b, k)
                                    dve.wait_ge(place_ready, i + 1)
                                    place_hot(dve, ((pss * LAPS + turn) * 2 + (b + 1) // 2) * 16 + 16, 1 - q)
                                    dve.wait_ge(hot_ready, i + 1)
                                    cg.step(v.tensor_tensor(BLOCK[:, q], times(IOTA[:, 0:NB], U),
                                                            per(HI[:, ds(k, U)], NB), ALU.is_equal))
                                    dve.sem_inc(block_ready, 1)
                                    dve.wait_ge(v_ready, i + 1)
                                    cg.step(v.tensor_tensor(PICK, PS[1 + q][:, 0:U * NB].rearrange("p (u n) -> p u n", u=U),
                                                            BLOCK[:, q], ALU.mult))
                                    for u in range(U):
                                        w = dve.snap(regs[u], min_val=0, max_val=NP)
                                        v.tensor_tensor(PROD[:, u, :], SEL[:, q, u, :], UB[:, ds(w, W)], ALU.mult)
                                    cg.step(v.tensor_reduce(own, PICK, AXX, ALU.add))
                                    v.tensor_reduce(Z[:, :, 0], PROD[:, 0:U, :], AXX, ALU.add)
                                    cg.step(v.tensor_scalar(shift, own, SC[:, 0:1], None, ALU.add))
                                    v.tensor_tensor(score, own, Z[:, :, 0], ALU.add)
                                    cg.step(v.scalar_tensor_tensor(shift, shift, SLOPE2, shift, ALU.mult, ALU.max))
                                    cg.step(v.scalar_tensor_tensor(score, score, SLOPE2, score, ALU.mult, ALU.max))
                                    cg.step(v.tensor_tensor(score, score, shift, ALU.subtract))
                                    v.tensor_tensor(ZL[:, q, :, 0], score, PEN[:, ds(k, U)],
                                                    ALU.add).then_inc(z_ready, 1)
                                    assert cg.n == STEPS
                        dve.wait_ge(last_sum, 1)
                        ce.step(v.tensor_scalar(RDEN[:], PS[0][:, 0:NB], TINY, None, ALU.max))
                        ce.step(v.reciprocal(RDEN[:], RDEN[:]))

        def edges2():
            ic_ready, opened, sel_ready, pe_done = sem("e2_ic"), sem("e2_opened"), sem("e2_sel"), sem("e2_pe")
            rows_used, z_ready, w_ready, added = sem("e2_used"), sem("e2_z"), sem("e2_w"), sem("e2_added")
            acc_chain, chain = sem("e2_acc"), sem("e2_chain")
            pass_chain, zeroed = sem("e2_pass"), sem("e2_zeroed")
            gathered = [sem(f"e2_gathered{b}") for b in range(RING)]
            STEPS = 6
            with nc.Block() as block:
                @block.scalar
                def _(act):
                    first_indices(SRC, ic_ready)
                    with act.Fori(0, passes(act)) as pss:
                        with act.Fori(0, LAPS) as turn:
                            for b in range(RING):
                                act.wait_ge(z_ready, number(pss, turn, b) + 1)
                                a.activation(WE[:, b % 2, :, 0], ZL[:, b % 2, :, 0], ACT.Exp).then_inc(w_ready, 1)
                                k = act.snap(turn * AHEAD + (b * U + AHEAD), min_val=AHEAD, max_val=K + AHEAD - U)
                                act.wait_ge(pe_done, number(pss, turn, b) + 3)
                                a.copy(IC[:, b * U:(b + 1) * U], SRC[:, ds(k, U)]).then_inc(ic_ready, 1)

                @block.gpsimd
                def _(pool):
                    gather_rows(pool, T2, D + 2, ic_ready, opened, gathered, pe_done, 2)

                @block.tensor
                def _(pe):
                    t.matmul(PS[1][:, 0:U * W], ZERO[:, 0:P], ZERO[:], start=True, stop=True).then_inc(pe_done, 2)
                    with pe.Fori(0, passes(pe)) as pss:
                        pe.wait_ge(opened, pss + 1)
                        pe.sem_inc(passed, 1)
                        with pe.Fori(0, LAPS) as turn:
                            for b in range(RING):
                                i = number(pss, turn, b)
                                pe.wait_ge(sel_ready, i + 1)
                                pe.wait_ge(gathered[b], turn * (16 * U) + 16 * U)
                                pe.wait_ge(added, i + 1)
                                for u in range(U):
                                    last = t.matmul(PS[b % 2][:, u * W:(u + 1) * W], G[:, b, u, 0:D],
                                                    SEL[:, b % 2, u, :], start=True, stop=True)
                                last.then_inc(pe_done, 1)

                @block.vector
                def _(dve):
                    regs = [[dve.alloc_register(f"e2_base{q}_{u}") for u in range(U)] for q in range(2)]
                    v.memset(ACC[:], 0.0).then_inc(acc_chain, 1)
                    v.memset(SHIFT[:], 0.0).then_inc(zeroed, 1)
                    dve.wait_ge(zeroed, 1)
                    dve.sem_inc(added, 1)
                    dve.reg_load(regs[1], BASE[0:1, 0:U])
                    np_ = passes(dve)
                    with dve.Fori(0, np_) as pss:
                        place_windows(Chain(dve, pass_chain, pss * 3))
                        dve.wait_ge(opened, pss + 1)
                        pass_wait(dve)
                        with dve.Fori(0, LAPS) as turn:
                            for b in range(RING):
                                i = number(pss, turn, b)
                                k = tiles_of(dve, turn, b)
                                cg = Chain(dve, chain, i * STEPS)
                                dve.reg_load(regs[b % 2], BASE[0:1, ds(k, U)])
                                dve.wait_ge(pe_done, i + 1)
                                cg.step(select(b, k))
                                for u in range(U):
                                    w = dve.snap(regs[b % 2][u], min_val=0, max_val=NP)
                                    ins = v.tensor_tensor(PROD[:, u, :], SEL[:, b % 2, u, :], UB[:, ds(w, W)], ALU.mult)
                                cg.step(ins)
                                cg.step(v.tensor_reduce(Z[:, :, 0], PROD[:, 0:U, :], AXX, ALU.add))
                                dve.wait_ge(gathered[b], turn * (16 * U) + 16 * U)
                                cg.step(v.tensor_tensor(Z[:, :, 0], Z[:, :, 0], G[:, b, :, D], ALU.add))
                                cg.step(v.scalar_tensor_tensor(Z[:, :, 0], Z[:, :, 0], SLOPE2, Z[:, :, 0],
                                                               ALU.mult, ALU.max))
                                cg.step(v.tensor_tensor(Z[:, :, 0], Z[:, :, 0], G[:, b, :, D + 1], ALU.subtract))
                                v.tensor_tensor(ZL[:, b % 2, :, 0], Z[:, :, 0], PEN[:, ds(k, U)],
                                                ALU.add).then_inc(z_ready, 1)
                                dve.wait_ge(pe_done, i + 2)
                                add_sums(dve, regs[1 - b % 2], i * U, 1 - b % 2, acc_chain)
                                dve.sem_inc(added, 1)
                                dve.wait_ge(w_ready, i + 1)
                                v.tensor_tensor(SEL[:, b % 2], SEL[:, b % 2], per(WE[:, b % 2, :, 0], W),
                                                ALU.mult).then_inc(sel_ready, 1)
                                assert cg.n == STEPS
                    dve.wait_ge(pe_done, np_ * GROUPS + 2)
                    add_sums(dve, regs[1], np_ * (GROUPS * U), 1, acc_chain)
                    pass_wait(dve)

        def edges3():
            ic_ready, turned, scanned = sem("e3_ic"), sem("e3_turned"), sem("e3_scanned")
            back, copied, zeroed = sem("e3_back"), sem("e3_copied"), sem("e3_zeroed")
            gathered = [sem(f"e3_gathered{b}") for b in range(RING)]
            mask_in, stored = [sem("e3_mask0"), sem("e3_mask1")], [sem("e3_stored0"), sem("e3_stored1")]
            chain = sem("e3_chain")
            L = U * P
            MB = BUF[:, 3 * WIDE:3 * WIDE + L].bitcast(BF).rearrange("p (q e) -> p q e", q=2)
            RM = GW[:].rearrange("p q u f -> p q (u f)")
            RB = BUF[:, 3 * WIDE + L:3 * WIDE + 3 * L].rearrange("p (q u f) -> p q u f", q=2, u=U)
            groups_out = RUNS.rearrange("(i u p) f -> p i u f", u=U, p=P)
            with nc.Block() as block:
                @block.scalar
                def _(act):
                    first_indices(IDX3, ic_ready)
                    act.sem_inc(copied, 2)
                    with act.Fori(0, LAPS) as turn:
                        for b in range(RING):
                            i, q = turn * RING + b, 1 - b % 2
                            k = act.snap(turn * AHEAD + (b * U + AHEAD), min_val=AHEAD, max_val=K + AHEAD - U)
                            act.wait_ge(turned, i + 1)
                            a.copy(IC[:, b * U:(b + 1) * U], IDX3[:, ds(k, U)]).then_inc(ic_ready, 1)
                            act.wait_ge(back, i + 2)
                            act.wait_ge(stored[q], (turn * 2 + b // 2) * 16 + 16)
                            a.copy(RB[:, q, 0:4, :], PS[4 + 2 * q][:].rearrange("p (u f) -> p u f", u=4))
                            a.copy(RB[:, q, 4:8, :], PS[5 + 2 * q][:].rearrange("p (u f) -> p u f", u=4)).then_inc(copied, 1)
                    act.wait_ge(back, GROUPS + 2)
                    act.wait_ge(stored[1], (LAPS * 2) * 16 + 16)
                    a.copy(RB[:, 1, 0:4, :], PS[6][:].rearrange("p (u f) -> p u f", u=4))
                    a.copy(RB[:, 1, 4:8, :], PS[7][:].rearrange("p (u f) -> p u f", u=4)).then_inc(copied, 1)

                @block.gpsimd
                def _(pool):
                    with pool.Fori(0, LAPS) as turn:
                        for b in range(RING):
                            pool.wait_ge(ic_ready, turn * RING + b + 1)
                            pass_wait(pool)
                            gather_group(pool, T3, D, b, gathered)

                @block.sync
                def _(sp):
                    sp.sem_inc(stored[0], 16)
                    sp.sem_inc(stored[1], 16)
                    sp.wait_ge(zeroed, 1)
                    with sp.Fori(0, LAPS) as turn:
                        for b in range(RING):
                            i, q = turn * RING + b, 1 - b % 2
                            sp.wait_ge(scanned, i + 1)
                            sp.dma_start(MB[:, b % 2, :], MASKD[ds(turn * (RING * L) + b * L, L)].unsqueeze(0)
                                         .to_broadcast([P, L])).then_inc(mask_in[b % 2], 16)
                            sp.wait_ge(copied, i + 3)
                            sp.dma_start(groups_out[:, ds(i, 1), :, :].rearrange("p i u f -> p (i u) f"),
                                         RB[:, q]).then_inc(stored[q], 16)
                    sp.wait_ge(copied, GROUPS + 3)
                    sp.dma_start(groups_out[:, GROUPS, :, :], RB[:, 1]).then_inc(stored[1], 16)
                    sp.wait_ge(stored[0], LAPS * 2 * 16 + 16)
                    sp.wait_ge(stored[1], LAPS * 2 * 16 + 32)

                def turn_back(pe, q):
                    for u in range(U):
                        last = t.transpose(PS[4 + 2 * q + u // 4][:, (u % 4) * P:(u % 4 + 1) * P],
                                           RM[:, q, u * P:(u + 1) * P], IDENT[:])
                    last.then_inc(back, 1)

                @block.tensor
                def _(pe):
                    pe.sem_inc(back, 1)
                    with pe.Fori(0, LAPS) as turn:
                        for b in range(RING):
                            i, q = turn * RING + b, b % 2
                            pe.wait_ge(gathered[b], turn * (16 * U) + 16 * U)
                            pe.wait_ge(scanned, i + 1)
                            for u in range(U):
                                last = t.transpose(PS[2 * q + u // 4][:, (u % 4) * P:(u % 4 + 1) * P],
                                                   G[:, b, u, 0:D], IDENT[:])
                            last.then_inc(turned, 1)
                            pe.wait_ge(scanned, i + 2)
                            pe.wait_ge(copied, i + 1)
                            turn_back(pe, 1 - q)
                    pe.wait_ge(scanned, GROUPS + 2)
                    pe.wait_ge(copied, GROUPS + 1)
                    turn_back(pe, 1)

                @block.vector
                def _(dve):
                    v.memset(GW[:], 0.0).then_inc(chain, 1)
                    dve.wait_ge(chain, 1)
                    dve.sem_inc(scanned, 2)
                    dve.sem_inc(zeroed, 1)
                    with dve.Fori(0, LAPS) as turn:
                        for b in range(RING):
                            i, q = turn * RING + b, b % 2
                            dve.wait_ge(turned, i + 1)
                            dve.wait_ge(mask_in[q], (turn * 2 + b // 2) * 16 + 16)
                            dve.wait_ge(back, i + 1)
                            for h in range(2):
                                before = RM[:, 1 - q, L - 1:L] if h == 0 else RM[:, q, L // 2 - 1:L // 2]
                                dve.wait_ge(chain, i * 2 + h + 1)
                                v.tensor_tensor_scan(RM[:, q, h * 512:(h + 1) * 512],
                                                     MB[:, q, h * 512:(h + 1) * 512], PS[2 * q + h][:],
                                                     before, ALU.min, ALU.max).then_inc(chain, 1)
                            dve.wait_ge(chain, i * 2 + 3)
                            dve.sem_inc(scanned, 1)

        def moments(ch, b, nb, blk):
            pass_wait(ch.eng)
            for j in range(nb):
                ins = v.bn_stats(BN6[:, b, j, :], X[:, ds(blk + j, 1), :].rearrange("p o f -> p (o f)"))
            ch.step(ins)
            pass_wait(ch.eng)
            for j in range(nb):
                ins = v.bn_aggr(SM[:, b, j, 4:6], BN6[:, b, j, :])
            ch.step(ins)
            return v.tensor_copy(MV[:, ds(blk, nb), :], SM[:, b, 0:nb, 4:6])

        def normalize(dve, ch, root_in, root_out):
            ch.step(v.tensor_copy(RSTD[:], MV[:, :, 1]))
            dve.sem_inc(root_in, 1)
            dve.wait_ge(root_out, 1)
            ch.step(v.reciprocal(RSTD[:], RSTD[:]))
            ch.step(v.scalar_tensor_tensor(NBIA[:], MV[:, :, 0], -1.0, RSTD[:], ALU.mult, ALU.mult))

        def rows(ap, nb):
            return ap[:, 0:nb * P].rearrange("p (b f) -> p b f", f=D)

        def close0():
            w_in, sums_ready, pe_done, taken, chain = sem("c0_w"), sem("c0_sums"), sem("c0_pe"), sem("c0_taken"), sem("c0_chain")
            x_in, x_used, x_tail, sx_zero = [sem("c0_x0"), sem("c0_x1")], sem("c0_xused"), sem("c0_xtail"), sem("c0_sxzero")
            STEPS = 8
            B0 = WS[:, 0:D]
            with nc.Block() as block:
                @block.sync
                def _(sp):
                    sp.dma_start(B0, bias0.to_broadcast([P, D])).then_inc(w_in, 16)
                    with sp.Fori(0, NODE_TURNS - 1) as turn:
                        for b in range(2):
                            i, nb, blk, col = half(turn, b)
                            sp.wait_ge(x_used, i + 1)
                            sp.dma_start(rows(SX[:, b], nb),
                                         x[ds(col, nb * P), :].rearrange("(b p) f -> p b f", p=P)).then_inc(x_in[b], 16)
                    last = NODE_TURNS - 1
                    for b in range(2):
                        i, nb, blk, col = half(last, b)
                        whole = nb - b
                        sp.wait_ge(x_used, i + 1)
                        if b:
                            sp.dma_start(SX[0:LAST, b, whole * P:nb * P], x[(NB - 1) * P:N]).then_inc(x_tail, 16)
                            sp.wait_ge(x_tail, 16)
                        sp.dma_start(rows(SX[:, b], whole),
                                     x[col:col + whole * P].rearrange("(b p) f -> p b f", p=P)).then_inc(x_in[b], 16)
                    sp.wait_ge(w_in, 16)

                @block.scalar
                def _(act):
                    with act.Fori(0, NODE_TURNS) as turn:
                        for b in range(2):
                            i, nb, blk, col = half(turn, b)
                            act.wait_ge(pe_done, i + 1)
                            a.copy(SA[:, b, 0:nb * P], ACC[:, ds(col, nb * P)])
                            a.copy(SD[:, b, 0:nb * P], DEN[:, ds(col, nb * P)]).then_inc(sums_ready, 1)

                @block.tensor
                def _(pe):
                    pe.sem_inc(pe_done, 2)
                    with pe.Fori(0, NODE_TURNS) as turn:
                        for b in range(2):
                            i, nb, blk, col = half(turn, b)
                            pe.wait_ge(sums_ready, i + 1)
                            pe.wait_ge(taken, i + 1)
                            for j in range(nb):
                                t.transpose(PS[b][:, j * P:(j + 1) * P], SA[:, b, j * P:(j + 1) * P], IDENT[:])
                                last = t.transpose(PS[2 + b][:, j * 8:j * 8 + 1 + H], SD[:, b, j * P:(j + 1) * P],
                                                   IDENT[0:1 + H, 0:1 + H])
                            last.then_inc(pe_done, 1)

                @block.vector
                def _(dve):
                    dve.sem_inc(taken, 2)
                    v.memset(SX[:], 0.0).then_inc(sx_zero, 1)
                    dve.wait_ge(sx_zero, 1)
                    dve.sem_inc(x_used, 2)
                    dve.wait_ge(w_in, 16)
                    with dve.Fori(0, NODE_TURNS) as turn:
                        for b in range(2):
                            i, nb, blk, col = half(turn, b)
                            ch = Chain(dve, chain, i * STEPS)
                            den = PS[2 + b][:, 0:nb * 8].rearrange("p (b h) -> p b h", h=8)
                            rec = SM[:, b, 0:nb, 0:H]
                            heads = lambda y: y.rearrange("p (c f) -> p c f", f=DH)
                            Y = YS[:, b, 0:nb * P]
                            dve.wait_ge(pe_done, i + 3)
                            v.tensor_copy(DEG[:, ds(blk, nb)], den[:, :, 0])
                            ch.step(v.tensor_scalar(rec, den[:, :, 1:1 + H], GUARD0[:], None, ALU.add))
                            ch.step(v.reciprocal(rec, rec))
                            ch.step(v.tensor_tensor(Y.rearrange("p (b h f) -> p b h f", h=H, f=DH),
                                                    PS[b][:, 0:nb * P].rearrange("p (b h f) -> p b h f", h=H, f=DH),
                                                    per(rec, DH), ALU.mult))
                            dve.sem_inc(taken, 1)
                            ch.step(v.tensor_tensor(rows(Y, nb), rows(Y, nb), times(B0, nb), ALU.add))
                            dve.wait_ge(x_in[b], turn * 16 + 16)
                            ch.step(v.tensor_tensor(X[:, ds(blk, nb), :], rows(SX[:, b], nb), rows(Y, nb), ALU.add))
                            dve.sem_inc(x_used, 1)
                            ch.step(moments(ch, b, nb, blk))
                            assert ch.n == STEPS

        def open1():
            w_in, root_in, root_out, chain = sem("o1_w"), sem("o1_rin"), sem("o1_rout"), sem("o1_chain")
            loop_chain, sx_ready, x_done, pe_turned = sem("o1_lchain"), sem("o1_sx"), sem("o1_x"), sem("o1_turned")
            sa_ready, pe_done, hs_done = sem("o1_sa"), sem("o1_pe"), sem("o1_hs")
            cum_in = sem("o1_cumin")
            stored = [sem("o1_stored0"), sem("o1_stored1")]
            table = T1.rearrange("(b p) f -> p b f", p=P)
            with nc.Block() as block:
                @block.sync
                def _(sp):
                    sp.dma_start(WS[:, 0:D], w_selfT).then_inc(w_in, 16)
                    sp.dma_start(WB[0:1, 0:D], b_self).then_inc(w_in, 16)
                    sp.sem_inc(stored[0], 16)
                    sp.sem_inc(stored[1], 16)
                    sp.dma_start(ENDF[:], CUMD.rearrange("(b p) -> p b", p=P), allow_slow_non_contiguous=True).then_inc(cum_in, 16)
                    with sp.Fori(0, NODE_TURNS) as turn:
                        for b in range(2):
                            i, nb, blk, col = half(turn, b)
                            sp.wait_ge(sx_ready, i + 1)
                            sp.dma_start(table[:, ds(blk, nb), :], rows(SX[:, b], nb)).then_inc(stored[b], 16)
                    sp.wait_ge(stored[0], NODE_TURNS * 16 + 16)
                    sp.wait_ge(stored[1], NODE_TURNS * 16 + 16)
                    sp.wait_ge(cum_in, 16)

                @block.vector
                def _(dve):
                    ch = Chain(dve, chain)
                    normalize(dve, ch, root_in, root_out)
                    with dve.Fori(0, NODE_TURNS) as turn:
                        for b in range(2):
                            i, nb, blk, col = half(turn, b)
                            cl = Chain(dve, loop_chain, i)
                            dve.wait_ge(stored[b], turn * 16 + 16)
                            dve.wait_ge(x_done, i + 1)
                            dve.wait_ge(pe_turned, i + 1)
                            cl.step(v.tensor_tensor(rows(YS[:, b], nb), X[:, ds(blk, nb), :],
                                                    per(RSTD[:, ds(blk, nb)], D), ALU.mult))
                            v.tensor_tensor(rows(SX[:, b], nb), rows(YS[:, b], nb),
                                            per(NBIA[:, ds(blk, nb)], D), ALU.add).then_inc(sx_ready, 1)
                    ch.step(v.tensor_scalar(RDEG[:], DEG[:], 1.0, None, ALU.max))
                    v.reciprocal(RDEG[:], RDEG[:])
                    v.tensor_scalar(HAS[:], DEG[:], 0.0, None, ALU.is_gt)
                    dve.wait_ge(cum_in, 16)
                    ch.step(v.tensor_scalar(ENDF[:], ENDF[:], -1.0, 0.0, ALU.add, ALU.max))
                    ch.step(v.tensor_scalar(ENDI[:], ENDF[:], float(U * P), None, ALU.add))

                @block.gpsimd
                def _(pool):
                    pool.sem_inc(x_done, 2)
                    with pool.Fori(0, NODE_TURNS) as turn:
                        for b in range(2):
                            i, nb, blk, col = half(turn, b)
                            pool.wait_ge(sx_ready, i + 1)
                            g.tensor_copy(X[:, ds(blk, nb), :], rows(SX[:, b], nb)).then_inc(x_done, 1)

                @block.tensor
                def _(pe):
                    pe.sem_inc(pe_turned, 2)
                    pe.wait_ge(w_in, 32)
                    with pe.Fori(0, NODE_TURNS) as turn:
                        for b in range(2):
                            i, nb, blk, col = half(turn, b)
                            pe.wait_ge(sx_ready, i + 1)
                            pe.wait_ge(hs_done, i + 1)
                            for j in range(nb):
                                last = t.transpose(PS[b][:, j * P:(j + 1) * P], SX[:, b, j * P:(j + 1) * P], IDENT[:])
                            last.then_inc(pe_turned, 1)
                            pe.wait_ge(sa_ready, i + 1)
                            for j in range(nb):
                                o = PS[2 + b][:, j * P:(j + 1) * P]
                                t.matmul(o, SA[:, b, j * P:(j + 1) * P], WS[:, 0:D], start=True, stop=False)
                                last = t.matmul(o, ONE[0:1, :], WB[0:1, 0:D], start=False, stop=True)
                            last.then_inc(pe_done, 1)

                @block.scalar
                def _(act):
                    act.sem_inc(hs_done, 2)
                    act.wait_ge(root_in, 1)
                    a.activation(RSTD[:], RSTD[:], ACT.Sqrt, bias=EPS[:]).then_inc(root_out, 1)
                    with act.Fori(0, NODE_TURNS) as turn:
                        for b in range(2):
                            i, nb, blk, col = half(turn, b)
                            act.wait_ge(pe_turned, i + 3)
                            a.copy(SA[:, b, 0:nb * P], PS[b][:, 0:nb * P]).then_inc(sa_ready, 1)
                            act.wait_ge(pe_done, i + 1)
                            a.copy(HS[:, ds(blk, nb), :], rows(PS[2 + b], nb)).then_inc(hs_done, 1)

        def close1():
            w_in, sums_ready, pe_done, taken, chain = sem("c1_w"), sem("c1_sums"), sem("c1_pe"), sem("c1_taken"), sem("c1_chain")
            root_in, root_out, going = sem("c1_rin"), sem("c1_rout"), sem("c1_going")
            STEPS = 14
            GA, BE = WS[:, D:2 * D], WS[:, 2 * D:3 * D]
            with nc.Block() as block:
                @block.sync
                def _(sp):
                    sp.dma_start(WS[:, 0:D], w_msgT).then_inc(w_in, 16)
                    sp.dma_start(GA, gamma.to_broadcast([P, D])).then_inc(w_in, 16)
                    sp.dma_start(BE, beta.to_broadcast([P, D])).then_inc(w_in, 16)
                    sp.wait_ge(w_in, 48)

                @block.scalar
                def _(act):
                    with act.Fori(0, NODE_TURNS) as turn:
                        for b in range(2):
                            i, nb, blk, col = half(turn, b)
                            act.wait_ge(root_in, i + 1)
                            a.activation(SM[:, b, 0:nb, 2], SM[:, b, 0:nb, 5], ACT.Sqrt,
                                         bias=EPS[:]).then_inc(root_out, 1)

                @block.gpsimd
                def _(pool):
                    with pool.Fori(0, NODE_TURNS) as turn:
                        for b in range(2):
                            i, nb, blk, col = half(turn, b)
                            pool.wait_ge(pe_done, i + 1)
                            pool.sem_inc(going, 1)
                            g.tensor_copy(SA[:, b, 0:nb * P], ACC[:, ds(col, nb * P)]).then_inc(sums_ready, 1)

                @block.tensor
                def _(pe):
                    pe.sem_inc(pe_done, 2)
                    pe.wait_ge(w_in, 48)
                    with pe.Fori(0, NODE_TURNS) as turn:
                        for b in range(2):
                            i, nb, blk, col = half(turn, b)
                            pe.wait_ge(sums_ready, i + 1)
                            pe.wait_ge(taken, i + 1)
                            for j in range(nb):
                                last = t.matmul(PS[b][:, j * P:(j + 1) * P], SA[:, b, j * P:(j + 1) * P],
                                                WS[:, 0:D], start=True, stop=True)
                            last.then_inc(pe_done, 1)

                @block.vector
                def _(dve):
                    dve.sem_inc(taken, 2)
                    dve.wait_ge(w_in, 48)
                    with dve.Fori(0, NODE_TURNS) as turn:
                        for b in range(2):
                            i, nb, blk, col = half(turn, b)
                            ch = Chain(dve, chain, i * STEPS)
                            Y = rows(YS[:, b], nb)
                            mean, dev = SM[:, b, 0:nb, 4], SM[:, b, 0:nb, 2]
                            dve.wait_ge(pe_done, i + 3)
                            ch.step(v.tensor_tensor(Y, rows(PS[b], nb), per(RDEG[:, ds(blk, nb)], D), ALU.mult))
                            dve.sem_inc(taken, 1)
                            ch.step(v.tensor_tensor(Y, Y, HS[:, ds(blk, nb), :], ALU.add))
                            ch.step(v.tensor_scalar(Y, Y, 0.0, None, ALU.max))
                            for j in range(nb):
                                ins = v.bn_stats(BN6[:, b, j, :], YS[:, b, j * P:(j + 1) * P])
                            ch.step(ins)
                            pass_wait(dve)
                            for j in range(nb):
                                ins = v.bn_aggr(SM[:, b, j, 4:6], BN6[:, b, j, :])
                            ch.step(ins)
                            dve.sem_inc(root_in, 1)
                            ch.step(v.tensor_tensor(Y, Y, per(mean, D), ALU.subtract))
                            dve.wait_ge(root_out, i + 1)
                            ch.step(v.reciprocal(dev, dev))
                            ch.step(v.tensor_tensor(Y, Y, per(dev, D), ALU.mult))
                            ch.step(v.tensor_tensor(Y, Y, times(GA, nb), ALU.mult))
                            ch.step(v.tensor_tensor(Y, Y, times(BE, nb), ALU.add))
                            ch.step(v.tensor_tensor(X[:, ds(blk, nb), :], X[:, ds(blk, nb), :], Y, ALU.add))
                            ch.step(moments(ch, b, nb, blk))
                            assert ch.n == STEPS

        def open2():
            w_in, root_in, root_out, chain = sem("o2_w"), sem("o2_rin"), sem("o2_rout"), sem("o2_chain")
            loop_chain, sx_ready, x_done, pe_turned = sem("o2_lchain"), sem("o2_sx"), sem("o2_x"), sem("o2_turned")
            sa_ready, pe_done, u_done, w_ready = sem("o2_sa"), sem("o2_pe"), sem("o2_u"), sem("o2_wready")
            going = sem("o2_going")
            with nc.Block() as block:
                @block.sync
                def _(sp):
                    sp.dma_start(WS[:, 0:1], w_i).then_inc(w_in, 16)
                    sp.dma_start(WS[:, 1:2], w_j).then_inc(w_in, 16)
                    sp.wait_ge(w_in, 32)

                @block.vector
                def _(dve):
                    ch = Chain(dve, chain)
                    normalize(dve, ch, root_in, root_out)
                    v.memset(UB[:, NP:WIDE], 0.0)
                    dve.wait_ge(w_in, 32)
                    ch.step(v.tensor_copy(WB[:, 0:D], WS[:, 0:1].to_broadcast([P, D])))
                    dve.sem_inc(w_ready, 1)
                    with dve.Fori(0, NODE_TURNS) as turn:
                        for b in range(2):
                            i, nb, blk, col = half(turn, b)
                            cl = Chain(dve, loop_chain, i)
                            dve.wait_ge(x_done, i + 1)
                            dve.wait_ge(pe_turned, i + 1)
                            cl.step(v.tensor_tensor(rows(YS[:, b], nb), X[:, ds(blk, nb), :],
                                                    per(RSTD[:, ds(blk, nb)], D), ALU.mult))
                            v.tensor_tensor(rows(SX[:, b], nb), rows(YS[:, b], nb),
                                            per(NBIA[:, ds(blk, nb)], D), ALU.add).then_inc(sx_ready, 1)
                    ch.step(v.tensor_scalar(HI.bitcast(I32), SRC[:], P - 1, None, ALU.bitwise_and))
                    ch.step(v.tensor_copy(LO, HI.bitcast(I32)))
                    ch.step(v.tensor_scalar(REL[:].bitcast(I32), SRC[:], 7, None, ALU.logical_shift_right))
                    v.tensor_copy(HI, REL[:].bitcast(I32))
                    dve.wait_ge(u_done, 2 * NODE_TURNS + 2)
                    v.tensor_reduce(SC[:, 1:2], UB[:, 0:N], AXX, ALU.min)
                    ch.step(v.tensor_reduce(SC[:, 0:1], UB[:, 0:N], AXX, ALU.max))
                    ch.step(v.tensor_tensor(SC[:, 2:3], SC[:, 0:1], SC[:, 1:2], ALU.subtract))
                    is_wide(ch, SC[:, 2:3], FLAG[:, 3:4])
                    ch.step(v.tensor_scalar(VC[:, :, 1], VC[:, :, 0], SC[:, 0:1], None, ALU.add))
                    ch.step(v.scalar_tensor_tensor(VC[:, :, 1], VC[:, :, 1], SLOPE2, VC[:, :, 1], ALU.mult, ALU.max))
                @block.gpsimd
                def _(pool):
                    pool.sem_inc(x_done, 2)
                    with pool.Fori(0, NODE_TURNS) as turn:
                        for b in range(2):
                            i, nb, blk, col = half(turn, b)
                            pool.wait_ge(sx_ready, i + 1)
                            pool.sem_inc(going, 1)
                            g.tensor_copy(X[:, ds(blk, nb), :], rows(SX[:, b], nb)).then_inc(x_done, 1)

                @block.tensor
                def _(pe):
                    pe.sem_inc(pe_turned, 2)
                    pe.wait_ge(w_ready, 1)
                    with pe.Fori(0, NODE_TURNS) as turn:
                        for b in range(2):
                            i, nb, blk, col = half(turn, b)
                            pe.wait_ge(sx_ready, i + 1)
                            pe.wait_ge(u_done, i + 1)
                            for j in range(nb):
                                last = t.transpose(PS[b][:, j * P:(j + 1) * P], SX[:, b, j * P:(j + 1) * P], IDENT[:])
                            last.then_inc(pe_turned, 1)
                            pe.wait_ge(sa_ready, i + 1)
                            for j in range(nb):
                                t.matmul(PS[2 + b][:, j:j + 1], SA[:, b, j * P:(j + 1) * P], WS[:, 1:2],
                                         start=True, stop=True)
                            t.matmul(PS[4 + b][:, 0:nb * P], WB[:, 0:D], SA[:, b, 0:nb * P],
                                     start=True, stop=True).then_inc(pe_done, 1)

                @block.scalar
                def _(act):
                    act.sem_inc(u_done, 2)
                    act.wait_ge(root_in, 1)
                    a.activation(RSTD[:], RSTD[:], ACT.Sqrt, bias=EPS[:]).then_inc(root_out, 1)
                    with act.Fori(0, NODE_TURNS) as turn:
                        for b in range(2):
                            i, nb, blk, col = half(turn, b)
                            act.wait_ge(pe_turned, i + 3)
                            a.copy(SA[:, b, 0:nb * P], PS[b][:, 0:nb * P]).then_inc(sa_ready, 1)
                            act.wait_ge(pe_done, i + 1)
                            a.copy(VC[:, ds(blk, nb), 0], PS[2 + b][:, 0:nb])
                            a.copy(UB[:, ds(col, nb * P)], PS[4 + b][:, 0:nb * P]).then_inc(u_done, 1)

        def table2():
            made, stored = sem("t2_made"), [sem("t2_stored0"), sem("t2_stored1")]
            table = T2.rearrange("(b p) f -> p b f", p=P)
            with nc.Block() as block:
                @block.sync
                def _(sp):
                    sp.sem_inc(stored[0], 16)
                    sp.sem_inc(stored[1], 16)
                    with sp.Fori(0, NODE_TURNS) as turn:
                        for b in range(2):
                            i, nb, blk, col = half(turn, b)
                            sp.wait_ge(made, i + 1)
                            sp.dma_start(table[:, ds(blk, nb), :], YW[:, 4 * b:4 * b + nb, 0:D + 2]).then_inc(stored[b], 16)
                    sp.wait_ge(stored[0], NODE_TURNS * 16 + 16)
                    sp.wait_ge(stored[1], NODE_TURNS * 16 + 16)

                @block.vector
                def _(dve):
                    with dve.Fori(0, NODE_TURNS) as turn:
                        for b in range(2):
                            i, nb, blk, col = half(turn, b)
                            dve.wait_ge(stored[b], turn * 16 + 16)
                            v.tensor_tensor(YW[:, 4 * b:4 * b + nb, 0:D], X[:, ds(blk, nb), :],
                                            per(RDEN[:, ds(blk, nb)], D), ALU.mult)
                            v.tensor_copy(YW[:, 4 * b:4 * b + nb, D:D + 2], VC[:, ds(blk, nb), :]).then_inc(made, 1)

        def close2():
            sums_ready, pe_done, taken, chain = sem("c2_sums"), sem("c2_pe"), sem("c2_taken"), sem("c2_chain")
            STEPS = 4
            with nc.Block() as block:
                @block.scalar
                def _(act):
                    with act.Fori(0, NODE_TURNS) as turn:
                        for b in range(2):
                            i, nb, blk, col = half(turn, b)
                            act.wait_ge(pe_done, i + 1)
                            a.copy(SA[:, b, 0:nb * P], ACC[:, ds(col, nb * P)]).then_inc(sums_ready, 1)

                @block.tensor
                def _(pe):
                    pe.sem_inc(pe_done, 2)
                    with pe.Fori(0, NODE_TURNS) as turn:
                        for b in range(2):
                            i, nb, blk, col = half(turn, b)
                            pe.wait_ge(sums_ready, i + 1)
                            pe.wait_ge(taken, i + 1)
                            for j in range(nb):
                                last = t.transpose(PS[b][:, j * P:(j + 1) * P], SA[:, b, j * P:(j + 1) * P], IDENT[:])
                            last.then_inc(pe_done, 1)

                @block.vector
                def _(dve):
                    dve.sem_inc(taken, 2)
                    with dve.Fori(0, NODE_TURNS) as turn:
                        for b in range(2):
                            i, nb, blk, col = half(turn, b)
                            ch = Chain(dve, chain, i * STEPS)
                            dve.wait_ge(pe_done, i + 3)
                            ch.step(v.scalar_tensor_tensor(X[:, ds(blk, nb), :], rows(PS[b], nb), 0.0,
                                                           X[:, ds(blk, nb), :], ALU.max, ALU.add))
                            dve.sem_inc(taken, 1)
                            ch.step(moments(ch, b, nb, blk))
                            assert ch.n == STEPS

        def open3():
            w_in, root_in, root_out, chain = sem("o3_w"), sem("o3_rin"), sem("o3_rout"), sem("o3_chain")
            loop_chain, sx_ready, x_done, pe_turned = sem("o3_lchain"), sem("o3_sx"), sem("o3_x"), sem("o3_turned")
            sa_ready, pe_done, hs_done, msg_done = sem("o3_sa"), sem("o3_pe"), sem("o3_hs"), sem("o3_msg")
            idx_in, going = sem("o3_idx"), sem("o3_going")
            stored = [sem("o3_stored0"), sem("o3_stored1")]
            table = T3.rearrange("(r b p) f -> p r b f", r=R, p=P)
            MS = BUF[:, 3 * WIDE:3 * WIDE + 8 * R * D].rearrange("p (q b m) -> p q b m", q=2, b=4)
            BR = WB[:, 0:R * D]
            with nc.Block() as block:
                @block.sync
                def _(sp):
                    sp.dma_start(WS[:].rearrange("p (r f) -> p r f", r=R + 1),
                                 w_rel.rearrange("r k f -> k r f")).then_inc(w_in, 16)
                    sp.dma_start(BR, b_rel[0:R, :].rearrange("r f -> (r f)").unsqueeze(0).to_broadcast([P, R * D])).then_inc(w_in, 16)
                    sp.dma_start(WB[:, R * D:(R + 1) * D], b_rel[R:R + 1, :].to_broadcast([P, D])).then_inc(w_in, 16)
                    sp.dma_start(IDX3, IDX3D).then_inc(idx_in, 16)
                    sp.sem_inc(stored[0], 16 * R)
                    sp.sem_inc(stored[1], 16 * R)
                    with sp.Fori(0, NODE_TURNS) as turn:
                        for b in range(2):
                            i, nb, blk, col = half(turn, b)
                            sp.wait_ge(msg_done, i + 3)
                            for r in range(R):
                                sp.dma_start(table[:, r, ds(blk, nb), :],
                                             MS[:, b, 0:nb, r * D:(r + 1) * D]).then_inc(stored[b], 16)
                    sp.wait_ge(stored[0], (NODE_TURNS + 1) * 16 * R)
                    sp.wait_ge(stored[1], (NODE_TURNS + 1) * 16 * R)
                    sp.wait_ge(idx_in, 16)

                @block.vector
                def _(dve):
                    ch = Chain(dve, chain)
                    normalize(dve, ch, root_in, root_out)
                    dve.sem_inc(msg_done, 2)
                    dve.wait_ge(w_in, 48)
                    with dve.Fori(0, NODE_TURNS) as turn:
                        for b in range(2):
                            i, nb, blk, col = half(turn, b)
                            cl = Chain(dve, loop_chain, i)
                            dve.wait_ge(x_done, i + 1)
                            dve.wait_ge(pe_turned, i + 1)
                            cl.step(v.tensor_tensor(rows(YS[:, b], nb), X[:, ds(blk, nb), :],
                                                    per(RSTD[:, ds(blk, nb)], D), ALU.mult))
                            v.tensor_tensor(rows(SX[:, b], nb), rows(YS[:, b], nb),
                                            per(NBIA[:, ds(blk, nb)], D), ALU.add).then_inc(sx_ready, 1)
                            dve.wait_ge(pe_done, i + 1)
                            dve.wait_ge(stored[b], turn * (16 * R) + 16 * R)
                            for j in range(nb):
                                ins = v.tensor_tensor(MS[:, b, j, :], PS[2 + j][:], BR, ALU.add)
                            ins.then_inc(msg_done, 1)

                @block.gpsimd
                def _(pool):
                    pool.sem_inc(x_done, 2)
                    with pool.Fori(0, NODE_TURNS) as turn:
                        for b in range(2):
                            i, nb, blk, col = half(turn, b)
                            pool.wait_ge(sx_ready, i + 1)
                            pool.sem_inc(going, 1)
                            g.tensor_copy(X[:, ds(blk, nb), :], rows(SX[:, b], nb)).then_inc(x_done, 1)

                @block.tensor
                def _(pe):
                    pe.sem_inc(pe_turned, 2)
                    pe.wait_ge(w_in, 48)
                    with pe.Fori(0, NODE_TURNS) as turn:
                        for b in range(2):
                            i, nb, blk, col = half(turn, b)
                            pe.wait_ge(sx_ready, i + 1)
                            pe.wait_ge(hs_done, i + 1)
                            for j in range(nb):
                                last = t.transpose(PS[b][:, j * P:(j + 1) * P], SX[:, b, j * P:(j + 1) * P], IDENT[:])
                            last.then_inc(pe_turned, 1)
                            pe.wait_ge(sa_ready, i + 1)
                            pe.wait_ge(msg_done, i + 2)
                            for j in range(nb):
                                blkT = SA[:, b, j * P:(j + 1) * P]
                                o = PS[6 + b][:, j * P:(j + 1) * P]
                                t.matmul(PS[2 + j][:], blkT, WS[:, 0:R * D], start=True, stop=True)
                                t.matmul(o, blkT, WS[:, R * D:(R + 1) * D], start=True, stop=False)
                                last = t.matmul(o, ONE[0:1, :], WB[0:1, R * D:(R + 1) * D], start=False, stop=True)
                            last.then_inc(pe_done, 1)

                @block.scalar
                def _(act):
                    act.sem_inc(hs_done, 2)
                    act.wait_ge(root_in, 1)
                    a.activation(RSTD[:], RSTD[:], ACT.Sqrt, bias=EPS[:]).then_inc(root_out, 1)
                    with act.Fori(0, NODE_TURNS) as turn:
                        for b in range(2):
                            i, nb, blk, col = half(turn, b)
                            act.wait_ge(pe_turned, i + 3)
                            a.copy(SA[:, b, 0:nb * P], PS[b][:, 0:nb * P]).then_inc(sa_ready, 1)
                            act.wait_ge(pe_done, i + 1)
                            a.copy(HS[:, ds(blk, nb), :], rows(PS[6 + b], nb)).then_inc(hs_done, 1)

        def take_maxima():
            got = sem("f_got")
            with nc.Block() as block:
                @block.gpsimd
                def _(pool):
                    for blk in range(NB):
                        pool.indirect_dma_start(out=AGG[:, blk, :], out_offset=None, in_=RUNS,
                                                in_offset=bass.IndirectOffsetOnAxis(ap=ENDI[:, blk:blk + 1], axis=0)
                                                ).then_inc(got, 16)
                    pool.wait_ge(got, NB * 16)

        def finish():
            chain, loop_chain, more = sem("f_chain"), sem("f_lchain"), sem("f_more")
            root_in, root_out, stored = sem("f_rin"), sem("f_rout"), sem("f_stored")
            STEPS = 6
            with nc.Block() as block:
                @block.scalar
                def _(act):
                    act.wait_ge(root_in, 1)
                    a.activation(RSTD[:], RSTD[:], ACT.Sqrt, bias=EPS[:]).then_inc(root_out, 1)

                @block.vector
                def _(dve):
                    with dve.Fori(0, NODE_TURNS) as turn:
                        for b in range(2):
                            i, nb, blk, col = half(turn, b)
                            cl = Chain(dve, loop_chain, i * STEPS)
                            Y = rows(YS[:, b], nb)
                            cl.step(v.tensor_tensor(Y, AGG[:, ds(blk, nb), :], per(HAS[:, ds(blk, nb)], D), ALU.mult))
                            cl.step(v.tensor_tensor(Y, Y, HS[:, ds(blk, nb), :], ALU.add))
                            cl.step(v.tensor_tensor(X[:, ds(blk, nb), :], X[:, ds(blk, nb), :], Y, ALU.add))
                            cl.step(moments(cl, b, nb, blk))
                            pass_wait(dve)
                            assert cl.n == STEPS
                    ch = Chain(dve, chain)
                    normalize(dve, ch, root_in, root_out)
                    with dve.Fori(0, NODE_TURNS) as turn:
                        for b in range(2):
                            i, nb, blk, col = half(turn, b)
                            cm = Chain(dve, more, i * 2)
                            cm.step(v.tensor_tensor(X[:, ds(blk, nb), :], X[:, ds(blk, nb), :],
                                                    per(RSTD[:, ds(blk, nb)], D), ALU.mult))
                            cm.step(v.tensor_tensor(X[:, ds(blk, nb), :], X[:, ds(blk, nb), :],
                                                    per(NBIA[:, ds(blk, nb)], D), ALU.add))
                            pass_wait(dve)

                @block.sync
                def _(sp):
                    sp.wait_ge(more, 4 * NODE_TURNS)
                    sp.dma_start(out[0:(NB - 1) * P].rearrange("(b p) f -> p b f", p=P), X[:, 0:NB - 1, :]).then_inc(stored, 16)
                    sp.dma_start(out[(NB - 1) * P:N], X[0:LAST, NB - 1, :]).then_inc(stored, 16)
                    sp.wait_ge(stored, 32)

        for stage in (edge_lists, table0, exact0, edges0, close0, open1, edges1, close1, open2, exact2, edges2v_wide,
                      edges2v_near, table2, edges2, close2, open3, edges3, take_maxima, exact3, finish):
            before = nc.snapshot_sems()
            stage()
            nc.clear_and_free_semaphores(nc.allocated_since(before))
            nc.all_engine_barrier()


def kernel(x, src, dst, edge_type_4, L0_gnn_W_proj, L0_gnn_a_src, L0_gnn_a_tgt, L0_gnn_bias, L1_gnn_W_msg,
           L1_gnn_W_self, L1_gnn_b_self, L1_gnn_gamma, L1_gnn_beta, L2_gnn_w_i, L2_gnn_w_j, L3_gnn_weight,
           L3_gnn_bias):
    import concourse.bacc as bacc
    from concourse.bass_utils import run_bass_kernel_spmd

    x = np.asarray(x)
    row = lambda y: np.asarray(y).reshape(1, -1)
    arrays = {
        "x": x, "xT": x.T, "src": src, "dst": dst, "etype": edge_type_4, "w_proj": L0_gnn_W_proj,
        "a_src": row(L0_gnn_a_src), "a_tgt": row(L0_gnn_a_tgt), "bias0": row(L0_gnn_bias),
        "w_msgT": np.asarray(L1_gnn_W_msg).T, "w_selfT": np.asarray(L1_gnn_W_self).T, "b_self": row(L1_gnn_b_self),
        "gamma": row(L1_gnn_gamma), "beta": row(L1_gnn_beta), "w_i": row(L2_gnn_w_i).T, "w_j": row(L2_gnn_w_j).T,
        "w_rel": L3_gnn_weight, "b_rel": L3_gnn_bias,
    }
    arrays = {n: np.ascontiguousarray(y) for n, y in arrays.items()}
    nc = bacc.Bacc("TRN2", target_bir_lowering=False, num_devices=1)
    args = {n: nc.dram_tensor(n, y.shape, mybir.dt.from_np(y.dtype), kind="ExternalInput").ap()
            for n, y in arrays.items()}
    args["out"] = nc.dram_tensor("out", (N, D), FP, kind="ExternalOutput").ap()
    build(nc, **args)
    return run_bass_kernel_spmd(nc, [arrays], core_ids=[0]).results[0]["out"]
```
